# Optimizing a Trainium2 kernel written in Bass

```python
import numpy as np
import jax
import jax.numpy as jnp

def _softmax(x, axis=-1):
    return jax.nn.softmax(x, axis=axis)

def _gelu(x):
    return jax.nn.gelu(x, approximate=True)

def _silu(x):
    return jax.nn.silu(x)

def _sigmoid(x):
    return jax.nn.sigmoid(x)

def _layernorm(x, axis=-1, eps=1e-05):
    m = jnp.mean(x, axis=axis, keepdims=True)
    v = jnp.var(x, axis=axis, keepdims=True)
    return (x - m) / jnp.sqrt(v + eps)

def _scatter_add(tgt, idx, src, axis=0):
    return tgt.at[idx].add(src)

def _segment_sum(src, seg, n):
    return jax.ops.segment_sum(src, seg, n)
kernel_name = 'mk_xattn_seq_d2_seqx_r8_344056'

def setup_inputs(seed: int=0):
    np.random.seed(seed)
    _w = jnp.asarray

    def _rec_inputs():
        import jax
        import jax.numpy as jnp
        _rk = jax.random.key(seed)
        x = 7.22e-05 + 1 * jax.random.normal(jax.random.fold_in(_rk, 1), (32, 64, 256), jnp.float32)
        _lenS = 64 - jax.random.randint(jax.random.fold_in(_rk, 7), (32,), 0, max(1, 64 // 4) + 1, jnp.int32)
        _lenS2 = 64 - jax.random.randint(jax.random.fold_in(_rk, 8), (32,), 0, max(1, 64 // 4) + 1, jnp.int32)
        _ctx_1024P = jax.random.normal(jax.random.fold_in(_rk, 11), (32, 16, 128), jnp.float32)
        _ctx_1024c = jax.random.dirichlet(jax.random.fold_in(_rk, 511), 0.3 * jnp.ones((16,), jnp.float32), (32, 64))
        _ctx_1024t = jnp.einsum('bsk,bkd->bsd', _ctx_1024c, _ctx_1024P)
        _ctx_1024t = _ctx_1024t * jax.lax.rsqrt(jnp.mean(jnp.square(_ctx_1024t)) + 1e-12) * 0.953939
        ctx_1024 = -0.000514642 + 1.00011 * (_ctx_1024t + 0.3 * jax.random.normal(jax.random.fold_in(_rk, 611), (32, 64, 128), jnp.float32))
        pos_1xS = jnp.broadcast_to(jnp.arange(64, dtype=jnp.int32), (1, 64))
        _validS = jnp.arange(64)[None, :] < _lenS[:, None]
        _validS2 = jnp.arange(64)[None, :] < _lenS2[:, None]
        _causal = jnp.tril(jnp.ones((64, 64), dtype=bool))
        mask_BxS_ik0 = jnp.where(jnp.broadcast_to(_validS[:, :], (32, 64)), 0, 1).astype(jnp.int32)
        return (x, ctx_1024, pos_1xS, mask_BxS_ik0)
    x, ctx_1024, pos_1xS, mask_BxS_ik0 = _rec_inputs()

    def _L0_xattn_setup():
        import jax, jax.numpy as jnp
        import numpy as np
        H = 256
        NH = 16
        HD = H // NH
        CH = 128
        CC = 128
        CHD = CC // NH
        I = 688
        B = 2
        L = 256
        LE = 128
        EPS = 1e-06

        def rms_norm(x, w):
            xf = x.astype(jnp.float32)
            var = jnp.mean(xf * xf, axis=-1, keepdims=True)
            return (w * (xf * jax.lax.rsqrt(var + EPS))).astype(x.dtype)

        def expert_mask(tt):
            vm = jnp.zeros(tt.shape, dtype=bool)
            vm = vm.at[:, :-1].set((tt[:, :-1] == 1) & (tt[:, 1:] == 1))
            return vm

        def rotate_half(x):
            d = x.shape[-1] // 2
            return jnp.concatenate([-x[..., d:], x[..., :d]], axis=-1)

        def apply_rotary(q, k, position_ids, seq_len):
            inv = 1.0 / 10000.0 ** (jnp.arange(0, HD, 2, dtype=jnp.float32) / HD)
            t = jnp.arange(seq_len, dtype=jnp.float32)
            freqs = jnp.outer(t, inv)
            emb = jnp.concatenate([freqs, freqs], axis=-1)
            cos = jnp.cos(emb)[position_ids][:, None].astype(q.dtype)
            sin = jnp.sin(emb)[position_ids][:, None].astype(q.dtype)
            return (q * cos + rotate_half(q) * sin, k * cos + rotate_half(k) * sin)

        def sdpa(q, k, v, causal):
            scale = 1.0 / np.sqrt(q.shape[-1])
            scores = jnp.einsum('bhqd,bhkd->bhqk', q * scale, k)
            if causal:
                mask = jnp.tril(jnp.ones((q.shape[-2], k.shape[-2]), dtype=bool))
                scores = jnp.where(mask, scores, jnp.finfo(jnp.float32).min)
            p = jax.nn.softmax(scores.astype(jnp.float32), axis=-1).astype(q.dtype)
            return jnp.einsum('bhqk,bhkd->bhqd', p, v)

        def heads(x, nh, hd):
            b, l, _ = x.shape
            return x.reshape(b, l, nh, hd).transpose(0, 2, 1, 3)
        key = jax.random.key(seed)
        ks = jax.random.split(key, 20)
        s = 0.02
        f32 = jnp.float32
        return {'hidden_states': jax.random.normal(ks[0], (B, L, H), f32), 'encoder_outputs': jax.random.normal(ks[1], (B, LE, CH), f32), 'token_type_ids': jax.random.randint(ks[2], (B, L), 0, 2, jnp.int32), 'position_ids': jnp.arange(L, dtype=jnp.int32)[None, :], 'ln_in_w': jnp.ones((H,), f32), 'ln_post_attn_w': jnp.ones((H,), f32), 'ln_post_cross_w': jnp.ones((H,), f32), 'v_qkv': jax.random.normal(ks[3], (H, 3 * H), f32) * s, 'l_qkv': jax.random.normal(ks[4], (H, 3 * H), f32) * s, 'v_dense': jax.random.normal(ks[5], (H, H), f32) * s, 'l_dense': jax.random.normal(ks[6], (H, H), f32) * s, 'cq_w': jax.random.normal(ks[7], (H, CC), f32) * s, 'ckv_w': jax.random.normal(ks[8], (CH, 2 * CC), f32) * s, 'cdense_w': jax.random.normal(ks[9], (CC, H), f32) * s, 'v_gate': jax.random.normal(ks[10], (H, I), f32) * s, 'v_up': jax.random.normal(ks[11], (H, I), f32) * s, 'v_down': jax.random.normal(ks[12], (I, H), f32) * s, 'l_gate': jax.random.normal(ks[13], (H, I), f32) * s, 'l_up': jax.random.normal(ks[14], (H, I), f32) * s, 'l_down': jax.random.normal(ks[15], (I, H), f32) * s}
    _L0_xattn_all = _L0_xattn_setup()
    _L0_xattn_in = {k: v for k, v in _L0_xattn_all.items() if k in ('ln_in_w', 'ln_post_attn_w', 'ln_post_cross_w', 'v_qkv', 'l_qkv', 'v_dense', 'l_dense', 'cq_w', 'ckv_w', 'cdense_w', 'v_gate', 'v_up', 'v_down', 'l_gate', 'l_up', 'l_down')}
    del _L0_xattn_all

    def _L1_xattn_setup():
        import jax, jax.numpy as jnp
        import numpy as np
        EPS = 1e-06

        def _rmsnorm(x, w):
            var = jnp.mean(jnp.square(x), axis=-1, keepdims=True)
            return x * jax.lax.rsqrt(var + EPS) * w
        key = jax.random.key(seed)
        ks = jax.random.split(key, 6)
        B, N, M = (4, 512, 256)
        d_model, memory_dim = (256, 128)
        hidden_states = jax.random.normal(ks[0], (B, N, d_model), dtype=jnp.float32)
        memory = jax.random.normal(ks[1], (B, M, memory_dim), dtype=jnp.float32)
        W_mem = jax.random.normal(ks[2], (d_model, memory_dim), dtype=jnp.float32) / np.sqrt(memory_dim)
        W_gate = jax.random.normal(ks[3], (d_model, 2 * d_model), dtype=jnp.float32) / np.sqrt(2 * d_model)
        b_gate = jax.random.normal(ks[4], (d_model,), dtype=jnp.float32) * 0.01
        norm_w = jnp.ones((d_model,), dtype=jnp.float32)
        return {'hidden_states': hidden_states, 'memory': memory, 'W_mem': W_mem, 'W_gate': W_gate, 'b_gate': b_gate, 'norm_w': norm_w}
    _L1_xattn_all = _L1_xattn_setup()
    _L1_xattn_in = {k: v for k, v in _L1_xattn_all.items() if k in ('W_mem', 'W_gate', 'b_gate', 'norm_w')}
    del _L1_xattn_all
    return {'x': x, 'ctx_1024': ctx_1024, 'pos_1xS': pos_1xS, 'mask_BxS_ik0': mask_BxS_ik0, 'L0_xattn_ln_in_w': _L0_xattn_in['ln_in_w'], 'L0_xattn_ln_post_attn_w': _L0_xattn_in['ln_post_attn_w'], 'L0_xattn_ln_post_cross_w': _L0_xattn_in['ln_post_cross_w'], 'L0_xattn_v_qkv': _L0_xattn_in['v_qkv'], 'L0_xattn_l_qkv': _L0_xattn_in['l_qkv'], 'L0_xattn_v_dense': _L0_xattn_in['v_dense'], 'L0_xattn_l_dense': _L0_xattn_in['l_dense'], 'L0_xattn_cq_w': _L0_xattn_in['cq_w'], 'L0_xattn_ckv_w': _L0_xattn_in['ckv_w'], 'L0_xattn_cdense_w': _L0_xattn_in['cdense_w'], 'L0_xattn_v_gate': _L0_xattn_in['v_gate'], 'L0_xattn_v_up': _L0_xattn_in['v_up'], 'L0_xattn_v_down': _L0_xattn_in['v_down'], 'L0_xattn_l_gate': _L0_xattn_in['l_gate'], 'L0_xattn_l_up': _L0_xattn_in['l_up'], 'L0_xattn_l_down': _L0_xattn_in['l_down'], 'L1_xattn_W_mem': _L1_xattn_in['W_mem'], 'L1_xattn_W_gate': _L1_xattn_in['W_gate'], 'L1_xattn_b_gate': _L1_xattn_in['b_gate'], 'L1_xattn_norm_w': _L1_xattn_in['norm_w']}

def reference(x, ctx_1024, pos_1xS, mask_BxS_ik0, L0_xattn_ln_in_w, L0_xattn_ln_post_attn_w, L0_xattn_ln_post_cross_w, L0_xattn_v_qkv, L0_xattn_l_qkv, L0_xattn_v_dense, L0_xattn_l_dense, L0_xattn_cq_w, L0_xattn_ckv_w, L0_xattn_cdense_w, L0_xattn_v_gate, L0_xattn_v_up, L0_xattn_v_down, L0_xattn_l_gate, L0_xattn_l_up, L0_xattn_l_down, L1_xattn_W_mem, L1_xattn_W_gate, L1_xattn_b_gate, L1_xattn_norm_w):
    import jax
    import jax.numpy as jnp

    def _L0_xattn_ref(hidden_states, encoder_outputs, token_type_ids, position_ids, ln_in_w, ln_post_attn_w, ln_post_cross_w, v_qkv, l_qkv, v_dense, l_dense, cq_w, ckv_w, cdense_w, v_gate, v_up, v_down, l_gate, l_up, l_down):
        import jax, jax.numpy as jnp
        import numpy as np
        H = 256
        NH = 16
        HD = H // NH
        CH = 128
        CC = 128
        CHD = CC // NH
        I = 688
        B = 2
        L = 256
        LE = 128
        EPS = 1e-06

        def rms_norm(x, w):
            xf = x.astype(jnp.float32)
            var = jnp.mean(xf * xf, axis=-1, keepdims=True)
            return (w * (xf * jax.lax.rsqrt(var + EPS))).astype(x.dtype)

        def expert_mask(tt):
            vm = jnp.zeros(tt.shape, dtype=bool)
            vm = vm.at[:, :-1].set((tt[:, :-1] == 1) & (tt[:, 1:] == 1))
            return vm

        def rotate_half(x):
            d = x.shape[-1] // 2
            return jnp.concatenate([-x[..., d:], x[..., :d]], axis=-1)

        def apply_rotary(q, k, position_ids, seq_len):
            inv = 1.0 / 10000.0 ** (jnp.arange(0, HD, 2, dtype=jnp.float32) / HD)
            t = jnp.arange(seq_len, dtype=jnp.float32)
            freqs = jnp.outer(t, inv)
            emb = jnp.concatenate([freqs, freqs], axis=-1)
            cos = jnp.cos(emb)[position_ids][:, None].astype(q.dtype)
            sin = jnp.sin(emb)[position_ids][:, None].astype(q.dtype)
            return (q * cos + rotate_half(q) * sin, k * cos + rotate_half(k) * sin)

        def sdpa(q, k, v, causal):
            scale = 1.0 / np.sqrt(q.shape[-1])
            scores = jnp.einsum('bhqd,bhkd->bhqk', q * scale, k)
            if causal:
                mask = jnp.tril(jnp.ones((q.shape[-2], k.shape[-2]), dtype=bool))
                scores = jnp.where(mask, scores, jnp.finfo(jnp.float32).min)
            p = jax.nn.softmax(scores.astype(jnp.float32), axis=-1).astype(q.dtype)
            return jnp.einsum('bhqk,bhkd->bhqd', p, v)

        def heads(x, nh, hd):
            b, l, _ = x.shape
            return x.reshape(b, l, nh, hd).transpose(0, 2, 1, 3)
        b, l, _ = hidden_states.shape
        vm = expert_mask(token_type_ids)[..., None]
        residual = hidden_states
        x = rms_norm(hidden_states, ln_in_w)
        mixed = jnp.where(vm, x @ v_qkv, x @ l_qkv)
        q, k, v = jnp.split(mixed, 3, axis=-1)
        q, k, v = (heads(q, NH, HD), heads(k, NH, HD), heads(v, NH, HD))
        q, k = apply_rotary(q, k, position_ids, l)
        ctx = sdpa(q, k, v, causal=True)
        ctx = ctx.transpose(0, 2, 1, 3).reshape(b, l, H)
        attn_out = jnp.where(vm, ctx @ v_dense, ctx @ l_dense)
        hidden_states = residual + attn_out
        ci = rms_norm(hidden_states, ln_post_cross_w)
        cq = heads(ci @ cq_w, NH, CHD)
        ckv = encoder_outputs @ ckv_w
        ck, cv = jnp.split(ckv, 2, axis=-1)
        ck, cv = (heads(ck, NH, CHD), heads(cv, NH, CHD))
        cctx = sdpa(cq, ck, cv, causal=False)
        cctx = cctx.transpose(0, 2, 1, 3).reshape(b, l, CC)
        hidden_states = hidden_states + cctx @ cdense_w
        mi = rms_norm(hidden_states, ln_post_attn_w)
        v_out = jax.nn.silu(mi @ v_gate) * (mi @ v_up) @ v_down
        l_out = jax.nn.silu(mi @ l_gate) * (mi @ l_up) @ l_down
        hidden_states = hidden_states + jnp.where(vm, v_out, l_out)
        return hidden_states

    def _L1_xattn_ref(hidden_states, memory, W_mem, W_gate, b_gate, norm_w):
        import jax, jax.numpy as jnp
        import numpy as np
        EPS = 1e-06

        def _rmsnorm(x, w):
            var = jnp.mean(jnp.square(x), axis=-1, keepdims=True)
            return x * jax.lax.rsqrt(var + EPS) * w
        D = hidden_states.shape[-1]
        memory_proj = jnp.einsum('bme,de->bmd', memory, W_mem)
        scores = jnp.einsum('bnd,bmd->bnm', hidden_states, memory_proj) / jnp.sqrt(jnp.float32(D))
        attn = jax.nn.softmax(scores, axis=-1)
        memory_context = jnp.einsum('bnm,bmd->bnd', attn, memory_proj)
        gate_input = jnp.concatenate([hidden_states, memory_context], axis=-1)
        gate = jax.nn.sigmoid(jnp.einsum('bnf,df->bnd', gate_input, W_gate) + b_gate)
        fused = hidden_states + gate * memory_context
        return _rmsnorm(fused, norm_w)
    x = _L0_xattn_ref(x, ctx_1024, mask_BxS_ik0, pos_1xS, L0_xattn_ln_in_w, L0_xattn_ln_post_attn_w, L0_xattn_ln_post_cross_w, L0_xattn_v_qkv, L0_xattn_l_qkv, L0_xattn_v_dense, L0_xattn_l_dense, L0_xattn_cq_w, L0_xattn_ckv_w, L0_xattn_cdense_w, L0_xattn_v_gate, L0_xattn_v_up, L0_xattn_v_down, L0_xattn_l_gate, L0_xattn_l_up, L0_xattn_l_down)
    x = _L1_xattn_ref(x, ctx_1024, L1_xattn_W_mem, L1_xattn_W_gate, L1_xattn_b_gate, L1_xattn_norm_w)
    return x

_drawn_inputs = setup_inputs


def setup_inputs(seed=0):
    import zlib

    import numpy as np

    out = dict(_drawn_inputs(seed))
    spreads = {'L0_xattn_ln_in_w': (1.0, 0.6),
     'L0_xattn_ln_post_attn_w': (1.0, 0.6),
     'L0_xattn_ln_post_cross_w': (1.0, 0.6),
     'L1_xattn_norm_w': (1.0, 0.2)}
    factors = {'L0_xattn_v_qkv': 8.0,
     'L0_xattn_v_dense': 8.0,
     'L0_xattn_cq_w': 55.379,
     'L0_xattn_v_gate': 5.726,
     'L0_xattn_v_up': 5.625,
     'L0_xattn_v_down': 5.718,
     'L1_xattn_b_gate': 52.029}
    for name, (base, spread) in spreads.items():
        noise = np.random.default_rng([zlib.crc32(name.encode()), seed]).standard_normal(out[name].shape)
        drawn = base * np.exp(spread * noise) if base else spread * noise
        out[name] = jnp.asarray(drawn.astype(out[name].dtype))
    for name, factor in factors.items():
        out[name] = (out[name] * factor).astype(out[name].dtype)
    return out
```

```python
from contextlib import ExitStack

import numpy as np

import concourse.bass as bass
from concourse import mybir

F32 = mybir.dt.float32
F32R = mybir.dt.float32r
BF16 = mybir.dt.bfloat16
I32 = mybir.dt.int32
ALU = mybir.AluOpType
ACT = mybir.ActivationFunctionType
AX = mybir.AxisListType

P = 128
BATCH, SEQ, H = 32, 64, 256
NH, HD = 16, 16
CC, CHD = 128, 8
INTER = 688
N_TOK = BATCH * SEQ
TILES = 2
GT = TILES * P
GROUPS = N_TOK // GT
HC = H // P
NJ = 6
JW = -(-INTER // NJ)
JWS = [min(JW, INTER - j * JW) for j in range(NJ)]
PAIRS = NH // 2
EPS = 1e-6
NEG = -1.0e30
C_ID, C_ST, C_H16, C_H8, C_CAUS, C_BLK, C_ROPE, C_IOTA, C_END = np.cumsum(
    [0, P, SEQ, 4, 8, SEQ, P, 2 * HD, 1]).tolist()


def shape_constants():
    c = np.zeros((P, C_END), np.float32)
    row = np.arange(P)
    c[:, C_ID:C_ID + P] = np.eye(P)
    c[:, C_ST:C_ST + SEQ] = np.tile(np.eye(SEQ), (2, 1))
    c[:, C_H16:C_H16 + 4] = (row[:, None] % 64) // HD == np.arange(4)
    c[:, C_H8:C_H8 + 8] = (row[:, None] % 64) // CHD == np.arange(8)
    c[:, C_CAUS:C_CAUS + SEQ] = np.where(np.arange(SEQ) <= row[:, None] % SEQ, 0, NEG)
    c[:, C_BLK:C_BLK + P] = np.where(row[:, None] // SEQ == row // SEQ, 0, NEG)
    inv = (np.float32(1.0) / np.float32(10000.0) ** (np.arange(0, HD, 2, dtype=np.float32) / np.float32(HD)))
    freq = np.outer(np.arange(SEQ, dtype=np.float32), inv.astype(np.float32)).astype(np.float32)
    sin = np.sin(freq)
    c[:SEQ, C_ROPE:C_ROPE + HD] = np.tile(np.cos(freq), (1, 2))
    c[:SEQ, C_ROPE + HD:C_ROPE + 2 * HD] = np.concatenate([-sin, sin], 1)
    c[:, C_IOTA] = row
    return c


def xattn_kernel(nc, d, out):
    ctx = ExitStack()
    with ctx:
        def sb(name, shape, dt=F32):
            return ctx.enter_context(nc.sbuf_tensor(name, shape, dt))

        def sem(name):
            return ctx.enter_context(nc.semaphore(name))

        w_qkv = [sb(f"w_qkv_{s}", [P, 2, HC, 3 * H], F32R) for s in ("hi", "lo")]
        w_gu = [sb(f"w_gu_{s}", [P, 2, 2, HC, INTER], F32R) for s in ("hi", "lo")]
        w_down = sb("w_down", [JW, NJ, 2, H])
        w_dense = sb("w_dense", [P, HC, 2, H])
        w_cq = sb("w_cq", [P, HC, CC])
        w_ckv = sb("w_ckv", [P, 2 * CC])
        w_cdense = sb("w_cdense", [P, H])
        w_mem = sb("w_mem", [P, H])
        w_gate = sb("w_gate", [P, 2 * HC, H])
        b_gate = sb("b_gate", [P, H])
        w_norm = sb("w_norm", [P, H])
        ln = sb("ln", [P, 3, HC])
        cst = sb("cst", [P, C_END])
        ident = cst[:, C_ID:C_ID + P]
        ident_h = sb("ident_h", [P, P], BF16)
        causal_h = sb("causal_h", [P, 8, SEQ], BF16)
        block_h = sb("block_h", [P, P], BF16)
        pos_i = sb("pos_i", [SEQ, P], I32)
        pos_f = sb("pos_f", [SEQ, 3, P])
        rope = sb("rope", [P, 2 * HD])
        route = sb("route", [P, N_TOK], BF16)
        ones = sb("ones", [1, 1], BF16)
        route_t = sb("route_t", [P, 2, TILES * GROUPS])
        pow_eps = sb("pow_eps", [P, 2])

        x_sb = sb("x_sb", [P, TILES, H])
        xT = sb("xT", [P, HC, GT])
        xs = [[sb(f"xs_{e}{s}", [P, HC, GT], F32R) for s in ("hi", "lo")] for e in "vl"]
        ctxT_a = sb("ctxT_a", [P, GT])
        ss = sb("ss", [P, 4, TILES])
        var = sb("var", [P, 4, TILES])
        rstd = sb("rstd", [P, 4, TILES])
        rope_r = sb("rope_r", [P, TILES, 2 * HD])
        qkz = [sb(f"qkz{t}", [P, 8, P]) for t in range(TILES)]
        qT = [sb(f"qT{t}", [P, 4, P]) for t in range(TILES)]
        kT = [sb(f"kT{t}", [P, 16 * SEQ]) for t in range(TILES)]
        E = [sb(f"E{t}", [P, NH * SEQ]) for t in range(TILES)]
        pT = [sb(f"pT{t}", [P, PAIRS, P]) for t in range(TILES)]
        vb = [sb(f"vb{t}", [P, 2, PAIRS, 2, HD + 1]) for t in range(TILES)]
        cvb = [sb(f"cvb{t}", [P, 2, PAIRS, 2, CHD + 1]) for t in range(TILES)]
        mx = sb("mx", [P, TILES, NH])
        rec = sb("rec", [P, TILES, NH])
        att = [sb(f"att{t}", [P, H]) for t in range(TILES)]
        attT = [sb(f"attT{t}", [P, HC, P]) for t in range(TILES)]
        h1 = [sb(f"h1_{t}", [P, H]) for t in range(TILES)]
        h1T = [sb(f"h1T{t}", [P, HC, P]) for t in range(TILES)]

        h2 = [sb(f"h2_{t}", [P, H]) for t in range(TILES)]
        mi = [sb(f"mi{t}", [P, H]) for t in range(TILES)]
        ms = [[sb(f"ms_{e}{s}", [P, HC, GT], F32R) for s in ("hi", "lo")] for e in "vl"]
        th = [sb(f"th{k}", [P, GT]) for k in range(2)]
        hid = sb("hid", [P, NJ, GT])
        h3 = [sb(f"h3_{t}", [P, H]) for t in range(TILES)]
        h3T = [sb(f"h3T{t}", [P, HC, P]) for t in range(TILES)]
        ctxT_b = sb("ctxT_b", [P, GT])
        mp = [sb(f"mp{t}", [P, 2 * H]) for t in range(TILES)]
        mw = [sb(f"mw{t}", [P, P]) for t in range(TILES)]
        mwT = [sb(f"mwT{t}", [P, P]) for t in range(TILES)]
        mm = sb("mm", [P, TILES, 4])
        mc = [sb(f"mc{t}", [P, 2 * H]) for t in range(TILES)]
        z = [sb(f"z{t}", [P, H]) for t in range(TILES)]
        res = [sb(f"res{t}", [P, H]) for t in range(TILES)]

        xy = [ctx.enter_context(nc.psum_tensor(f"xy{t}", [P, 2, 512], F32)) for t in range(TILES)]
        X = [xy[t][:, 0, :] for t in range(TILES)]
        Y = [xy[t][:, 1, :] for t in range(TILES)]
        Z = [ctx.enter_context(nc.psum_tensor(f"z_ps{t}", [P, 512], F32)) for t in range(TILES)]
        B = [ctx.enter_context(nc.psum_tensor(f"b_ps{t}", [P, 512], F32)) for t in range(TILES)]

        names = """ld_cst ld_pos ld_types ld_ln ld_bias ld_wa ld_wb ld_x ld_xT ld_ca ld_cb ld_rest
            cst_ready pos_step hot_ready rope_ps rope_ready zeroed type_step route_ready route_ps route_t_ready small_ready
            wsplit_hi wsplit_lo cq_ready
            xh_ready xl_ready xv_ready xs_ready ssx r1v r1 roper
            qk_ps v_ps rope_a rope_b qkz_ready vb_ready q_ps k_ps qT_ready kT_ready s_ps max_ready sub_ready exp_ready
            pT_psx pT_psy pT_readyx pT_ready pv_ps rec_ready att_ready attT_ps attT_ready dense_ps h1a h1_ready ss1 r2v r2
            h1T_ps h1T_ready cq_ps ckv_ps cq_ev ck_ev cvb_ready cQ_ps cK_ps cqT_ready ckT_ready cs_ps cmax csub cexp
            cpT_psx cpT_psy cpT_readyx cpT_ready cpv_ps crec catt_ready cattT_ps cattT_ready cdense_ps h2_ready ss2 r3v r3 mi_ready
            miT_ps mh_ready ml_ready mv_ready ms_ready gu_ps th_ready gt_ready hid_ready down_ps h3a h3_ready h3T_ps h3T_ready
            mem_ps mem_ready ms_ps mmax mmaxs mexp mrec mw_ready mwT_ps mwT_ready mc_ps mc_ready gate_ps zb_ready tz_ready gm_ready
            fused_ready ss4 r4v r4 out_ready""".split()
        S = {n: sem(n) for n in names}

        def tl(n, t):
            return 2 * n + t + 1

        def first(n):
            return isinstance(n, int) and n == 0

        stage = [E[0][:, :], E[1][:, :], pT[0][:].rearrange("p a b -> p (a b)"), pT[1][:].rearrange("p a b -> p (a b)")]
        split = []
        for e, k in enumerate("vl"):
            for c in range(HC):
                split.append((d[f"L0_xattn_{k}_qkv"][c * P:(c + 1) * P, :], (0, c), w_qkv[0][:, e, c, :], w_qkv[1][:, e, c, :], 3 * H))
        for g, nm in enumerate(("gate", "up")):
            for e, k in enumerate("vl"):
                for c in range(HC):
                    split.append((d[f"L0_xattn_{k}_{nm}"][c * P:(c + 1) * P, :], (2, c), w_gu[0][:, g, e, c, :], w_gu[1][:, g, e, c, :], INTER))
        NSTAGE = len(stage)

        stored = [sem(f"stored{t}") for t in range(TILES)]
        wload = [sem(f"wload{k}") for k in range(NSTAGE)]

        def order(a, b):
            A, Bs = a is not None, b is not None
            def both(name):
                return [(name, a, 0), (name, a, 1)] if A else []
            def bt(name, *tiles):
                return [(name, b, t) for t in tiles] if Bs else []
            steps = []
            steps += [("xsplit", a, 0)] if A else []
            steps += bt("miT", 0) + bt("mlp", 0) + bt("mlp", 1)
            steps += both("qkv") + bt("mlp", 2) + both("rope") + both("qkT") + bt("mlp", 3) + both("score") + bt("mlp", 4)
            steps += both("probT") + bt("mlp", 5) + both("pv") + bt("down", 0) + both("ctxT") + bt("down", 1) + both("dense")
            steps += bt("h3T", 0, 1) + both("h1T") + bt("mem", 0, 1) + both("cproj") + bt("mscore", 0, 1) + both("cqkT")
            steps += bt("attnT", 0, 1) + both("cscore") + bt("mc", 0, 1) + both("cprobT") + bt("gate", 0, 1)
            steps += both("cpv") + both("cctxT") + both("cdense")
            return steps

        def run(eng, steps):
            def one(a, b):
                for name, n, t in order(a, b):
                    if name in steps:
                        steps[name](n, t)
            one(0, None)
            one(1, 0)
            with eng.Fori(2, GROUPS) as n:
                one(n, n - 1)
            one(None, GROUPS - 1)

        block = ctx.enter_context(nc.Block())

        @block.sync
        def _(sp):
            def load_xT(n):
                if not first(n):
                    sp.wait_ge(S["xl_ready"], n)
                sp.dma_start(xT[:, :, :], d["xT"][:, bass.ds(n * GT, GT)].rearrange("(c p) n -> p c n", p=P)).then_inc(S["ld_xT"], 16)

            def load_x(n):
                if not first(n):
                    sp.wait_ge(S["h1_ready"], tl(n, 1) - 2)
                sp.dma_start(x_sb[:, :, :], d["x"][bass.ds(n * GT, GT), :].rearrange("(t p) h -> p t h", p=P)).then_inc(S["ld_x"], 16)

            def load_ctx_a(n):
                if not first(n):
                    sp.wait_ge(S["ckv_ps"], tl(n, 1) - 2)
                sp.dma_start(ctxT_a[:, :], d["ctxT"][:, bass.ds(n * GT, GT)]).then_inc(S["ld_ca"], 16)

            def load_ctx_b(n):
                if not first(n):
                    sp.wait_ge(S["mem_ps"], tl(n, 1) - 2)
                sp.dma_start(ctxT_b[:, :], d["ctxT"][:, bass.ds(n * GT, GT)]).then_inc(S["ld_cb"], 16)

            def store(n):
                for t in range(TILES):
                    sp.wait_ge(S["out_ready"], tl(n, t))
                    sp.dma_start(out[bass.ds(n * GT + t * P, P), :], res[t][:, :]).then_inc(stored[t], 16)

            sp.dma_start(cst[:, :], d["consts"]).then_inc(S["ld_cst"], 16)
            sp.dma_start(ln[:, :, :].rearrange("p i c -> p (i c)"), d["ln"]).then_inc(S["ld_ln"], 16)
            load_xT(0)
            for k, (src, _, _, _, cols) in enumerate(split):
                if k >= NSTAGE:
                    sp.wait_ge(S["wsplit_lo"], k - NSTAGE + 1)
                sp.dma_start(stage[k % NSTAGE][:, 0:cols], src).then_inc(wload[k % NSTAGE], 16)
                if k == 3:
                    load_x(0)
                    load_ctx_a(0)
            load_xT(1)
            load_x(1)
            load_ctx_a(1)
            load_ctx_b(0)
            with sp.Fori(2, GROUPS) as n:
                load_xT(n)
                load_x(n)
                load_ctx_a(n)
                load_ctx_b(n - 1)
                store(n - 2)
            load_ctx_b(GROUPS - 1)
            store(GROUPS - 2)
            store(GROUPS - 1)
            for t in range(TILES):
                sp.wait_ge(stored[t], 16 * GROUPS)

        @block.scalar
        def _(act):
            for c in range(HC):
                act.dma_start(w_cq[:, c, :], d["L0_xattn_cq_w"][c * P:(c + 1) * P, :]).then_inc(S["ld_wa"], 16)
                for e, k in enumerate("vl"):
                    act.dma_start(w_dense[:, c, e, :], d[f"L0_xattn_{k}_dense"][c * P:(c + 1) * P, :]).then_inc(S["ld_wa"], 16)
            act.dma_start(w_ckv[:, :], d["L0_xattn_ckv_w"]).then_inc(S["ld_wa"], 16)
            act.dma_start(w_cdense[:, :], d["L0_xattn_cdense_w"]).then_inc(S["ld_wa"], 16)
            act.dma_start(w_mem[:, :], d["W_memT"]).then_inc(S["ld_wb"], 16)
            act.dma_start(w_gate[:, :, :], d["W_gateT"].rearrange("(c p) n -> p c n", p=P)).then_inc(S["ld_wb"], 16)
            for e, k in enumerate("vl"):
                act.dma_start(w_down[:, 0:NJ - 1, e, :],
                              d[f"L0_xattn_{k}_down"][0:(NJ - 1) * JW, :].rearrange("(j p) n -> p j n", p=JW)).then_inc(S["ld_wb"], 16)
                act.dma_start(w_down[0:JWS[-1], NJ - 1, e, :], d[f"L0_xattn_{k}_down"][(NJ - 1) * JW:INTER, :]).then_inc(S["ld_wb"], 16)
            act.wait_ge(S["ld_ln"], 16)
            for k, (_, (i, c), hi, _, cols) in enumerate(split):
                act.wait_ge(wload[k % NSTAGE], 16 * (k // NSTAGE + 1))
                act.activation(hi, stage[k % NSTAGE][:, 0:cols], ACT.Copy, scale=ln[:, i, c:c + 1]).then_inc(S["wsplit_hi"], 1)

            def square_sum(src, scratch, k, t, done):
                act.activation(scratch, src, ACT.Square, scale=H ** -0.5, accum_out=ss[:, k, t:t + 1]).then_inc(done, 1)

            def xsplit(n, t):
                act.wait_ge(S["ld_xT"], 16 * n + 16)
                if not first(n):
                    act.wait_ge(S["v_ps"], tl(n, 1) - 2)
                act.activation(xs[1][0][:, :, :], xT[:, :, :], ACT.Copy).then_inc(S["xh_ready"], 1)
                act.wait_ge(S["ld_x"], 16 * n + 16)
                for t in range(TILES):
                    if not first(n):
                        act.wait_ge(S["ss2"], tl(n, t) - 2)
                    square_sum(x_sb[:, t, :], att[t][:, :], 0, t, S["ssx"])

            def rope_v(n, t):
                act.wait_ge(S["v_ps"], tl(n, t))
                act.wait_ge(S["r1"], tl(n, t))
                v = Y[t][:, 0:H].rearrange("p (a e k) -> p a e k", e=2, k=HD)
                for b in range(2):
                    rows = slice(b * SEQ, (b + 1) * SEQ)
                    for e in range(2):
                        act.activation(vb[t][e * SEQ:(e + 1) * SEQ, b, :, e, 0:HD], v[rows, :, e, :], ACT.Copy,
                                       scale=rstd[rows, 0, t:t + 1]).then_inc(S["vb_ready"], 1)

            def qkT(n, t):
                act.wait_ge(S["q_ps"], tl(n, t))
                act.activation(qT[t][:, :, :], Z[t][:, :].rearrange("p (g q) -> p g q", g=4), ACT.Copy).then_inc(S["qT_ready"], 1)

            def score(n, t):
                act.wait_ge(S["sub_ready"], tl(n, t))
                act.activation(E[t][:, :], E[t][:, :], ACT.Exp, scale=HD ** -0.5).then_inc(S["exp_ready"], 1)

            def probT(n, t):
                act.wait_ge(S["pT_psx"], tl(n, t))
                act.activation(pT[t][:, 0:4, :], X[t].rearrange("p (a q) -> p a q", a=4), ACT.Copy).then_inc(S["pT_readyx"], 1)

            def ctxT(n, t):
                act.wait_ge(S["attT_ps"], tl(n, t))
                act.activation(attT[t][:, :, :], Y[t][:, 0:H].rearrange("p (c q) -> p c q", c=HC), ACT.Copy).then_inc(S["attT_ready"], 1)

            def dense(n, t):
                act.wait_ge(S["h1_ready"], tl(n, t))
                square_sum(h1[t][:, :], att[t][:, :], 1, t, S["ss1"])

            def h1T_(n, t):
                act.wait_ge(S["h1T_ps"], tl(n, t))
                act.activation(h1T[t][:, :, :], Z[t][:, 0:H].rearrange("p (c q) -> p c q", c=HC), ACT.Copy).then_inc(S["h1T_ready"], 1)

            def cproj(n, t):
                act.wait_ge(S["ckv_ps"], tl(n, t))
                for b in range(2):
                    rows = slice(b * SEQ, (b + 1) * SEQ)
                    act.activation(qkz[t][rows, 2:4, b * SEQ:(b + 1) * SEQ],
                                   X[t][rows, 0:CC].rearrange("p (g c) -> p g c", g=2), ACT.Copy).then_inc(S["ck_ev"], 1)
                v = X[t][:, CC:2 * CC].rearrange("p (a e k) -> p a e k", e=2, k=CHD)
                for b in range(2):
                    rows = slice(b * SEQ, (b + 1) * SEQ)
                    for e in range(2):
                        act.activation(cvb[t][e * SEQ:(e + 1) * SEQ, b, :, e, 0:CHD], v[rows, :, e, :], ACT.Copy).then_inc(S["cvb_ready"], 1)

            def cqkT(n, t):
                act.wait_ge(S["cQ_ps"], tl(n, t))
                act.activation(qT[t][:, 0:2, :], Z[t][:, 0:2 * P].rearrange("p (g q) -> p g q", g=2), ACT.Copy).then_inc(S["cqT_ready"], 1)

            def cscore(n, t):
                act.wait_ge(S["csub"], tl(n, t))
                act.activation(E[t][:, :], E[t][:, :], ACT.Exp, scale=CHD ** -0.5).then_inc(S["cexp"], 1)

            def cprobT(n, t):
                act.wait_ge(S["cpT_psx"], tl(n, t))
                act.activation(pT[t][:, 0:4, :], X[t].rearrange("p (a q) -> p a q", a=4), ACT.Copy).then_inc(S["cpT_readyx"], 1)

            def cctxT(n, t):
                act.wait_ge(S["cattT_ps"], tl(n, t))
                act.activation(attT[t][:, 0, :], Y[t][:, 0:CC], ACT.Copy).then_inc(S["cattT_ready"], 1)

            def cdense(n, t):
                act.wait_ge(S["h2_ready"], tl(n, t))
                square_sum(h2[t][:, :], att[t][:, :], 2, t, S["ss2"])

            def miT(n, t):
                act.wait_ge(S["miT_ps"], n + 1)
                if not first(n):
                    act.wait_ge(S["gu_ps"], NJ * n)
                act.activation(ms[1][0][:, :, :], B[0][:, :].rearrange("p (c q) -> p c q", c=HC), ACT.Copy).then_inc(S["mh_ready"], 1)

            def mlp(n, j):
                act.wait_ge(S["gu_ps"], NJ * n + j + 1)
                if j >= 2:
                    act.wait_ge(S["gt_ready"], NJ * n + j - 1)
                act.activation(th[j % 2][0:JWS[j], :], B[(j + 1) % 2][0:JWS[j], 0:GT], ACT.Tanh, scale=0.5).then_inc(S["th_ready"], 1)

            def h3T_(n, t):
                act.wait_ge(S["h3T_ps"], tl(n, t))
                act.activation(h3T[t][:, :, :], B[t][:, 0:H].rearrange("p (c q) -> p c q", c=HC), ACT.Copy).then_inc(S["h3T_ready"], 1)

            def mem(n, t):
                act.wait_ge(S["mem_ps"], tl(n, t))
                act.activation(mp[t][:, :], B[t][:, :], ACT.Copy).then_inc(S["mem_ready"], 1)

            def mscore(n, t):
                act.wait_ge(S["mmaxs"], tl(n, t))
                act.activation(mw[t][:, :], B[t][:, 0:P], ACT.Exp, scale=H ** -0.5, bias=mm[:, t, 1:2],
                               accum_out=mm[:, t, 2:3]).then_inc(S["mexp"], 1)

            def attnT(n, t):
                act.wait_ge(S["mwT_ps"], tl(n, t))
                act.activation(mwT[t][:, :], B[t][:, P:2 * P], ACT.Copy).then_inc(S["mwT_ready"], 1)

            def mc_(n, t):
                act.wait_ge(S["mc_ps"], tl(n, t))
                act.activation(mc[t][:, :], B[t][:, :], ACT.Copy).then_inc(S["mc_ready"], 1)

            def gate(n, t):
                act.wait_ge(S["zb_ready"], tl(n, t))
                act.activation(z[t][:, :], z[t][:, :], ACT.Tanh, scale=0.5).then_inc(S["tz_ready"], 1)
                act.wait_ge(S["fused_ready"], tl(n, t))
                square_sum(h3[t][:, :], z[t][:, :], 3, t, S["ss4"])

            run(act, dict(xsplit=xsplit, rope=rope_v, qkT=qkT, score=score, probT=probT, ctxT=ctxT, dense=dense, h1T=h1T_,
                          cproj=cproj, cqkT=cqkT, cscore=cscore, cprobT=cprobT, cctxT=cctxT, cdense=cdense, miT=miT, mlp=mlp,
                          h3T=h3T_, mem=mem, mscore=mscore, attnT=attnT, mc=mc_, gate=gate))

        @block.vector
        def _(dve):
            dve.wait_ge(S["ld_cst"], 16)
            dve.tensor_copy(ident_h[:, :], ident).then_inc(S["cst_ready"], 1)
            dve.tensor_copy(causal_h[:, :, :], cst[:, C_CAUS:C_CAUS + SEQ].unsqueeze(1).to_broadcast([P, 8, SEQ])).then_inc(S["cst_ready"], 1)
            dve.tensor_copy(block_h[:, :], cst[:, C_BLK:C_BLK + P]).then_inc(S["cst_ready"], 1)
            dve.wait_ge(S["ld_pos"], 32)
            dve.tensor_copy(pos_f[:, 0, :], pos_i[:, :]).then_inc(S["pos_step"], 1)
            dve.wait_ge(S["pos_step"], 1)
            dve.tensor_scalar(pos_f[:, 1, :], pos_f[:, 0, :], 0.0, float(SEQ), ALU.is_lt, ALU.mult).then_inc(S["pos_step"], 1)
            dve.wait_ge(S["pos_step"], 2)
            dve.tensor_tensor(pos_f[:, 2, :], pos_f[:, 0, :], pos_f[:, 1, :], ALU.add).then_inc(S["pos_step"], 1)
            dve.wait_ge(S["pos_step"], 3)
            dve.tensor_scalar(pos_f[:, 0, :], pos_f[:, 2, :], 0.0, float(SEQ - 1), ALU.max, ALU.min).then_inc(S["pos_step"], 1)
            dve.wait_ge(S["pos_step"], 4)
            dve.tensor_scalar(pos_f[:, 1, :], pos_f[:, 0, :], cst[0:SEQ, C_IOTA:C_IOTA + 1], None, ALU.is_equal).then_inc(S["hot_ready"], 1)
            dve.wait_ge(S["rope_ps"], 1)
            dve.tensor_copy(rope[:, :], Z[0][:, 0:2 * HD]).then_inc(S["rope_ready"], 1)
            dve.wait_ge(S["route_ps"], 1)
            dve.tensor_copy(route_t[:, 0, :], Z[1][:, 0:TILES * GROUPS]).then_inc(S["route_t_ready"], 1)
            dve.tensor_scalar(route_t[:, 1, :], Z[1][:, 0:TILES * GROUPS], -1.0, 1.0, ALU.mult, ALU.add).then_inc(S["route_t_ready"], 1)
            dve.wait_ge(S["ld_ln"], 16)
            dve.wait_ge(S["ld_wa"], 16 * 8)
            for c in range(HC):
                dve.tensor_scalar(w_cq[:, c, :], w_cq[:, c, :], ln[:, 1, c:c + 1], None, ALU.mult).then_inc(S["cq_ready"], 1)
            for k, (_, (i, c), hi, lo, cols) in enumerate(split):
                dve.wait_ge(S["wsplit_hi"], k + 1)
                dve.scalar_tensor_tensor(out=lo, in0=stage[k % NSTAGE][:, 0:cols], scalar=ln[:, i, c:c + 1], in1=hi.bitcast(F32),
                                         op0=ALU.mult, op1=ALU.subtract).then_inc(S["wsplit_lo"], 1)

            def xsplit(n, t):
                dve.wait_ge(S["xh_ready"], n + 1)
                dve.tensor_tensor(xs[1][1][:, :, :], xT[:, :, :], xs[1][0][:, :, :].bitcast(F32), ALU.subtract).then_inc(S["xl_ready"], 1)
                for t in range(TILES):
                    dve.wait_ge(S["r1"], tl(n, t))
                    dve.tensor_scalar(rope_r[:, t, :], rope[:, :], rstd[:, 0, t:t + 1], None, ALU.mult).then_inc(S["roper"], 1)

            def rope_q(n, t):
                dve.wait_ge(S["qk_ps"], tl(n, t))
                dve.wait_ge(S["roper"], tl(n, t))
                if not first(n):
                    dve.wait_ge(S["cpT_psy"], tl(n, t) - 2)
                qk = X[t].rearrange("p (h d) -> p h d", d=HD)
                straight = E[t][:, 0:2 * H].rearrange("p (h d) -> p h d", d=HD)
                turned = E[t][:, 2 * H:4 * H].rearrange("p (h d) -> p h d", d=HD)
                hd2 = HD // 2

                def table(a, b):
                    return rope_r[:, t, a:b].unsqueeze(1).to_broadcast([P, 2 * NH, b - a])
                dve.tensor_tensor(straight, qk, table(0, HD), ALU.mult).then_inc(S["rope_a"], 1)
                dve.tensor_tensor(turned[:, :, 0:hd2], qk[:, :, hd2:HD], table(HD, HD + hd2), ALU.mult).then_inc(S["rope_b"], 1)
                dve.tensor_tensor(turned[:, :, hd2:HD], qk[:, :, 0:hd2], table(HD + hd2, 2 * HD), ALU.mult).then_inc(S["rope_b"], 1)

            def expand(t, groups, heads, mask, done):
                k = Y[t][:, 0:groups * SEQ].rearrange("p (g k) -> p g k", g=groups)
                dve.tensor_tensor(kT[t][:, :].rearrange("p (g h k) -> p g h k", g=groups, h=heads),
                                  k.unsqueeze(2).to_broadcast([P, groups, heads, SEQ]),
                                  mask.unsqueeze(1).unsqueeze(3).to_broadcast([P, groups, heads, SEQ]), ALU.mult).then_inc(done, 1)

            def qkT(n, t):
                dve.wait_ge(S["k_ps"], tl(n, t))
                expand(t, 4, 4, cst[:, C_H16:C_H16 + 4], S["kT_ready"])

            def max_sub(t, n, s_ps, max_ready, sub_ready):
                s = xy[t][:, :, :].rearrange("p b (h k) -> p (b h) k", k=SEQ)
                dve.wait_ge(s_ps, tl(n, t))
                dve.tensor_reduce(mx[:, t, :], s, AX.X, ALU.max).then_inc(max_ready, 1)
                dve.wait_ge(max_ready, tl(n, t))
                dve.tensor_tensor(E[t][:, :].rearrange("p (h k) -> p h k", k=SEQ), s,
                                  mx[:, t, :].unsqueeze(2).to_broadcast([P, NH, SEQ]), ALU.subtract).then_inc(sub_ready, 1)

            def score(n, t):
                max_sub(t, n, S["s_ps"], S["max_ready"], S["sub_ready"])

            def probT(n, t):
                dve.wait_ge(S["pT_psy"], tl(n, t))
                dve.tensor_copy(pT[t][:, 4:8, :], Y[t].rearrange("p (a q) -> p a q", a=4)).then_inc(S["pT_ready"], 1)

            def normed(t, n, hd, pv_ps, rec_ready, done):
                o = Z[t][:, 0:NH * (hd + 1)].rearrange("p (h d) -> p h d", d=hd + 1)
                dve.wait_ge(pv_ps, tl(n, t))
                dve.reciprocal(rec[:, t, :], o[:, :, hd]).then_inc(rec_ready, 1)
                dve.wait_ge(rec_ready, tl(n, t))
                dve.tensor_tensor(att[t][:, 0:NH * hd].rearrange("p (h d) -> p h d", d=hd), o[:, :, 0:hd],
                                  rec[:, t, :].unsqueeze(2).to_broadcast([P, NH, hd]), ALU.mult).then_inc(done, 1)

            def pv(n, t):
                normed(t, n, HD, S["pv_ps"], S["rec_ready"], S["att_ready"])

            def routed_add(out_, ps, rest, n, t, mid, done):
                dve.scalar_tensor_tensor(out=out_, in0=ps[:, 0:H], scalar=route_t[:, 0, bass.ds(2 * n + t, 1)], in1=rest,
                                         op0=ALU.mult, op1=ALU.add).then_inc(mid, 1)
                dve.wait_ge(mid, tl(n, t))
                dve.scalar_tensor_tensor(out=out_, in0=ps[:, H:2 * H], scalar=route_t[:, 1, bass.ds(2 * n + t, 1)], in1=out_,
                                         op0=ALU.mult, op1=ALU.add).then_inc(done, 1)

            def dense(n, t):
                dve.wait_ge(S["dense_ps"], tl(n, t))
                if not first(n):
                    dve.wait_ge(S["h2_ready"], tl(n, t) - 2)
                routed_add(h1[t][:, :], X[t], x_sb[:, t, :], n, t, S["h1a"], S["h1_ready"])

            def cproj(n, t):
                dve.wait_ge(S["cq_ps"], tl(n, t))
                dve.wait_ge(S["r2"], tl(n, t))
                for b in range(2):
                    rows = slice(b * SEQ, (b + 1) * SEQ)
                    dve.tensor_scalar(qkz[t][rows, 0:2, b * SEQ:(b + 1) * SEQ],
                                      Y[t][rows, 0:CC].rearrange("p (g c) -> p g c", g=2),
                                      rstd[rows, 1, t:t + 1], None, ALU.mult).then_inc(S["cq_ev"], 1)

            def cqkT(n, t):
                dve.wait_ge(S["cK_ps"], tl(n, t))
                expand(t, 2, 8, cst[:, C_H8:C_H8 + 8], S["ckT_ready"])

            def cscore(n, t):
                max_sub(t, n, S["cs_ps"], S["cmax"], S["csub"])

            def cprobT(n, t):
                dve.wait_ge(S["cpT_psy"], tl(n, t))
                dve.tensor_copy(pT[t][:, 4:8, :], Y[t].rearrange("p (a q) -> p a q", a=4)).then_inc(S["cpT_ready"], 1)

            def cpv(n, t):
                normed(t, n, CHD, S["cpv_ps"], S["crec"], S["catt_ready"])

            def cdense(n, t):
                dve.wait_ge(S["cdense_ps"], tl(n, t))
                if not first(n):
                    dve.wait_ge(S["h3_ready"], tl(n, t) - 2)
                dve.tensor_tensor(h2[t][:, :], X[t][:, 0:H], h1[t][:, :], ALU.add).then_inc(S["h2_ready"], 1)

            def miT(n, t):
                dve.wait_ge(S["mh_ready"], n + 1)
                dve.tensor_tensor(ms[1][1][:, :, :], B[0][:, :].rearrange("p (c q) -> p c q", c=HC),
                                  ms[1][0][:, :, :].bitcast(F32), ALU.subtract).then_inc(S["ml_ready"], 1)

            def mlp(n, j):
                w, g, u = JWS[j], B[(j + 1) % 2][0:JWS[j], 0:GT], B[(j + 1) % 2][0:JWS[j], GT:2 * GT]
                dve.wait_ge(S["th_ready"], NJ * n + j + 1)
                if not first(n):
                    dve.wait_ge(S["down_ps"], tl(n, 1) - 2)
                dve.scalar_tensor_tensor(out=hid[0:w, j, :], in0=th[j % 2][0:w, :], scalar=1.0, in1=g,
                                         op0=ALU.add, op1=ALU.mult).then_inc(S["gt_ready"], 1)
                dve.wait_ge(S["gt_ready"], NJ * n + j + 1)
                dve.scalar_tensor_tensor(out=hid[0:w, j, :], in0=hid[0:w, j, :], scalar=0.5, in1=u,
                                         op0=ALU.mult, op1=ALU.mult).then_inc(S["hid_ready"], 1)

            def down(n, t):
                dve.wait_ge(S["down_ps"], tl(n, t))
                if not first(n):
                    dve.wait_ge(S["out_ready"], tl(n, t) - 2)
                routed_add(h3[t][:, :], B[t], h2[t][:, :], n, t, S["h3a"], S["h3_ready"])

            def mscore(n, t):
                dve.wait_ge(S["ms_ps"], tl(n, t))
                dve.tensor_reduce(mm[:, t, 0:1], B[t][:, 0:P], AX.X, ALU.max, negate=True).then_inc(S["mmax"], 1)
                dve.wait_ge(S["mmax"], tl(n, t))
                dve.tensor_scalar(mm[:, t, 1:2], mm[:, t, 0:1], H ** -0.5, None, ALU.mult).then_inc(S["mmaxs"], 1)
                dve.wait_ge(S["mexp"], tl(n, t))
                dve.reciprocal(mm[:, t, 3:4], mm[:, t, 2:3]).then_inc(S["mrec"], 1)
                dve.wait_ge(S["mrec"], tl(n, t))
                dve.tensor_scalar(mw[t][:, :], mw[t][:, :], mm[:, t, 3:4], None, ALU.mult).then_inc(S["mw_ready"], 1)

            def gate(n, t):
                dve.wait_ge(S["gate_ps"], tl(n, t))
                if n is not None and t == 0:
                    dve.wait_ge(S["ld_rest"], 16 * 2)
                dve.tensor_tensor(z[t][:, :], B[t][:, 0:H], b_gate[:, :], ALU.add).then_inc(S["zb_ready"], 1)
                dve.wait_ge(S["tz_ready"], tl(n, t))
                dve.scalar_tensor_tensor(out=z[t][:, :], in0=z[t][:, :], scalar=1.0, in1=mc[t][:, 0:H],
                                         op0=ALU.add, op1=ALU.mult).then_inc(S["gm_ready"], 1)
                dve.wait_ge(S["gm_ready"], tl(n, t))
                dve.scalar_tensor_tensor(out=h3[t][:, :], in0=z[t][:, :], scalar=0.5, in1=h3[t][:, :],
                                         op0=ALU.mult, op1=ALU.add).then_inc(S["fused_ready"], 1)
                dve.wait_ge(S["r4"], tl(n, t))
                if not first(n):
                    dve.wait_ge(stored[t], 16 * n)
                dve.scalar_tensor_tensor(out=res[t][:, :], in0=h3[t][:, :], scalar=rstd[:, 3, t:t + 1], in1=w_norm[:, :],
                                         op0=ALU.mult, op1=ALU.mult).then_inc(S["out_ready"], 1)

            run(dve, dict(xsplit=xsplit, rope=rope_q, qkT=qkT, score=score, probT=probT, pv=pv, dense=dense, cproj=cproj,
                          cqkT=cqkT, cscore=cscore, cprobT=cprobT, cpv=cpv, cdense=cdense, miT=miT, mlp=mlp, down=down,
                          mscore=mscore, gate=gate))

        @block.gpsimd
        def _(pool):
            pool.dma_start(pos_i[:, 0:SEQ], d["pos"][0, :].partition_broadcast(SEQ)).then_inc(S["ld_pos"], 16)
            pool.dma_start(pos_i[:, SEQ:P], d["pos"][0, :].partition_broadcast(SEQ)).then_inc(S["ld_pos"], 16)
            half_tok = N_TOK // 2
            for k in range(2):
                pool.dma_start(kT[k][:, :].bitcast(I32), d["types"][0, k * half_tok:(k + 1) * half_tok].partition_broadcast(P)).then_inc(S["ld_types"], 16)
            pool.dma_start(b_gate[:, :], d["b_gate"].partition_broadcast(P)).then_inc(S["ld_rest"], 16)
            pool.dma_start(w_norm[:, :], d["w_norm"].partition_broadcast(P)).then_inc(S["ld_rest"], 16)
            pool.memset(pow_eps[:, 0:1], -0.5).then_inc(S["small_ready"], 1)
            pool.memset(pow_eps[:, 1:2], EPS).then_inc(S["small_ready"], 1)
            pool.memset(ones[:, :], 1.0).then_inc(S["small_ready"], 1)
            pool.memset(route[:, SEQ - 1:N_TOK:SEQ], 0.0).then_inc(S["route_ready"], 1)
            pool.wait_ge(S["ld_types"], 32)
            for k in range(2):
                pool.tensor_scalar(kT[k][:, :], kT[k][:, :].bitcast(I32), 1.0, None, ALU.is_equal).then_inc(S["type_step"], 1)
            pool.wait_ge(S["type_step"], 2)
            for k in range(2):
                hot = kT[k][:, :].rearrange("p (b s) -> p b s", s=SEQ)
                pool.tensor_tensor(route[:, k * half_tok:(k + 1) * half_tok].rearrange("p (b s) -> p b s", s=SEQ)[:, :, 0:SEQ - 1],
                                   hot[:, :, 0:SEQ - 1], hot[:, :, 1:SEQ], ALU.mult).then_inc(S["route_ready"], 1)
            pool.wait_ge(S["small_ready"], 3)
            for t in range(TILES):
                pool.memset(qkz[t][:, :, :], 0.0).then_inc(S["zeroed"], 1)
                pool.memset(vb[t][:, :, :, :, :], 0.0).then_inc(S["zeroed"], 1)
                pool.memset(cvb[t][:, :, :, :, :], 0.0).then_inc(S["zeroed"], 1)
            pool.wait_ge(S["zeroed"], 3 * TILES)
            for t in range(TILES):
                for e in range(2):
                    rows = slice(e * SEQ, (e + 1) * SEQ)
                    pool.memset(vb[t][rows, :, :, e, HD:HD + 1], 1.0).then_inc(S["zeroed"], 1)
                    pool.memset(cvb[t][rows, :, :, e, CHD:CHD + 1], 1.0).then_inc(S["zeroed"], 1)
                    pool.wait_ge(S["zeroed"], 3 * TILES + 4 * t + 2 * e + 2)

            def inv_rms(k, t, n, sums, mid, done):
                pool.wait_ge(sums, tl(n, t))
                pool.tensor_tensor(var[:, k, t:t + 1], ss[:, k, t:t + 1], pow_eps[:, 1:2], ALU.add).then_inc(mid, 1)
                pool.wait_ge(mid, tl(n, t))
                pool.tensor_tensor(rstd[:, k, t:t + 1], var[:, k, t:t + 1], pow_eps[:, 0:1], ALU.pow).then_inc(done, 1)

            def parts(n, s, hi_ready, lo_ready, mv, ready):
                m = route[:, bass.ds(n * GT, GT)].unsqueeze(1).to_broadcast([P, HC, GT])
                for k in range(2):
                    pool.wait_ge(S["route_ready"], 3)
                    pool.wait_ge((hi_ready, lo_ready)[k], n + 1)
                    pool.tensor_tensor(s[0][k][:, :, :], s[1][k][:, :, :].bitcast(F32), m, ALU.mult).then_inc(mv, 1)
                for k in range(2):
                    pool.wait_ge(mv, 2 * n + k + 1)
                    pool.tensor_tensor(s[1][k][:, :, :], s[1][k][:, :, :].bitcast(F32), s[0][k][:, :, :].bitcast(F32),
                                       ALU.subtract).then_inc(ready, 1)

            def xsplit(n, t):
                for t in range(TILES):
                    inv_rms(0, t, n, S["ssx"], S["r1v"], S["r1"])
                parts(n, xs, S["xh_ready"], S["xl_ready"], S["xv_ready"], S["xs_ready"])

            def rope_add(n, t):
                pool.wait_ge(S["rope_a"], tl(n, t))
                pool.wait_ge(S["rope_b"], 4 * n + 2 * t + 2)
                for b in range(2):
                    rows = slice(b * SEQ, (b + 1) * SEQ)
                    pool.tensor_tensor(qkz[t][rows, :, b * SEQ:(b + 1) * SEQ],
                                       E[t][rows, 0:2 * H].rearrange("p (g c) -> p g c", g=8),
                                       E[t][rows, 2 * H:4 * H].rearrange("p (g c) -> p g c", g=8), ALU.add).then_inc(S["qkz_ready"], 1)
                    pool.wait_ge(S["qkz_ready"], 4 * n + 2 * t + b + 1)

            def dense(n, t):
                inv_rms(1, t, n, S["ss1"], S["r2v"], S["r2"])

            def cdense(n, t):
                inv_rms(2, t, n, S["ss2"], S["r3v"], S["r3"])
                pool.wait_ge(S["r3"], tl(n, t))
                if not first(n):
                    pool.wait_ge(S["miT_ps"], n)
                pool.tensor_tensor(mi[t][:, :], h2[t][:, :], rstd[:, 2, t:t + 1].to_broadcast([P, H]), ALU.mult).then_inc(S["mi_ready"], 1)

            def miT(n, t):
                parts(n, ms, S["mh_ready"], S["ml_ready"], S["mv_ready"], S["ms_ready"])

            def gate(n, t):
                inv_rms(3, t, n, S["ss4"], S["r4v"], S["r4"])

            run(pool, dict(xsplit=xsplit, rope=rope_add, dense=dense, cdense=cdense, miT=miT, gate=gate))

        @block.tensor
        def _(pe):
            def split_product(o, stationary, moving, start, stop):
                (sh, sl), (mh, ml) = stationary, moving
                pe.matmul(o, sh, mh, start=start, stop=False)
                pe.matmul(o, sh, ml, start=False, stop=False)
                return pe.matmul(o, sl, mh, start=False, stop=stop)

            pe.wait_ge(S["ld_cst"], 16)
            pe.wait_ge(S["hot_ready"], 1)
            pe.matmul(Z[0][:, 0:2 * HD], pos_f[:, 1, :], cst[0:SEQ, C_ROPE:C_ROPE + 2 * HD], start=True, stop=True).then_inc(S["rope_ps"], 1)
            pe.wait_ge(S["route_ready"], 3)
            pe.wait_ge(S["small_ready"], 3)
            for i in range(TILES * GROUPS):
                last = pe.matmul(Z[1][:, i:i + 1], route[0:1, i * P:(i + 1) * P], ones[:, :], start=True, stop=True)
            last.then_inc(S["route_ps"], 1)

            def qkv(n, t):
                cols = slice(t * P, (t + 1) * P)
                pe.wait_ge(S["xs_ready"], 2 * n + 2)
                if first(n):
                    pe.wait_ge(S["wsplit_lo"], 4)
                    pe.wait_ge(S["zeroed"], 7 * TILES)
                else:
                    pe.wait_ge(S["h2_ready"], tl(n, t) - 2)
                for o, a, b, done in ((X[t], 0, 2 * H, S["qk_ps"]), (Y[t][:, 0:H], 2 * H, 3 * H, S["v_ps"])):
                    for e in range(2):
                        for c in range(HC):
                            last = split_product(o, [xs[e][s][:, c, cols] for s in range(2)], [w_qkv[s][:, e, c, a:b] for s in range(2)],
                                                 start=(e == 0 and c == 0), stop=(e == 1 and c == HC - 1))
                    last.then_inc(done, 1)

            def turn(n, t, groups, q_ps, k_ps):
                for g in range(groups):
                    last = pe.transpose(Z[t][:, g * P:(g + 1) * P], qkz[t][:, g, :], ident)
                last.then_inc(q_ps, 1)
                for g in range(groups):
                    last = pe.matmul(Y[t][:, g * SEQ:(g + 1) * SEQ], qkz[t][:, groups + g, :], cst[:, C_ST:C_ST + SEQ], start=True, stop=True)
                last.then_inc(k_ps, 1)

            def qkT(n, t):
                pe.wait_ge(S["qkz_ready"], 4 * n + 2 * t + 2)
                pe.wait_ge(S["vb_ready"], 4 * tl(n, t))
                turn(n, t, 4, S["q_ps"], S["k_ps"])

            def score(n, t):
                pe.wait_ge(S["qT_ready"], tl(n, t))
                pe.wait_ge(S["kT_ready"], tl(n, t))
                for b in range(2):
                    pe.matmul(xy[t][:, b, :], ident_h[:, :], causal_h[:, :, :].rearrange("p h k -> p (h k)"), start=True, stop=False)
                    for g in (2 * b, 2 * b + 1):
                        last = pe.matmul(xy[t][:, b, (g % 2) * GT:(g % 2 + 1) * GT], qT[t][:, g, :], kT[t][:, g * GT:(g + 1) * GT],
                                         start=False, stop=(g % 2 == 1))
                last.then_inc(S["s_ps"], 1)

            def turn_probs(t, psx, psy):
                for a in range(PAIRS):
                    last = pe.transpose(xy[t][:, a // 4, (a % 4) * P:(a % 4 + 1) * P], E[t][:, a * P:(a + 1) * P], ident)
                    if a == 3:
                        last.then_inc(psx, 1)
                last.then_inc(psy, 1)

            def probT(n, t):
                pe.wait_ge(S["exp_ready"], tl(n, t))
                turn_probs(t, S["pT_psx"], S["pT_psy"])

            def apply(t, v, hd, done):
                for b in range(2):
                    for a in range(PAIRS):
                        last = pe.matmul(Z[t][b * SEQ:(b + 1) * SEQ, a * 2 * (hd + 1):(a + 1) * 2 * (hd + 1)],
                                         pT[t][:, a, b * SEQ:(b + 1) * SEQ], v[t][:, b, a, :, :].rearrange("p e k -> p (e k)"),
                                         start=True, stop=True)
                last.then_inc(done, 1)

            def pv(n, t):
                pe.wait_ge(S["pT_readyx"], tl(n, t))
                pe.wait_ge(S["pT_ready"], tl(n, t))
                apply(t, vb, HD, S["pv_ps"])

            def ctxT(n, t):
                pe.wait_ge(S["att_ready"], tl(n, t))
                for c in range(HC):
                    last = pe.transpose(Y[t][:, c * P:(c + 1) * P], att[t][:, c * P:(c + 1) * P], ident)
                last.then_inc(S["attT_ps"], 1)

            def dense(n, t):
                pe.wait_ge(S["attT_ready"], tl(n, t))
                if first(n):
                    pe.wait_ge(S["ld_wa"], 16 * 8)
                for c in range(HC):
                    last = pe.matmul(X[t], attT[t][:, c, :], w_dense[:, c, :, :].rearrange("p e n -> p (e n)"), start=(c == 0), stop=(c == HC - 1))
                last.then_inc(S["dense_ps"], 1)

            def h1T_(n, t):
                pe.wait_ge(S["h1_ready"], tl(n, t))
                for c in range(HC):
                    last = pe.transpose(Z[t][:, c * P:(c + 1) * P], h1[t][:, c * P:(c + 1) * P], ident)
                last.then_inc(S["h1T_ps"], 1)

            def cproj(n, t):
                pe.wait_ge(S["ld_ca"], 16 * n + 16)
                pe.wait_ge(S["h1T_ready"], tl(n, t))
                if first(n):
                    pe.wait_ge(S["cq_ready"], HC)
                pe.matmul(X[t][:, 0:2 * CC], ctxT_a[:, t * P:(t + 1) * P], w_ckv[:, :], start=True, stop=True).then_inc(S["ckv_ps"], 1)
                for c in range(HC):
                    last = pe.matmul(Y[t][:, 0:CC], h1T[t][:, c, :], w_cq[:, c, :], start=(c == 0), stop=(c == HC - 1))
                last.then_inc(S["cq_ps"], 1)

            def cqkT(n, t):
                pe.wait_ge(S["cq_ev"], 2 * tl(n, t))
                pe.wait_ge(S["ck_ev"], 2 * tl(n, t))
                turn(n, t, 2, S["cQ_ps"], S["cK_ps"])

            def cscore(n, t):
                pe.wait_ge(S["cqT_ready"], tl(n, t))
                pe.wait_ge(S["ckT_ready"], tl(n, t))
                pe.wait_ge(S["cvb_ready"], 4 * tl(n, t))
                for g in range(2):
                    last = pe.matmul(xy[t][:, g, :], qT[t][:, g, :], kT[t][:, g * 512:(g + 1) * 512], start=True, stop=True)
                last.then_inc(S["cs_ps"], 1)

            def cprobT(n, t):
                pe.wait_ge(S["cexp"], tl(n, t))
                turn_probs(t, S["cpT_psx"], S["cpT_psy"])

            def cpv(n, t):
                pe.wait_ge(S["cpT_readyx"], tl(n, t))
                pe.wait_ge(S["cpT_ready"], tl(n, t))
                apply(t, cvb, CHD, S["cpv_ps"])

            def cctxT(n, t):
                pe.wait_ge(S["catt_ready"], tl(n, t))
                pe.transpose(Y[t][:, 0:CC], att[t][:, 0:CC], ident).then_inc(S["cattT_ps"], 1)

            def cdense(n, t):
                pe.wait_ge(S["cattT_ready"], tl(n, t))
                pe.matmul(X[t][:, 0:H], attT[t][:, 0, :], w_cdense[:, :], start=True, stop=True).then_inc(S["cdense_ps"], 1)

            def miT(n, t):
                if not first(n):
                    pe.wait_ge(S["out_ready"], 2 * n)
                for t in range(TILES):
                    pe.wait_ge(S["mi_ready"], tl(n, t))
                    for c in range(HC):
                        last = pe.transpose(B[0][:, c * GT + t * P:c * GT + (t + 1) * P], mi[t][:, c * P:(c + 1) * P], ident)
                last.then_inc(S["miT_ps"], 1)

            def mlp(n, j):
                w, bank = JWS[j], B[(j + 1) % 2]
                pe.wait_ge(S["ms_ready"], 2 * n + 2)
                if first(n) and j == 0:
                    pe.wait_ge(S["wsplit_lo"], len(split))
                if j >= 2:
                    pe.wait_ge(S["hid_ready"], NJ * n + j - 1)
                for g in range(2):
                    for e in range(2):
                        for c in range(HC):
                            last = split_product(bank[0:w, g * GT:(g + 1) * GT],
                                                 [w_gu[s][:, g, e, c, j * JW:j * JW + w] for s in range(2)],
                                                 [ms[e][s][:, c, :] for s in range(2)],
                                                 start=(e == 0 and c == 0), stop=(e == 1 and c == HC - 1))
                last.then_inc(S["gu_ps"], 1)

            def down(n, t):
                if t == 0:
                    pe.wait_ge(S["hid_ready"], NJ * n + NJ)
                if first(n):
                    pe.wait_ge(S["ld_wb"], 16 * 6)
                for j in range(NJ):
                    last = pe.matmul(B[t][:, :], hid[0:JWS[j], j, t * P:(t + 1) * P], w_down[0:JWS[j], j, :, :].rearrange("p e n -> p (e n)"),
                                     start=(j == 0), stop=(j == NJ - 1))
                last.then_inc(S["down_ps"], 1)

            def h3T_(n, t):
                pe.wait_ge(S["h3_ready"], tl(n, t))
                for c in range(HC):
                    last = pe.transpose(B[t][:, c * P:(c + 1) * P], h3[t][:, c * P:(c + 1) * P], ident)
                last.then_inc(S["h3T_ps"], 1)

            def mem(n, t):
                pe.wait_ge(S["ld_cb"], 16 * n + 16)
                pe.wait_ge(S["h3T_ready"], tl(n, t))
                tok = ctxT_b[:, t * P:(t + 1) * P]
                pe.matmul(B[t][:, 0:H], tok, w_mem[:, :], start=True, stop=True)
                for c in range(HC):
                    last = pe.matmul(B[t][:, H + c * P:H + (c + 1) * P], w_mem[:, c * P:(c + 1) * P], tok, start=True, stop=True)
                last.then_inc(S["mem_ps"], 1)

            def mscore(n, t):
                pe.wait_ge(S["mem_ready"], tl(n, t))
                pe.matmul(B[t][:, 0:P], ident_h[:, :], block_h[:, :], start=True, stop=False)
                for c in range(HC):
                    last = pe.matmul(B[t][:, 0:P], h3T[t][:, c, :], mp[t][:, H + c * P:H + (c + 1) * P], start=False, stop=(c == HC - 1))
                last.then_inc(S["ms_ps"], 1)

            def attnT(n, t):
                pe.wait_ge(S["mw_ready"], tl(n, t))
                pe.transpose(B[t][:, P:2 * P], mw[t][:, :], ident).then_inc(S["mwT_ps"], 1)

            def mc_(n, t):
                pe.wait_ge(S["mwT_ready"], tl(n, t))
                pe.matmul(B[t][:, 0:H], mwT[t][:, :], mp[t][:, 0:H], start=True, stop=True)
                for c in range(HC):
                    last = pe.matmul(B[t][:, H + c * P:H + (c + 1) * P], mp[t][:, c * P:(c + 1) * P], mwT[t][:, :], start=True, stop=True)
                last.then_inc(S["mc_ps"], 1)

            def gate(n, t):
                pe.wait_ge(S["mc_ready"], tl(n, t))
                for c in range(2 * HC):
                    lhs = h3T[t][:, c, :] if c < HC else mc[t][:, H + (c - HC) * P:H + (c - HC + 1) * P]
                    last = pe.matmul(B[t][:, 0:H], lhs, w_gate[:, c, :], start=(c == 0), stop=(c == 2 * HC - 1))
                last.then_inc(S["gate_ps"], 1)

            run(pe, dict(qkv=qkv, qkT=qkT, score=score, probT=probT, pv=pv, ctxT=ctxT, dense=dense, h1T=h1T_, cproj=cproj,
                         cqkT=cqkT, cscore=cscore, cprobT=cprobT, cpv=cpv, cctxT=cctxT, cdense=cdense, miT=miT, mlp=mlp,
                         down=down, h3T=h3T_, mem=mem, mscore=mscore, attnT=attnT, mc=mc_, gate=gate))


def kernel(**inputs):
    import concourse.bacc as bacc
    from concourse.bass_utils import run_bass_kernel_spmd

    a = {k: np.asarray(v) for k, v in inputs.items()}
    feeds = {k: a[k] for k in a if k.startswith("L0_xattn_") and not k.startswith("L0_xattn_ln_")}
    norms = [a["L0_xattn_" + k] for k in ("ln_in_w", "ln_post_cross_w", "ln_post_attn_w")]
    feeds.update(
        x=a["x"].reshape(N_TOK, H), xT=a["x"].reshape(N_TOK, H).T, ctxT=a["ctx_1024"].reshape(N_TOK, CC).T,
        types=a["mask_BxS_ik0"].reshape(1, N_TOK), pos=a["pos_1xS"],
        W_memT=a["L1_xattn_W_mem"].T, W_gateT=a["L1_xattn_W_gate"].T, b_gate=a["L1_xattn_b_gate"], w_norm=a["L1_xattn_norm_w"],
        ln=np.stack(norms).reshape(3 * HC, P).T, consts=shape_constants(),
    )
    nc = bacc.Bacc("TRN2", target_bir_lowering=False, num_devices=1)
    arrays, d = {}, {}
    for name, v in feeds.items():
        v = np.ascontiguousarray(v)
        arrays[f"in_{name}_dram"] = v
        d[name] = nc.dram_tensor(f"in_{name}_dram", v.shape, mybir.dt.from_np(v.dtype), kind="ExternalInput").ap()
    out = nc.dram_tensor("out_0_dram", (N_TOK, H), F32, kind="ExternalOutput").ap()
    xattn_kernel(nc, d, out)
    r = run_bass_kernel_spmd(nc, [arrays], core_ids=[0])
    return r.results[0]["out_0_dram"].reshape(BATCH, SEQ, H)
```

```python
from contextlib import ExitStack

import numpy as np

import concourse.bass as bass
from concourse import mybir

F32 = mybir.dt.float32
F32R = mybir.dt.float32r
BF16 = mybir.dt.bfloat16
I32 = mybir.dt.int32
ALU = mybir.AluOpType
ACT = mybir.ActivationFunctionType
AX = mybir.AxisListType

P = 128
BATCH, SEQ, H = 32, 64, 256
NH, HD = 16, 16
CC, CHD = 128, 8
INTER = 688
N_TOK = BATCH * SEQ
TILES = 2
GT = TILES * P
GROUPS = N_TOK // GT
HC = H // P
NJ = 6
JW = -(-INTER // NJ)
JWS = [min(JW, INTER - j * JW) for j in range(NJ)]
PAIRS = NH // 2
EPS = 1e-6
NEG = -1.0e30
C_ID, C_ST, C_H16, C_H8, C_CAUS, C_BLK, C_ROPE, C_IOTA, C_END = np.cumsum(
    [0, P, SEQ, 4, 8, SEQ, P, 2 * HD, 1]).tolist()


def shape_constants():
    c = np.zeros((P, C_END), np.float32)
    row = np.arange(P)
    c[:, C_ID:C_ID + P] = np.eye(P)
    c[:, C_ST:C_ST + SEQ] = np.tile(np.eye(SEQ), (2, 1))
    c[:, C_H16:C_H16 + 4] = (row[:, None] % 64) // HD == np.arange(4)
    c[:, C_H8:C_H8 + 8] = (row[:, None] % 64) // CHD == np.arange(8)
    c[:, C_CAUS:C_CAUS + SEQ] = np.where(np.arange(SEQ) <= row[:, None] % SEQ, 0, NEG)
    c[:, C_BLK:C_BLK + P] = np.where(row[:, None] // SEQ == row // SEQ, 0, NEG)
    inv = (np.float32(1.0) / np.float32(10000.0) ** (np.arange(0, HD, 2, dtype=np.float32) / np.float32(HD)))
    freq = np.outer(np.arange(SEQ, dtype=np.float32), inv.astype(np.float32)).astype(np.float32)
    sin = np.sin(freq)
    c[:SEQ, C_ROPE:C_ROPE + HD] = np.tile(np.cos(freq), (1, 2))
    c[:SEQ, C_ROPE + HD:C_ROPE + 2 * HD] = np.concatenate([-sin, sin], 1)
    c[:, C_IOTA] = row
    return c


def xattn_kernel(nc, d, out):
    ctx = ExitStack()
    with ctx:
        def sb(name, shape, dt=F32):
            return ctx.enter_context(nc.sbuf_tensor(name, shape, dt))

        def sem(name):
            return ctx.enter_context(nc.semaphore(name))

        w_qkv = [sb(f"w_qkv_{s}", [P, 2, HC, 3 * H], F32R) for s in ("hi", "lo")]
        w_gu = [sb(f"w_gu_{s}", [P, 2, 2, HC, INTER], F32R) for s in ("hi", "lo")]
        w_down = [sb(f"w_down_{s}", [JW, NJ, 2, H], F32R) for s in ("hi", "lo")]
        w_dense = sb("w_dense", [P, HC, 2, H])
        w_cq = sb("w_cq", [P, HC, CC])
        w_ckv = sb("w_ckv", [P, 2 * CC])
        w_cdense = sb("w_cdense", [P, H])
        w_mem = sb("w_mem", [P, H])
        w_gate = sb("w_gate", [P, 2 * HC, H])
        b_gate = sb("b_gate", [P, H])
        w_norm = sb("w_norm", [P, H])
        ln = sb("ln", [P, 3, HC])
        cst = sb("cst", [P, C_END])
        ident = cst[:, C_ID:C_ID + P]
        ident_h = sb("ident_h", [P, P], BF16)
        causal_h = sb("causal_h", [P, 8, SEQ], BF16)
        block_h = sb("block_h", [P, P], BF16)
        rope = sb("rope", [P, 2 * HD])
        route = sb("route", [P, N_TOK], BF16)
        ones = sb("ones", [1, 1], BF16)
        route_t = sb("route_t", [P, 2, TILES * GROUPS])
        pow_eps = sb("pow_eps", [P, 2])

        x_sb = sb("x_sb", [P, TILES, H])
        xT = sb("xT", [P, HC, GT])
        xs = [[sb(f"xs_{e}{s}", [P, HC, GT], F32R) for s in ("hi", "lo")] for e in "vl"]
        ctxT_a = sb("ctxT_a", [P, GT])
        ss = sb("ss", [P, 4, TILES])
        var = sb("var", [P, 4, TILES])
        rstd = sb("rstd", [P, 4, TILES])
        rope_r = sb("rope_r", [P, TILES, 2 * HD])
        qkz = [sb(f"qkz{t}", [P, 8, P]) for t in range(TILES)]
        qT = [sb(f"qT{t}", [P, 4, P]) for t in range(TILES)]
        kc = [sb(f"kc{t}", [P, 4 * SEQ]) for t in range(TILES)]
        kT = [sb(f"kT{t}", [P, 16 * SEQ]) for t in range(TILES)]
        E = [sb(f"E{t}", [P, NH * SEQ]) for t in range(TILES)]
        pT = [kT[t][:, :].rearrange("p (a q) -> p a q", a=PAIRS) for t in range(TILES)]
        vb = [sb(f"vb{t}", [P, 2, PAIRS, 2, HD + 1]) for t in range(TILES)]
        mx = sb("mx", [P, TILES, NH])
        rec = sb("rec", [P, TILES, NH])
        att = [sb(f"att{t}", [P, H]) for t in range(TILES)]
        attT = [sb(f"attT{t}", [P, HC, P]) for t in range(TILES)]
        h1 = [sb(f"h1_{t}", [P, H]) for t in range(TILES)]
        mi = att
        h1T = attT

        h2 = [sb(f"h2_{t}", [P, H]) for t in range(TILES)]
        ms = [[sb(f"ms_{e}{s}", [P, HC, GT], F32R) for s in ("hi", "lo")] for e in "vl"]
        th = [sb(f"th{k}", [P, GT]) for k in range(2)]
        with nc.sbuf_tensor("raw", [P, 4, 3 * H], F32) as raw:
            pass
        hid = [sb(f"hid_{s}", [P, NJ, GT], F32R) for s in ("hi", "lo")]
        h3 = [sb(f"h3_{t}", [P, H]) for t in range(TILES)]
        h3T = [sb(f"h3T{t}", [P, HC, P]) for t in range(TILES)]
        ctxT_b = sb("ctxT_b", [P, GT])
        mp = [sb(f"mp{t}", [P, 2 * H]) for t in range(TILES)]
        mw = [sb(f"mw{t}", [P, P]) for t in range(TILES)]
        mwT = [sb(f"mwT{t}", [P, P]) for t in range(TILES)]
        mm = sb("mm", [P, TILES, 4])
        mc = [sb(f"mc{t}", [P, 2 * H]) for t in range(TILES)]
        z = [sb(f"z{t}", [P, H]) for t in range(TILES)]

        pos_i = h3[0][0:SEQ, 0:P].bitcast(I32)
        half_tok = N_TOK // 2
        types_raw = [kT[k][:, :] for k in range(2)]
        pos_f = mp[0][0:SEQ, 0:3 * P].rearrange("p (a s) -> p a s", a=3)

        xy = [ctx.enter_context(nc.psum_tensor(f"xy{t}", [P, 2, 512], F32)) for t in range(TILES)]
        X = [xy[t][:, 0, :] for t in range(TILES)]
        Y = [xy[t][:, 1, :] for t in range(TILES)]
        Z = [ctx.enter_context(nc.psum_tensor(f"z_ps{t}", [P, 512], F32)) for t in range(TILES)]
        B = [ctx.enter_context(nc.psum_tensor(f"b_ps{t}", [P, 512], F32)) for t in range(TILES)]

        names = """ld_cst ld_pos ld_types ld_ln ld_wa ld_wb ld_x ld_xT ld_ca ld_cb ld_bias ld_norm
            wsplit_hi wsplit_lo cst_ready pos_step hot_ready rope_ps rope_ready zeroed type_step route_ready route_ps route_t_ready small_ready cq_ready
            xh_ready xl_ready xv_hi xv_lo xs_hi xs_lo ssx r1v r1 roper
            qk_ps v_ps rope_a rope_b qkz_ready vb_ready q_ps k_ps qT_ready kc_ready kT_ready s_ps max_ready sub_ready exp_ready
            pT_psx pT_psy pT_readyx pT_ready pv_ps rec_ready att_ready attT_ps attT_ready dense_ps h1a h1_ready ss1 r2v r2
            h1T_ps h1T_ready cq_ps ckv_ps cq_ev ck_ev cvb_ready cQ_ps cK_ps cqT_ready ckc_ready ckT_ready cs_ps cmax csub cexp
            cpT_psx cpT_psy cpT_readyx cpT_ready cpv_ps crec catt_ready cattT_ps cattT_ready cdense_ps h2_ready ss2 r3v r3 mi_ready
            miT_ps mh_ready ml_ready mv_hi mv_lo ms_hi ms_lo gu_ps th_ready gt_ready hid_ready hid_hi hid_lo down_ps h3a h3_ready h3T_ps h3T_ready
            mem_ps mem_ready ms_ps mmax mmaxs mexp mrec mw_ready mwT_ps mwT_ready mc_ps mc_ready gate_ps zb_ready tz_ready gm_ready
            fused_ready ss4 r4v r4 out_ready""".split()
        S = {n: sem(n) for n in names}

        def tl(n, t):
            return 2 * n + t + 1

        def first(n):
            return isinstance(n, int) and n == 0

        stage = [raw[:, k, :] for k in range(4)]
        split = []
        for e, k in enumerate("vl"):
            for c in range(HC):
                split.append((d[f"L0_xattn_{k}_qkv"][c * P:(c + 1) * P, :], (0, c), w_qkv[0][:, e, c, :], w_qkv[1][:, e, c, :], P, 3 * H))
        for g, nm in enumerate(("gate", "up")):
            for e, k in enumerate("vl"):
                for c in range(HC):
                    split.append((d[f"L0_xattn_{k}_{nm}"][c * P:(c + 1) * P, :], (2, c), w_gu[0][:, g, e, c, :], w_gu[1][:, g, e, c, :], P, INTER))
        N_QKV = 2 * HC
        for e, k in enumerate("vl"):
            for j in range(0, NJ, 3):
                if j + 3 < NJ:
                    split.append((d[f"L0_xattn_{k}_down"][j * JW:(j + 3) * JW, :].rearrange("(j p) n -> p j n", p=JW), None,
                                  w_down[0][:, j:j + 3, e, :], w_down[1][:, j:j + 3, e, :], JW, 3 * H))
                else:
                    split.append((d[f"L0_xattn_{k}_down"][j * JW:(j + 2) * JW, :].rearrange("(j p) n -> p j n", p=JW), None,
                                  w_down[0][:, j:j + 2, e, :], w_down[1][:, j:j + 2, e, :], JW, 2 * H))
                    split.append((d[f"L0_xattn_{k}_down"][(j + 2) * JW:INTER, :], None,
                                  w_down[0][0:JWS[-1], j + 2, e, :], w_down[1][0:JWS[-1], j + 2, e, :], JWS[-1], H))
        NSTAGE = len(stage)

        def staged(k):
            _, _, hi, _, rows, cols = split[k]
            raw = stage[k % NSTAGE][0:rows, 0:cols]
            return raw if len(hi.shape) == 2 else raw.rearrange("p (j n) -> p j n", n=H)

        stored = [sem(f"stored{t}") for t in range(TILES)]
        wload = [sem(f"wload{k}") for k in range(NSTAGE)]

        def order(a, b, more):
            def A(*steps):
                return [(name, a, t) for name, t in steps] if a is not None else []

            def B(*steps):
                return [(name, b, t) for name, t in steps] if b is not None else []

            def mlp(*js):
                return B(*[x for j in js for x in (("mlp", j), ("hid", j))])

            def nxt(*steps):
                return [(name, a + 1, t) for name, t in steps] if more else []
            return (A(("qkv", 0)) + B(("miT", 0)) + A(("qkv", 1), ("rope", 0), ("rope", 1)) + B(("mlp", 0), ("hid", 0), ("mlp", 1))
                    + A(("qkT", 0), ("qkT", 1)) + B(("mlp", 2)) + A(("score", 0)) + B(("hid", 1)) + A(("score", 1))
                    + B(("mlp", 3), ("hid", 2)) + A(("probT", 0)) + B(("mlp", 4)) + A(("pv", 0)) + B(("hid", 3), ("hid", 4))
                    + A(("probT", 1)) + B(("mlp", 5)) + A(("ctxT", 0)) + B(("hid", 5)) + A(("pv", 1), ("dense", 0))
                    + nxt(("xsplit", 0)) + A(("ctxT", 1)) + B(("down", 0)) + A(("h1T", 0), ("dense", 1)) + B(("down", 1), ("h3T", 0))
                    + A(("cproj", 0)) + B(("mem", 0)) + A(("h1T", 1), ("cqkT", 0)) + B(("h3T", 1), ("mscore", 0)) + A(("cproj", 1))
                    + B(("mem", 1), ("attnT", 0)) + A(("cqkT", 1)) + B(("mscore", 1)) + A(("cscore", 0)) + B(("mc", 0))
                    + A(("cscore", 1)) + B(("attnT", 1)) + A(("cprobT", 0)) + B(("gate", 0), ("mc", 1))
                    + A(("cprobT", 1), ("cpv", 0), ("cpv", 1), ("cctxT", 0), ("cctxT", 1), ("cdense", 0), ("cdense", 1))
                    + B(("gate", 1)) + nxt(("xsq", 0), ("xsq", 1)))

        def run(eng, steps):
            def step(name, n, t):
                if name in steps:
                    steps[name](n, t)

            def one(a, b, more=True):
                for name, n, t in order(a, b, more):
                    step(name, n, t)
            for name, t in [("xsplit", 0)] + [("wsplit", k) for k in range(N_QKV)] + [("xsq", 0), ("xsq", 1)]:
                step(name, 0, t)
            for k, (name, n, t) in enumerate(order(0, None, True)):
                step(name, n, t)
                if N_QKV + k < len(split):
                    step("wsplit", 0, N_QKV + k)
            one(1, 0)
            with eng.Fori(2, GROUPS - 1) as n:
                one(n, n - 1)
            one(GROUPS - 1, GROUPS - 2, more=False)
            one(None, GROUPS - 1, more=False)

        block = ctx.enter_context(nc.Block())

        @block.sync
        def _(sp):
            def load_xT(n):
                if not first(n):
                    sp.wait_ge(S["xl_ready"], n)
                sp.dma_start(xT[:, :, :], d["xT"][:, bass.ds(n * GT, GT)].rearrange("(c p) n -> p c n", p=P)).then_inc(S["ld_xT"], 16)

            def load_x(n):
                if not first(n):
                    sp.wait_ge(S["h1_ready"], tl(n, 1) - 2)
                sp.dma_start(x_sb[:, :, :], d["x"][bass.ds(n * GT, GT), :].rearrange("(t p) h -> p t h", p=P)).then_inc(S["ld_x"], 16)

            def load_ctx_a(n):
                if not first(n):
                    sp.wait_ge(S["ckv_ps"], tl(n, 1) - 2)
                sp.dma_start(ctxT_a[:, :], d["ctxT"][:, bass.ds(n * GT, GT)]).then_inc(S["ld_ca"], 16)

            def load_ctx_b(n):
                if not first(n):
                    sp.wait_ge(S["mem_ps"], tl(n, 1) - 2)
                sp.dma_start(ctxT_b[:, :], d["ctxT"][:, bass.ds(n * GT, GT)]).then_inc(S["ld_cb"], 16)

            def store(n):
                for t in range(TILES):
                    sp.wait_ge(S["out_ready"], tl(n, t))
                    sp.dma_start(out[bass.ds(n * GT + t * P, P), :], z[t][:, :]).then_inc(stored[t], 16)

            def load_raw(k):
                src, _, _, _, rows, cols = split[k]
                if k >= NSTAGE:
                    sp.wait_ge(S["wsplit_lo"], k - NSTAGE + 1)
                sp.dma_start(staged(k), src).then_inc(wload[k % NSTAGE], 16)

            sp.dma_start(ln[:, :, :].rearrange("p i c -> p (i c)"), d["ln"]).then_inc(S["ld_ln"], 16)
            load_raw(0)
            load_xT(0)
            sp.dma_start(cst[:, :], d["consts"]).then_inc(S["ld_cst"], 16)
            for k in range(1, N_QKV):
                load_raw(k)
            load_x(0)
            for k in range(N_QKV, 2 * N_QKV):
                load_raw(k)
            for c in range(HC):
                sp.dma_start(w_cq[:, c, :], d["L0_xattn_cq_w"][c * P:(c + 1) * P, :]).then_inc(S["ld_wa"], 16)
                for e, k in enumerate("vl"):
                    sp.dma_start(w_dense[:, c, e, :], d[f"L0_xattn_{k}_dense"][c * P:(c + 1) * P, :]).then_inc(S["ld_wa"], 16)
            sp.dma_start(w_ckv[:, :], d["L0_xattn_ckv_w"]).then_inc(S["ld_wa"], 16)
            sp.dma_start(w_cdense[:, :], d["L0_xattn_cdense_w"]).then_inc(S["ld_wa"], 16)
            load_ctx_a(0)
            for k in range(2 * N_QKV, len(split)):
                load_raw(k)
            sp.dma_start(w_mem[:, :], d["W_memT"]).then_inc(S["ld_wb"], 16)
            sp.dma_start(w_gate[:, :, :], d["W_gateT"].rearrange("(c p) n -> p c n", p=P)).then_inc(S["ld_wb"], 16)
            load_xT(1)
            load_x(1)
            load_ctx_a(1)
            load_ctx_b(0)
            with sp.Fori(2, GROUPS) as n:
                load_xT(n)
                load_x(n)
                load_ctx_a(n)
                load_ctx_b(n - 1)
                store(n - 2)
            load_ctx_b(GROUPS - 1)
            store(GROUPS - 2)
            store(GROUPS - 1)
            for t in range(TILES):
                sp.wait_ge(stored[t], 16 * GROUPS)

        @block.scalar
        def _(act):
            def wsplit(n, k):
                _, norm, hi, _, _, _ = split[k]
                if k == 0:
                    act.wait_ge(S["ld_ln"], 16)
                act.wait_ge(wload[k % NSTAGE], 16 * (k // NSTAGE + 1))
                act.activation(hi, staged(k), ACT.Copy, scale=ln[:, norm[0], norm[1]:norm[1] + 1] if norm else 1.0).then_inc(S["wsplit_hi"], 1)

            def square_sum(src, scratch, k, t, done):
                act.activation(scratch, src, ACT.Square, scale=H ** -0.5, accum_out=ss[:, k, t:t + 1]).then_inc(done, 1)

            def xsplit(n, t):
                act.wait_ge(S["ld_xT"], 16 * n + 16)
                if not first(n):
                    act.wait_ge(S["v_ps"], 2 * n)
                act.activation(xs[1][0][:, :, :], xT[:, :, :], ACT.Copy).then_inc(S["xh_ready"], 1)

            def xsq(n, t):
                act.wait_ge(S["ld_x"], 16 * n + 16)
                if not first(n):
                    act.wait_ge(S["h2_ready"], tl(n, t) - 2)
                square_sum(x_sb[:, t, :], h1[t][:, :], 0, t, S["ssx"])

            def rope_v(n, t):
                act.wait_ge(S["v_ps"], tl(n, t))
                act.wait_ge(S["r1"], tl(n, t))
                v = Y[t][:, 0:H].rearrange("p (a e k) -> p a e k", e=2, k=HD)
                for b in range(2):
                    rows = slice(b * SEQ, (b + 1) * SEQ)
                    for e in range(2):
                        act.activation(vb[t][e * SEQ:(e + 1) * SEQ, b, :, e, 0:HD], v[rows, :, e, :], ACT.Copy,
                                       scale=rstd[rows, 0, t:t + 1]).then_inc(S["vb_ready"], 1)

            def qkT(n, t):
                act.wait_ge(S["q_ps"], tl(n, t))
                act.activation(qT[t][:, :, :], Z[t][:, :].rearrange("p (g q) -> p g q", g=4), ACT.Copy).then_inc(S["qT_ready"], 1)

            def score(n, t):
                act.wait_ge(S["sub_ready"], tl(n, t))
                act.activation(E[t][:, :], E[t][:, :], ACT.Exp, scale=HD ** -0.5).then_inc(S["exp_ready"], 1)

            def probT(n, t):
                act.wait_ge(S["pT_psx"], tl(n, t))
                act.activation(pT[t][:, 0:4, :], X[t].rearrange("p (a q) -> p a q", a=4), ACT.Copy).then_inc(S["pT_readyx"], 1)

            def ctxT(n, t):
                act.wait_ge(S["attT_ps"], tl(n, t))
                act.activation(attT[t][:, :, :], Y[t][:, 0:H].rearrange("p (c q) -> p c q", c=HC), ACT.Copy).then_inc(S["attT_ready"], 1)

            def dense(n, t):
                act.wait_ge(S["h1_ready"], tl(n, t))
                square_sum(h1[t][:, :], att[t][:, :], 1, t, S["ss1"])

            def h1T_(n, t):
                act.wait_ge(S["h1T_ps"], tl(n, t))
                act.activation(h1T[t][:, :, :], Z[t][:, 0:H].rearrange("p (c q) -> p c q", c=HC), ACT.Copy).then_inc(S["h1T_ready"], 1)

            def cproj(n, t):
                act.wait_ge(S["ckv_ps"], tl(n, t))
                for b in range(2):
                    rows = slice(b * SEQ, (b + 1) * SEQ)
                    act.activation(qkz[t][rows, 2:4, b * SEQ:(b + 1) * SEQ],
                                   X[t][rows, 0:CC].rearrange("p (g c) -> p g c", g=2), ACT.Copy).then_inc(S["ck_ev"], 1)
                v = X[t][:, CC:2 * CC].rearrange("p (a e k) -> p a e k", e=2, k=CHD)
                for b in range(2):
                    rows = slice(b * SEQ, (b + 1) * SEQ)
                    for e in range(2):
                        act.activation(vb[t][e * SEQ:(e + 1) * SEQ, b, :, e, HD - CHD:HD], v[rows, :, e, :], ACT.Copy).then_inc(S["cvb_ready"], 1)

            def cqkT(n, t):
                act.wait_ge(S["cQ_ps"], tl(n, t))
                act.activation(qT[t][:, 0:2, :], Z[t][:, 0:2 * P].rearrange("p (g q) -> p g q", g=2), ACT.Copy).then_inc(S["cqT_ready"], 1)

            def cscore(n, t):
                act.wait_ge(S["csub"], tl(n, t))
                act.activation(E[t][:, :], E[t][:, :], ACT.Exp, scale=CHD ** -0.5).then_inc(S["cexp"], 1)

            def cprobT(n, t):
                act.wait_ge(S["cpT_psx"], tl(n, t))
                act.activation(pT[t][:, 0:4, :], X[t].rearrange("p (a q) -> p a q", a=4), ACT.Copy).then_inc(S["cpT_readyx"], 1)

            def cctxT(n, t):
                act.wait_ge(S["cattT_ps"], tl(n, t))
                act.activation(attT[t][:, 0, :], Y[t][:, 0:CC], ACT.Copy).then_inc(S["cattT_ready"], 1)

            def cdense(n, t):
                act.wait_ge(S["h2_ready"], tl(n, t))
                square_sum(h2[t][:, :], att[t][:, :], 2, t, S["ss2"])

            def miT(n, t):
                act.wait_ge(S["miT_ps"], n + 1)
                if not first(n):
                    act.wait_ge(S["gu_ps"], NJ * n)
                act.activation(ms[1][0][:, :, :], B[0][:, :].rearrange("p (c q) -> p c q", c=HC), ACT.Copy).then_inc(S["mh_ready"], 1)

            def mlp(n, j):
                act.wait_ge(S["gu_ps"], NJ * n + j + 1)
                if j >= 2:
                    act.wait_ge(S["hid_lo"], NJ * n + j - 1)
                elif not first(n):
                    act.wait_ge(S["hid_lo"], NJ * n)
                act.activation(th[j % 2][0:JWS[j], :], B[(j + 1) % 2][0:JWS[j], 0:GT], ACT.Tanh, scale=0.5).then_inc(S["th_ready"], 1)

            def hid_hi(n, j):
                act.wait_ge(S["hid_ready"], NJ * n + j + 1)
                if not first(n):
                    act.wait_ge(S["down_ps"], 2 * n)
                act.activation(hid[0][0:JWS[j], j, :], th[j % 2][0:JWS[j], :], ACT.Copy).then_inc(S["hid_hi"], 1)

            def h3T_(n, t):
                act.wait_ge(S["h3T_ps"], tl(n, t))
                act.activation(h3T[t][:, :, :], B[t][:, 0:H].rearrange("p (c q) -> p c q", c=HC), ACT.Copy).then_inc(S["h3T_ready"], 1)

            def mem(n, t):
                act.wait_ge(S["mem_ps"], tl(n, t))
                act.activation(mp[t][:, :], B[t][:, :], ACT.Copy).then_inc(S["mem_ready"], 1)

            def mscore(n, t):
                act.wait_ge(S["mmaxs"], tl(n, t))
                act.activation(mw[t][:, :], B[t][:, 0:P], ACT.Exp, scale=H ** -0.5, bias=mm[:, t, 1:2],
                               accum_out=mm[:, t, 2:3]).then_inc(S["mexp"], 1)

            def attnT(n, t):
                act.wait_ge(S["mwT_ps"], tl(n, t))
                act.activation(mwT[t][:, :], B[t][:, P:2 * P], ACT.Copy).then_inc(S["mwT_ready"], 1)

            def mc_(n, t):
                act.wait_ge(S["mc_ps"], tl(n, t))
                act.activation(mc[t][:, :], B[t][:, :], ACT.Copy).then_inc(S["mc_ready"], 1)

            def gate(n, t):
                act.wait_ge(S["zb_ready"], tl(n, t))
                act.activation(z[t][:, :], z[t][:, :], ACT.Tanh, scale=0.5).then_inc(S["tz_ready"], 1)
                act.wait_ge(S["fused_ready"], tl(n, t))
                square_sum(h3[t][:, :], z[t][:, :], 3, t, S["ss4"])

            run(act, dict(wsplit=wsplit, xsplit=xsplit, rope=rope_v, qkT=qkT, score=score, probT=probT, ctxT=ctxT, dense=dense, h1T=h1T_,
                          cproj=cproj, cqkT=cqkT, cscore=cscore, cprobT=cprobT, cctxT=cctxT, cdense=cdense, miT=miT, mlp=mlp,
                          hid=hid_hi, h3T=h3T_, mem=mem, mscore=mscore, attnT=attnT, mc=mc_, gate=gate, xsq=xsq))

        @block.vector
        def _(dve):
            dve.wait_ge(S["ld_cst"], 16)
            dve.tensor_copy(ident_h[:, :], ident).then_inc(S["cst_ready"], 1)
            dve.tensor_copy(causal_h[:, :, :], cst[:, C_CAUS:C_CAUS + SEQ].unsqueeze(1).to_broadcast([P, 8, SEQ])).then_inc(S["cst_ready"], 1)
            dve.tensor_copy(block_h[:, :], cst[:, C_BLK:C_BLK + P]).then_inc(S["cst_ready"], 1)
            dve.wait_ge(S["ld_types"], 32)
            for k in range(2):
                dve.tensor_scalar(types_raw[k], types_raw[k].bitcast(I32), 1.0, None, ALU.is_equal).then_inc(S["type_step"], 1)
                dve.wait_ge(S["type_step"], k + 1)
                hot = types_raw[k].rearrange("p (b s) -> p b s", s=SEQ)
                dve.tensor_tensor(route[:, k * half_tok:(k + 1) * half_tok].rearrange("p (b s) -> p b s", s=SEQ)[:, :, 0:SEQ - 1],
                                  hot[:, :, 0:SEQ - 1], hot[:, :, 1:SEQ], ALU.mult).then_inc(S["route_ready"], 1)
            dve.wait_ge(S["ld_pos"], 32)
            dve.tensor_copy(pos_f[:, 0, :], pos_i).then_inc(S["pos_step"], 1)
            dve.wait_ge(S["pos_step"], 1)
            dve.tensor_scalar(pos_f[:, 1, :], pos_f[:, 0, :], 0.0, float(SEQ), ALU.is_lt, ALU.mult).then_inc(S["pos_step"], 1)
            dve.wait_ge(S["pos_step"], 2)
            dve.tensor_tensor(pos_f[:, 2, :], pos_f[:, 0, :], pos_f[:, 1, :], ALU.add).then_inc(S["pos_step"], 1)
            dve.wait_ge(S["pos_step"], 3)
            dve.tensor_scalar(pos_f[:, 0, :], pos_f[:, 2, :], 0.0, float(SEQ - 1), ALU.max, ALU.min).then_inc(S["pos_step"], 1)
            dve.wait_ge(S["pos_step"], 4)
            dve.tensor_scalar(pos_f[:, 1, :], pos_f[:, 0, :], cst[0:SEQ, C_IOTA:C_IOTA + 1], None, ALU.is_equal).then_inc(S["hot_ready"], 1)

            def wsplit(n, k):
                _, norm, hi, lo, _, _ = split[k]
                dve.wait_ge(S["wsplit_hi"], k + 1)
                if norm:
                    dve.scalar_tensor_tensor(out=lo, in0=staged(k), scalar=ln[:, norm[0], norm[1]:norm[1] + 1], in1=hi.bitcast(F32),
                                             op0=ALU.mult, op1=ALU.subtract).then_inc(S["wsplit_lo"], 1)
                else:
                    dve.tensor_tensor(lo, staged(k), hi.bitcast(F32), ALU.subtract).then_inc(S["wsplit_lo"], 1)
                if k == N_QKV - 1:
                    dve.wait_ge(S["rope_ps"], 1)
                    dve.tensor_copy(rope[:, :], Z[0][:, 0:2 * HD]).then_inc(S["rope_ready"], 1)
                    dve.wait_ge(S["rope_ready"], 1)
                    dve.wait_ge(S["route_ps"], 1)
                    dve.tensor_copy(route_t[:, 0, :], Z[1][:, 0:TILES * GROUPS]).then_inc(S["route_t_ready"], 1)
                    dve.tensor_scalar(route_t[:, 1, :], Z[1][:, 0:TILES * GROUPS], -1.0, 1.0, ALU.mult, ALU.add).then_inc(S["route_t_ready"], 1)
                if k == len(split) // 2:
                    dve.wait_ge(S["ld_wa"], 16 * 8)
                    for c in range(HC):
                        dve.tensor_scalar(w_cq[:, c, :], w_cq[:, c, :], ln[:, 1, c:c + 1], None, ALU.mult).then_inc(S["cq_ready"], 1)

            def route_hi(n, s, v_ready, ready):
                m = route[:, bass.ds(n * GT, GT)].unsqueeze(1).to_broadcast([P, HC, GT])
                dve.tensor_tensor(s[0][0][:, :, :], s[1][0][:, :, :].bitcast(F32), m, ALU.mult).then_inc(v_ready, 1)
                dve.wait_ge(v_ready, n + 1)
                dve.tensor_tensor(s[1][0][:, :, :], s[1][0][:, :, :].bitcast(F32), s[0][0][:, :, :].bitcast(F32),
                                  ALU.subtract).then_inc(ready, 1)

            def xsplit(n, t):
                if first(n):
                    dve.wait_ge(S["route_ready"], 3)
                dve.wait_ge(S["xh_ready"], n + 1)
                dve.tensor_tensor(xs[1][1][:, :, :], xT[:, :, :], xs[1][0][:, :, :].bitcast(F32), ALU.subtract).then_inc(S["xl_ready"], 1)
                dve.wait_ge(S["xl_ready"], n + 1)
                route_hi(n, xs, S["xv_hi"], S["xs_hi"])

            def xsq(n, t):
                dve.wait_ge(S["r1"], tl(n, t))
                dve.tensor_scalar(rope_r[:, t, :], rope[:, :], rstd[:, 0, t:t + 1], None, ALU.mult).then_inc(S["roper"], 1)

            def rope_q(n, t):
                dve.wait_ge(S["qk_ps"], tl(n, t))
                dve.wait_ge(S["roper"], tl(n, t))
                if not first(n):
                    dve.wait_ge(S["cpT_psy"], tl(n, t) - 2)
                qk = X[t].rearrange("p (h d) -> p h d", d=HD)
                straight = E[t][:, 0:2 * H].rearrange("p (h d) -> p h d", d=HD)
                turned = E[t][:, 2 * H:4 * H].rearrange("p (h d) -> p h d", d=HD)
                hd2 = HD // 2

                def table(a, b):
                    return rope_r[:, t, a:b].unsqueeze(1).to_broadcast([P, 2 * NH, b - a])
                dve.tensor_tensor(straight, qk, table(0, HD), ALU.mult).then_inc(S["rope_a"], 1)
                dve.tensor_tensor(turned[:, :, 0:hd2], qk[:, :, hd2:HD], table(HD, HD + hd2), ALU.mult).then_inc(S["rope_b"], 1)
                dve.tensor_tensor(turned[:, :, hd2:HD], qk[:, :, 0:hd2], table(HD + hd2, 2 * HD), ALU.mult).then_inc(S["rope_b"], 1)

            def compact(t, groups, done):
                dve.tensor_reduce(kc[t][:, 0:groups * SEQ].rearrange("p (g k) -> p g k", g=groups),
                                  Y[t][:, 0:groups * P].rearrange("p (g b k) -> p g k b", g=groups, b=2), AX.X, ALU.add).then_inc(done, 1)

            def qkT(n, t):
                dve.wait_ge(S["k_ps"], tl(n, t))
                compact(t, 4, S["kc_ready"])

            def max_sub(t, n, s_ps, max_ready, sub_ready):
                s = xy[t][:, :, :].rearrange("p b (h k) -> p (b h) k", k=SEQ)
                dve.wait_ge(s_ps, tl(n, t))
                dve.tensor_reduce(mx[:, t, :], s, AX.X, ALU.max).then_inc(max_ready, 1)
                dve.wait_ge(max_ready, tl(n, t))
                dve.tensor_tensor(E[t][:, :].rearrange("p (h k) -> p h k", k=SEQ), s,
                                  mx[:, t, :].unsqueeze(2).to_broadcast([P, NH, SEQ]), ALU.subtract).then_inc(sub_ready, 1)

            def score(n, t):
                max_sub(t, n, S["s_ps"], S["max_ready"], S["sub_ready"])

            def probT(n, t):
                dve.wait_ge(S["pT_psy"], tl(n, t))
                dve.tensor_copy(pT[t][:, 4:8, :], Y[t].rearrange("p (a q) -> p a q", a=4)).then_inc(S["pT_ready"], 1)

            def normed(t, n, hd, pv_ps, rec_ready, done):
                o = Z[t][:, 0:NH * (hd + 1)].rearrange("p (h d) -> p h d", d=hd + 1)
                if hd == HD and not first(n):
                    dve.wait_ge(S["miT_ps"], n)
                dve.wait_ge(pv_ps, tl(n, t))
                dve.reciprocal(rec[:, t, :], o[:, :, hd]).then_inc(rec_ready, 1)
                dve.wait_ge(rec_ready, tl(n, t))
                dve.tensor_tensor(att[t][:, 0:NH * hd].rearrange("p (h d) -> p h d", d=hd), o[:, :, 0:hd],
                                  rec[:, t, :].unsqueeze(2).to_broadcast([P, NH, hd]), ALU.mult).then_inc(done, 1)

            def pv(n, t):
                normed(t, n, HD, S["pv_ps"], S["rec_ready"], S["att_ready"])

            def routed_add(out_, ps, rest, n, t, mid, done):
                dve.scalar_tensor_tensor(out=out_, in0=ps[:, 0:H], scalar=route_t[:, 0, bass.ds(2 * n + t, 1)], in1=rest,
                                         op0=ALU.mult, op1=ALU.add).then_inc(mid, 1)
                dve.wait_ge(mid, tl(n, t))
                dve.scalar_tensor_tensor(out=out_, in0=ps[:, H:2 * H], scalar=route_t[:, 1, bass.ds(2 * n + t, 1)], in1=out_,
                                         op0=ALU.mult, op1=ALU.add).then_inc(done, 1)

            def dense(n, t):
                dve.wait_ge(S["dense_ps"], tl(n, t))
                if not first(n):
                    dve.wait_ge(S["h2_ready"], tl(n, t) - 2)
                routed_add(h1[t][:, :], X[t], x_sb[:, t, :], n, t, S["h1a"], S["h1_ready"])

            def cproj(n, t):
                dve.wait_ge(S["cq_ps"], tl(n, t))
                dve.wait_ge(S["r2"], tl(n, t))
                for b in range(2):
                    rows = slice(b * SEQ, (b + 1) * SEQ)
                    dve.tensor_scalar(qkz[t][rows, 0:2, b * SEQ:(b + 1) * SEQ],
                                      Y[t][rows, 0:CC].rearrange("p (g c) -> p g c", g=2),
                                      rstd[rows, 1, t:t + 1], None, ALU.mult).then_inc(S["cq_ev"], 1)

            def cqkT(n, t):
                dve.wait_ge(S["cK_ps"], tl(n, t))
                compact(t, 2, S["ckc_ready"])

            def cscore(n, t):
                max_sub(t, n, S["cs_ps"], S["cmax"], S["csub"])

            def cprobT(n, t):
                dve.wait_ge(S["cpT_psy"], tl(n, t))
                dve.tensor_copy(pT[t][:, 4:8, :], Y[t].rearrange("p (a q) -> p a q", a=4)).then_inc(S["cpT_ready"], 1)

            def cpv(n, t):
                normed(t, n, CHD, S["cpv_ps"], S["crec"], S["catt_ready"])

            def cdense(n, t):
                dve.wait_ge(S["cdense_ps"], tl(n, t))
                if not first(n):
                    dve.wait_ge(S["h3_ready"], tl(n, t) - 2)
                dve.tensor_tensor(h2[t][:, :], X[t][:, 0:H], h1[t][:, :], ALU.add).then_inc(S["h2_ready"], 1)

            def miT(n, t):
                dve.wait_ge(S["mh_ready"], n + 1)
                dve.tensor_tensor(ms[1][1][:, :, :], B[0][:, :].rearrange("p (c q) -> p c q", c=HC),
                                  ms[1][0][:, :, :].bitcast(F32), ALU.subtract).then_inc(S["ml_ready"], 1)
                dve.wait_ge(S["ml_ready"], n + 1)
                route_hi(n, ms, S["mv_hi"], S["ms_hi"])

            def mlp(n, j):
                w, g, u = JWS[j], B[(j + 1) % 2][0:JWS[j], 0:GT], B[(j + 1) % 2][0:JWS[j], GT:2 * GT]
                dve.wait_ge(S["th_ready"], NJ * n + j + 1)
                dve.scalar_tensor_tensor(out=th[j % 2][0:w, :], in0=th[j % 2][0:w, :], scalar=1.0, in1=g,
                                         op0=ALU.add, op1=ALU.mult).then_inc(S["gt_ready"], 1)
                dve.wait_ge(S["gt_ready"], NJ * n + j + 1)
                dve.scalar_tensor_tensor(out=th[j % 2][0:w, :], in0=th[j % 2][0:w, :], scalar=0.5, in1=u,
                                         op0=ALU.mult, op1=ALU.mult).then_inc(S["hid_ready"], 1)

            def down(n, t):
                dve.wait_ge(S["down_ps"], tl(n, t))
                if not first(n):
                    dve.wait_ge(S["out_ready"], tl(n, t) - 2)
                routed_add(h3[t][:, :], B[t], h2[t][:, :], n, t, S["h3a"], S["h3_ready"])

            def mscore(n, t):
                dve.wait_ge(S["ms_ps"], tl(n, t))
                dve.tensor_reduce(mm[:, t, 0:1], B[t][:, 0:P], AX.X, ALU.max, negate=True).then_inc(S["mmax"], 1)
                dve.wait_ge(S["mmax"], tl(n, t))
                dve.tensor_scalar(mm[:, t, 1:2], mm[:, t, 0:1], H ** -0.5, None, ALU.mult).then_inc(S["mmaxs"], 1)
                dve.wait_ge(S["mexp"], tl(n, t))
                dve.reciprocal(mm[:, t, 3:4], mm[:, t, 2:3]).then_inc(S["mrec"], 1)
                dve.wait_ge(S["mrec"], tl(n, t))
                dve.tensor_scalar(mw[t][:, :], mw[t][:, :], mm[:, t, 3:4], None, ALU.mult).then_inc(S["mw_ready"], 1)

            def gate(n, t):
                dve.wait_ge(S["gate_ps"], tl(n, t))
                if first(n) and t == 0:
                    dve.wait_ge(S["ld_bias"], 16)
                    dve.wait_ge(S["ld_norm"], 16)
                if not first(n):
                    dve.wait_ge(stored[t], 16 * n)
                dve.tensor_tensor(z[t][:, :], B[t][:, 0:H], b_gate[:, :], ALU.add).then_inc(S["zb_ready"], 1)
                dve.wait_ge(S["tz_ready"], tl(n, t))
                dve.scalar_tensor_tensor(out=z[t][:, :], in0=z[t][:, :], scalar=1.0, in1=mc[t][:, 0:H],
                                         op0=ALU.add, op1=ALU.mult).then_inc(S["gm_ready"], 1)
                dve.wait_ge(S["gm_ready"], tl(n, t))
                dve.scalar_tensor_tensor(out=h3[t][:, :], in0=z[t][:, :], scalar=0.5, in1=h3[t][:, :],
                                         op0=ALU.mult, op1=ALU.add).then_inc(S["fused_ready"], 1)
                dve.wait_ge(S["r4"], tl(n, t))
                dve.scalar_tensor_tensor(out=z[t][:, :], in0=h3[t][:, :], scalar=rstd[:, 3, t:t + 1], in1=w_norm[:, :],
                                         op0=ALU.mult, op1=ALU.mult).then_inc(S["out_ready"], 1)

            run(dve, dict(wsplit=wsplit, xsplit=xsplit, rope=rope_q, qkT=qkT, score=score, probT=probT, pv=pv, dense=dense, cproj=cproj,
                          cqkT=cqkT, cscore=cscore, cprobT=cprobT, cpv=cpv, cdense=cdense, miT=miT, mlp=mlp, down=down,
                          mscore=mscore, gate=gate, xsq=xsq))

        @block.gpsimd
        def _(pool):
            for k in range(2):
                pool.dma_start(types_raw[k].bitcast(I32), d["types"][0, k * half_tok:(k + 1) * half_tok].partition_broadcast(P)).then_inc(S["ld_types"], 16)
            for k in range(2):
                pool.dma_start(pos_i[:, k * SEQ:(k + 1) * SEQ], d["pos"][0, :].partition_broadcast(SEQ)).then_inc(S["ld_pos"], 16)
            pool.memset(pow_eps[:, 0:1], -0.5).then_inc(S["small_ready"], 1)
            pool.memset(pow_eps[:, 1:2], EPS).then_inc(S["small_ready"], 1)
            pool.memset(ones[:, :], 1.0).then_inc(S["small_ready"], 1)
            pool.memset(route[:, SEQ - 1:N_TOK:SEQ], 0.0).then_inc(S["route_ready"], 1)
            pool.dma_start(b_gate[:, :], d["b_gate"].partition_broadcast(P)).then_inc(S["ld_bias"], 16)
            pool.dma_start(w_norm[:, :], d["w_norm"].partition_broadcast(P)).then_inc(S["ld_norm"], 16)
            pool.wait_ge(S["small_ready"], 3)
            for t in range(TILES):
                pool.memset(qkz[t][:, :, :], 0.0).then_inc(S["zeroed"], 1)
                pool.memset(vb[t][:, :, :, :, :], 0.0).then_inc(S["zeroed"], 1)
            pool.wait_ge(S["zeroed"], 2 * TILES)
            for t in range(TILES):
                for e in range(2):
                    rows = slice(e * SEQ, (e + 1) * SEQ)
                    pool.memset(vb[t][rows, :, :, e, HD:HD + 1], 1.0).then_inc(S["zeroed"], 1)
                    pool.wait_ge(S["zeroed"], 2 * TILES + 2 * t + e + 1)

            def inv_rms(k, t, n, sums, mid, done):
                pool.wait_ge(sums, tl(n, t))
                pool.tensor_tensor(var[:, k, t:t + 1], ss[:, k, t:t + 1], pow_eps[:, 1:2], ALU.add).then_inc(mid, 1)
                pool.wait_ge(mid, tl(n, t))
                pool.tensor_tensor(rstd[:, k, t:t + 1], var[:, k, t:t + 1], pow_eps[:, 0:1], ALU.pow).then_inc(done, 1)

            def route_lo(n, s, lo_ready, v_ready, ready):
                m = route[:, bass.ds(n * GT, GT)].unsqueeze(1).to_broadcast([P, HC, GT])
                pool.wait_ge(S["route_ready"], 3)
                pool.wait_ge(lo_ready, n + 1)
                pool.tensor_tensor(s[0][1][:, :, :], s[1][1][:, :, :].bitcast(F32), m, ALU.mult).then_inc(v_ready, 1)
                pool.wait_ge(v_ready, n + 1)
                pool.tensor_tensor(s[1][1][:, :, :], s[1][1][:, :, :].bitcast(F32), s[0][1][:, :, :].bitcast(F32),
                                   ALU.subtract).then_inc(ready, 1)

            def xsplit(n, t):
                route_lo(n, xs, S["xl_ready"], S["xv_lo"], S["xs_lo"])

            def xsq(n, t):
                if not first(n):
                    pool.wait_ge(S["vb_ready"], 4 * (tl(n, t) - 2))
                inv_rms(0, t, n, S["ssx"], S["r1v"], S["r1"])

            def rope_add(n, t):
                pool.wait_ge(S["rope_a"], tl(n, t))
                pool.wait_ge(S["rope_b"], 4 * n + 2 * t + 2)
                for b in range(2):
                    rows = slice(b * SEQ, (b + 1) * SEQ)
                    pool.tensor_tensor(qkz[t][rows, :, b * SEQ:(b + 1) * SEQ],
                                       E[t][rows, 0:2 * H].rearrange("p (g c) -> p g c", g=8),
                                       E[t][rows, 2 * H:4 * H].rearrange("p (g c) -> p g c", g=8), ALU.add).then_inc(S["qkz_ready"], 1)
                    pool.wait_ge(S["qkz_ready"], 4 * n + 2 * t + b + 1)

            def expand(t, groups, heads, mask, done):
                pool.tensor_tensor(kT[t][:, :].rearrange("p (g h k) -> p g h k", g=groups, h=heads),
                                   kc[t][:, 0:groups * SEQ].rearrange("p (g k) -> p g k", g=groups).unsqueeze(2).to_broadcast([P, groups, heads, SEQ]),
                                   mask.unsqueeze(1).unsqueeze(3).to_broadcast([P, groups, heads, SEQ]), ALU.mult).then_inc(done, 1)

            def qkT(n, t):
                pool.wait_ge(S["kc_ready"], tl(n, t))
                if not first(n):
                    pool.wait_ge(S["cpv_ps"], tl(n, t) - 2)
                expand(t, 4, 4, cst[:, C_H16:C_H16 + 4], S["kT_ready"])

            def cqkT(n, t):
                pool.wait_ge(S["ckc_ready"], tl(n, t))
                expand(t, 2, 8, cst[:, C_H8:C_H8 + 8], S["ckT_ready"])

            def dense(n, t):
                inv_rms(1, t, n, S["ss1"], S["r2v"], S["r2"])

            def cdense(n, t):
                inv_rms(2, t, n, S["ss2"], S["r3v"], S["r3"])
                pool.wait_ge(S["r3"], tl(n, t))
                pool.tensor_tensor(mi[t][:, :], h2[t][:, :], rstd[:, 2, t:t + 1].to_broadcast([P, H]), ALU.mult).then_inc(S["mi_ready"], 1)

            def miT(n, t):
                route_lo(n, ms, S["ml_ready"], S["mv_lo"], S["ms_lo"])

            def hid_lo(n, j):
                pool.wait_ge(S["hid_hi"], NJ * n + j + 1)
                pool.tensor_tensor(hid[1][0:JWS[j], j, :], th[j % 2][0:JWS[j], :], hid[0][0:JWS[j], j, :].bitcast(F32),
                                   ALU.subtract).then_inc(S["hid_lo"], 1)

            def gate(n, t):
                inv_rms(3, t, n, S["ss4"], S["r4v"], S["r4"])

            run(pool, dict(xsplit=xsplit, xsq=xsq, rope=rope_add, qkT=qkT, cqkT=cqkT, dense=dense, cdense=cdense, miT=miT, hid=hid_lo, gate=gate))

        @block.tensor
        def _(pe):
            def split_product(o, stationary, moving, start, stop):
                (sh, sl), (mh, ml) = stationary, moving
                pe.matmul(o, sh, mh, start=start, stop=False)
                pe.matmul(o, sh, ml, start=False, stop=False)
                return pe.matmul(o, sl, mh, start=False, stop=stop)

            pe.wait_ge(S["ld_cst"], 16)
            pe.wait_ge(S["hot_ready"], 1)
            pe.matmul(Z[0][:, 0:2 * HD], pos_f[:, 1, :], cst[0:SEQ, C_ROPE:C_ROPE + 2 * HD], start=True, stop=True).then_inc(S["rope_ps"], 1)
            pe.wait_ge(S["route_ready"], 3)
            pe.wait_ge(S["small_ready"], 3)
            for i in range(TILES * GROUPS):
                last = pe.matmul(Z[1][:, i:i + 1], route[0:1, i * P:(i + 1) * P], ones[:, :], start=True, stop=True)
            last.then_inc(S["route_ps"], 1)

            def qkv(n, t):
                cols = slice(t * P, (t + 1) * P)
                pe.wait_ge(S["xs_hi"], n + 1)
                pe.wait_ge(S["xs_lo"], n + 1)
                if first(n):
                    pe.wait_ge(S["wsplit_lo"], 4)
                    pe.wait_ge(S["zeroed"], 4 * TILES)
                else:
                    pe.wait_ge(S["h2_ready"], tl(n, t) - 2)
                for o, a, b, done in ((X[t], 0, 2 * H, S["qk_ps"]), (Y[t][:, 0:H], 2 * H, 3 * H, S["v_ps"])):
                    for e in range(2):
                        for c in range(HC):
                            last = split_product(o, [xs[e][s][:, c, cols] for s in range(2)], [w_qkv[s][:, e, c, a:b] for s in range(2)],
                                                 start=(e == 0 and c == 0), stop=(e == 1 and c == HC - 1))
                    last.then_inc(done, 1)

            def turn(n, t, groups, q_ps, k_ps):
                for g in range(groups):
                    last = pe.transpose(Z[t][:, g * P:(g + 1) * P], qkz[t][:, g, :], ident)
                last.then_inc(q_ps, 1)
                for g in range(groups):
                    last = pe.transpose(Y[t][:, g * P:(g + 1) * P], qkz[t][:, groups + g, :], ident)
                last.then_inc(k_ps, 1)

            def qkT(n, t):
                pe.wait_ge(S["qkz_ready"], 4 * n + 2 * t + 2)
                pe.wait_ge(S["vb_ready"], 4 * tl(n, t))
                turn(n, t, 4, S["q_ps"], S["k_ps"])

            def score(n, t):
                pe.wait_ge(S["qT_ready"], tl(n, t))
                pe.wait_ge(S["kT_ready"], tl(n, t))
                for b in range(2):
                    pe.matmul(xy[t][:, b, :], ident_h[:, :], causal_h[:, :, :].rearrange("p h k -> p (h k)"), start=True, stop=False)
                    for g in (2 * b, 2 * b + 1):
                        last = pe.matmul(xy[t][:, b, (g % 2) * GT:(g % 2 + 1) * GT], qT[t][:, g, :], kT[t][:, g * GT:(g + 1) * GT],
                                         start=False, stop=(g % 2 == 1))
                last.then_inc(S["s_ps"], 1)

            def turn_probs(t, psx, psy):
                for a in range(PAIRS):
                    last = pe.transpose(xy[t][:, a // 4, (a % 4) * P:(a % 4 + 1) * P], E[t][:, a * P:(a + 1) * P], ident)
                    if a == 3:
                        last.then_inc(psx, 1)
                last.then_inc(psy, 1)

            def probT(n, t):
                pe.wait_ge(S["exp_ready"], tl(n, t))
                turn_probs(t, S["pT_psx"], S["pT_psy"])

            def apply(t, hd, done):
                for b in range(2):
                    for a in range(PAIRS):
                        last = pe.matmul(Z[t][b * SEQ:(b + 1) * SEQ, a * 2 * (hd + 1):(a + 1) * 2 * (hd + 1)],
                                         pT[t][:, a, b * SEQ:(b + 1) * SEQ], vb[t][:, b, a, :, HD - hd:HD + 1],
                                         start=True, stop=True)
                last.then_inc(done, 1)

            def pv(n, t):
                pe.wait_ge(S["pT_readyx"], tl(n, t))
                pe.wait_ge(S["pT_ready"], tl(n, t))
                apply(t, HD, S["pv_ps"])

            def ctxT(n, t):
                pe.wait_ge(S["att_ready"], tl(n, t))
                for c in range(HC):
                    last = pe.transpose(Y[t][:, c * P:(c + 1) * P], att[t][:, c * P:(c + 1) * P], ident)
                last.then_inc(S["attT_ps"], 1)

            def dense(n, t):
                pe.wait_ge(S["attT_ready"], tl(n, t))
                if first(n):
                    pe.wait_ge(S["ld_wa"], 16 * 8)
                for c in range(HC):
                    last = pe.matmul(X[t], attT[t][:, c, :], w_dense[:, c, :, :].rearrange("p e n -> p (e n)"), start=(c == 0), stop=(c == HC - 1))
                last.then_inc(S["dense_ps"], 1)

            def h1T_(n, t):
                pe.wait_ge(S["h1_ready"], tl(n, t))
                for c in range(HC):
                    last = pe.transpose(Z[t][:, c * P:(c + 1) * P], h1[t][:, c * P:(c + 1) * P], ident)
                last.then_inc(S["h1T_ps"], 1)

            def cproj(n, t):
                pe.wait_ge(S["ld_ca"], 16 * n + 16)
                pe.wait_ge(S["h1T_ready"], tl(n, t))
                if first(n):
                    pe.wait_ge(S["cq_ready"], HC)
                pe.matmul(X[t][:, 0:2 * CC], ctxT_a[:, t * P:(t + 1) * P], w_ckv[:, :], start=True, stop=True).then_inc(S["ckv_ps"], 1)
                for c in range(HC):
                    last = pe.matmul(Y[t][:, 0:CC], h1T[t][:, c, :], w_cq[:, c, :], start=(c == 0), stop=(c == HC - 1))
                last.then_inc(S["cq_ps"], 1)

            def cqkT(n, t):
                pe.wait_ge(S["cq_ev"], 2 * tl(n, t))
                pe.wait_ge(S["ck_ev"], 2 * tl(n, t))
                turn(n, t, 2, S["cQ_ps"], S["cK_ps"])

            def cscore(n, t):
                pe.wait_ge(S["cqT_ready"], tl(n, t))
                pe.wait_ge(S["ckT_ready"], tl(n, t))
                pe.wait_ge(S["cvb_ready"], 4 * tl(n, t))
                for g in range(2):
                    last = pe.matmul(xy[t][:, g, :], qT[t][:, g, :], kT[t][:, g * 512:(g + 1) * 512], start=True, stop=True)
                last.then_inc(S["cs_ps"], 1)

            def cprobT(n, t):
                pe.wait_ge(S["cexp"], tl(n, t))
                turn_probs(t, S["cpT_psx"], S["cpT_psy"])

            def cpv(n, t):
                pe.wait_ge(S["cpT_readyx"], tl(n, t))
                pe.wait_ge(S["cpT_ready"], tl(n, t))
                apply(t, CHD, S["cpv_ps"])

            def cctxT(n, t):
                pe.wait_ge(S["catt_ready"], tl(n, t))
                pe.transpose(Y[t][:, 0:CC], att[t][:, 0:CC], ident).then_inc(S["cattT_ps"], 1)

            def cdense(n, t):
                pe.wait_ge(S["cattT_ready"], tl(n, t))
                pe.matmul(X[t][:, 0:H], attT[t][:, 0, :], w_cdense[:, :], start=True, stop=True).then_inc(S["cdense_ps"], 1)

            def miT(n, t):
                if not first(n):
                    pe.wait_ge(S["out_ready"], 2 * n)
                for t in range(TILES):
                    pe.wait_ge(S["mi_ready"], tl(n, t))
                    for c in range(HC):
                        last = pe.transpose(B[0][:, c * GT + t * P:c * GT + (t + 1) * P], mi[t][:, c * P:(c + 1) * P], ident)
                last.then_inc(S["miT_ps"], 1)

            def mlp(n, j):
                w, bank = JWS[j], B[(j + 1) % 2]
                pe.wait_ge(S["ms_hi"], n + 1)
                pe.wait_ge(S["ms_lo"], n + 1)
                if first(n) and j == 0:
                    pe.wait_ge(S["wsplit_lo"], N_QKV + 4 * HC)
                if j >= 2:
                    pe.wait_ge(S["hid_ready"], NJ * n + j - 1)
                for g in range(2):
                    for e in range(2):
                        for c in range(HC):
                            last = split_product(bank[0:w, g * GT:(g + 1) * GT],
                                                 [w_gu[s][:, g, e, c, j * JW:j * JW + w] for s in range(2)],
                                                 [ms[e][s][:, c, :] for s in range(2)],
                                                 start=(e == 0 and c == 0), stop=(e == 1 and c == HC - 1))
                last.then_inc(S["gu_ps"], 1)

            def down(n, t):
                if t == 0:
                    pe.wait_ge(S["hid_lo"], NJ * n + NJ)
                if first(n) and t == 0:
                    pe.wait_ge(S["wsplit_lo"], len(split))
                for j in range(NJ):
                    last = split_product(B[t][:, :], [hid[s][0:JWS[j], j, t * P:(t + 1) * P] for s in range(2)],
                                         [w_down[s][0:JWS[j], j, :, :].rearrange("p e n -> p (e n)") for s in range(2)],
                                         start=(j == 0), stop=(j == NJ - 1))
                last.then_inc(S["down_ps"], 1)

            def h3T_(n, t):
                pe.wait_ge(S["h3_ready"], tl(n, t))
                for c in range(HC):
                    last = pe.transpose(B[t][:, c * P:(c + 1) * P], h3[t][:, c * P:(c + 1) * P], ident)
                last.then_inc(S["h3T_ps"], 1)

            def mem(n, t):
                pe.wait_ge(S["ld_cb"], 16 * n + 16)
                if first(n) and t == 0:
                    pe.wait_ge(S["ld_wb"], 16 * 2)
                pe.wait_ge(S["h3T_ready"], tl(n, t))
                tok = ctxT_b[:, t * P:(t + 1) * P]
                pe.matmul(B[t][:, 0:H], tok, w_mem[:, :], start=True, stop=True)
                for c in range(HC):
                    last = pe.matmul(B[t][:, H + c * P:H + (c + 1) * P], w_mem[:, c * P:(c + 1) * P], tok, start=True, stop=True)
                last.then_inc(S["mem_ps"], 1)

            def mscore(n, t):
                pe.wait_ge(S["mem_ready"], tl(n, t))
                pe.matmul(B[t][:, 0:P], ident_h[:, :], block_h[:, :], start=True, stop=False)
                for c in range(HC):
                    last = pe.matmul(B[t][:, 0:P], h3T[t][:, c, :], mp[t][:, H + c * P:H + (c + 1) * P], start=False, stop=(c == HC - 1))
                last.then_inc(S["ms_ps"], 1)

            def attnT(n, t):
                pe.wait_ge(S["mw_ready"], tl(n, t))
                pe.transpose(B[t][:, P:2 * P], mw[t][:, :], ident).then_inc(S["mwT_ps"], 1)

            def mc_(n, t):
                pe.wait_ge(S["mwT_ready"], tl(n, t))
                pe.matmul(B[t][:, 0:H], mwT[t][:, :], mp[t][:, 0:H], start=True, stop=True)
                for c in range(HC):
                    last = pe.matmul(B[t][:, H + c * P:H + (c + 1) * P], mp[t][:, c * P:(c + 1) * P], mwT[t][:, :], start=True, stop=True)
                last.then_inc(S["mc_ps"], 1)

            def gate(n, t):
                pe.wait_ge(S["mc_ready"], tl(n, t))
                for c in range(2 * HC):
                    lhs = h3T[t][:, c, :] if c < HC else mc[t][:, H + (c - HC) * P:H + (c - HC + 1) * P]
                    last = pe.matmul(B[t][:, 0:H], lhs, w_gate[:, c, :], start=(c == 0), stop=(c == 2 * HC - 1))
                last.then_inc(S["gate_ps"], 1)

            run(pe, dict(qkv=qkv, qkT=qkT, score=score, probT=probT, pv=pv, ctxT=ctxT, dense=dense, h1T=h1T_, cproj=cproj,
                         cqkT=cqkT, cscore=cscore, cprobT=cprobT, cpv=cpv, cctxT=cctxT, cdense=cdense, miT=miT, mlp=mlp,
                         down=down, h3T=h3T_, mem=mem, mscore=mscore, attnT=attnT, mc=mc_, gate=gate))


def kernel(**inputs):
    import concourse.bacc as bacc
    from concourse.bass_utils import run_bass_kernel_spmd

    a = {k: np.asarray(v) for k, v in inputs.items()}
    feeds = {k: a[k] for k in a if k.startswith("L0_xattn_") and not k.startswith("L0_xattn_ln_")}
    norms = [a["L0_xattn_" + k] for k in ("ln_in_w", "ln_post_cross_w", "ln_post_attn_w")]
    feeds.update(
        x=a["x"].reshape(N_TOK, H), xT=a["x"].reshape(N_TOK, H).T, ctxT=a["ctx_1024"].reshape(N_TOK, CC).T,
        types=a["mask_BxS_ik0"].reshape(1, N_TOK), pos=a["pos_1xS"],
        W_memT=a["L1_xattn_W_mem"].T, W_gateT=a["L1_xattn_W_gate"].T, b_gate=a["L1_xattn_b_gate"], w_norm=a["L1_xattn_norm_w"],
        ln=np.stack(norms).reshape(3 * HC, P).T, consts=shape_constants(),
    )
    nc = bacc.Bacc("TRN2", target_bir_lowering=False, num_devices=1)
    arrays, d = {}, {}
    for name, v in feeds.items():
        v = np.ascontiguousarray(v)
        arrays[f"in_{name}_dram"] = v
        d[name] = nc.dram_tensor(f"in_{name}_dram", v.shape, mybir.dt.from_np(v.dtype), kind="ExternalInput").ap()
    out = nc.dram_tensor("out_0_dram", (N_TOK, H), F32, kind="ExternalOutput").ap()
    xattn_kernel(nc, d, out)
    r = run_bass_kernel_spmd(nc, [arrays], core_ids=[0])
    return r.results[0]["out_0_dram"].reshape(BATCH, SEQ, H)
```

```python
from contextlib import ExitStack

import numpy as np

import concourse.bass as bass
from concourse import mybir

F32 = mybir.dt.float32
F32R = mybir.dt.float32r
BF16 = mybir.dt.bfloat16
I32 = mybir.dt.int32
ALU = mybir.AluOpType
ACT = mybir.ActivationFunctionType
AX = mybir.AxisListType

P = 128
BATCH, SEQ, H = 32, 64, 256
NH, HD = 16, 16
CC, CHD = 128, 8
INTER = 688
N_TOK = BATCH * SEQ
TILES = 2
GT = TILES * P
GROUPS = N_TOK // GT
HC = H // P
REST = P // 2
JWS = [min(P, INTER - REST - j0) for j0 in range(0, INTER - REST, P)] + [REST]
NJ = len(JWS)
J0 = np.cumsum([0] + JWS).tolist()
PAIRS = NH // 2
EPS = 1e-6
NEG = -1.0e30
C_ID, C_H16, C_H8, C_CAUS, C_BLK, C_ROPE, C_IOTA, C_NEXT, C_END = np.cumsum(
    [0, P, 4, 8, SEQ, P, 2 * HD, 1, 1]).tolist()


def shape_constants():
    c = np.zeros((P, C_END), np.float32)
    row = np.arange(P)
    c[:, C_ID:C_ID + P] = np.eye(P)
    c[:, C_H16:C_H16 + 4] = (row[:, None] % 64) // HD == np.arange(4)
    c[:, C_H8:C_H8 + 8] = (row[:, None] % 64) // CHD == np.arange(8)
    c[:, C_CAUS:C_CAUS + SEQ] = np.where(np.arange(SEQ) <= row[:, None] % SEQ, 0, NEG)
    c[:, C_BLK:C_BLK + P] = np.where(row[:, None] // SEQ == row // SEQ, 0, NEG)
    inv = (np.float32(1.0) / np.float32(10000.0) ** (np.arange(0, HD, 2, dtype=np.float32) / np.float32(HD)))
    freq = np.outer(np.arange(SEQ, dtype=np.float32), inv.astype(np.float32)).astype(np.float32)
    sin = np.sin(freq)
    c[:SEQ, C_ROPE:C_ROPE + HD] = np.tile(np.cos(freq), (1, 2))
    c[:SEQ, C_ROPE + HD:C_ROPE + 2 * HD] = np.concatenate([-sin, sin], 1)
    c[:, C_IOTA] = row
    c[:, C_NEXT] = row % SEQ < SEQ - 1
    return c


def xattn_kernel(nc, d, out):
    ctx = ExitStack()
    with ctx:
        def sb(name, shape, dt=F32):
            return ctx.enter_context(nc.sbuf_tensor(name, shape, dt))

        def sem(name):
            return ctx.enter_context(nc.semaphore(name))

        w_qkv = [sb(f"w_qkv_{s}", [P, 2, HC, 3 * H], F32R) for s in ("hi", "lo")]
        w_gu = [sb(f"w_gu_{s}", [P, 2, HC, 2 * INTER], F32R) for s in ("hi", "lo")]
        w_down = [sb(f"w_down_{s}", [P, NJ, 2, H], F32R) for s in ("hi", "lo")]
        w_dense = [sb(f"w_dense_{s}", [P, HC, 2, H], F32R) for s in ("hi", "lo")]
        w_cq = sb("w_cq", [P, HC, CC])
        w_ckv = sb("w_ckv", [P, 2 * CC])
        w_cdense = sb("w_cdense", [P, H])
        w_mem = sb("w_mem", [P, HC, CC])
        w_memT = sb("w_memT", [P, 2 * H])
        w_gate = sb("w_gate", [P, HC, H])
        b_gate = sb("b_gate", [P, H])
        w_norm = sb("w_norm", [P, H])
        ln = sb("ln", [P, 3, HC])
        cst = sb("cst", [P, C_END])
        ident = cst[:, C_ID:C_ID + P]
        ident_h = sb("ident_h", [P, P], BF16)
        causal_h = sb("causal_h", [P, 8, SEQ], BF16)
        block_h = sb("block_h", [P, P], BF16)
        rope = sb("rope", [P, 2 * HD])
        route = sb("route", [P, N_TOK], BF16)
        types_t = sb("types_t", [P, 2, TILES * GROUPS], I32)
        hot_t = sb("hot_t", [P, 2, TILES * GROUPS])
        route_t = sb("route_t", [P, 2, TILES * GROUPS])
        pow_eps = sb("pow_eps", [P, 2])

        x_sb = sb("x_sb", [P, TILES, H])
        xT = sb("xT", [P, HC, GT])
        xs = [[sb(f"xs_{e}{s}", [P, HC, GT], F32R) for s in ("hi", "lo")] for e in "vl"]
        ctxT_a = sb("ctxT_a", [P, GT])
        ss = sb("ss", [P, 4, TILES])
        var = sb("var", [P, 4, TILES])
        rstd = sb("rstd", [P, 4, TILES])
        rope_r = sb("rope_r", [P, TILES, 2 * HD])
        qkz = [sb(f"qkz{t}", [P, 8, P]) for t in range(TILES)]
        qT = [sb(f"qT{t}", [P, 4, P]) for t in range(TILES)]
        kT = [sb(f"kT{t}", [P, 16 * SEQ]) for t in range(TILES)]
        E = [sb(f"E{t}", [P, NH * SEQ]) for t in range(TILES)]
        pT = [kT[t][:, :].rearrange("p (a q) -> p a q", a=PAIRS) for t in range(TILES)]
        vb = [sb(f"vb{t}", [P, 2, PAIRS, 2, HD + 1]) for t in range(TILES)]
        mx = sb("mx", [P, TILES, NH])
        rec = sb("rec", [P, TILES, NH])
        att = [sb(f"att{t}", [P, H]) for t in range(TILES)]
        kc = att
        attT = [[sb(f"attT{t}_{s}", [P, HC, P], F32R) for s in ("hi", "lo")] for t in range(TILES)]
        h1 = [sb(f"h1_{t}", [P, H]) for t in range(TILES)]
        mi = att
        h1T = [qT[t][:, 2:4, :] for t in range(TILES)]
        cattT = [qT[t][:, 2, :] for t in range(TILES)]

        h2 = [sb(f"h2_{t}", [P, H]) for t in range(TILES)]
        ms = [[sb(f"ms_{e}{s}", [P, HC, GT], F32R) for s in ("hi", "lo")] for e in "vl"]
        th = [sb(f"th{k}", [P, GT]) for k in range(2)]
        with nc.sbuf_tensor("raw", [P, 4, 3 * H], F32) as raw:
            pass
        hid = [sb(f"hid_{s}", [P, NJ, GT], F32R) for s in ("hi", "lo")]
        h3 = [sb(f"h3_{t}", [P, H]) for t in range(TILES)]
        h3m = [sb(f"h3m{t}", [P, 2 * H]) for t in range(TILES)]
        h3T = [h3m[t][:, 0:H].rearrange("p (c q) -> p c q", c=HC) for t in range(TILES)]
        mp = [h3m[t][:, H:2 * H] for t in range(TILES)]
        ctxT_b = sb("ctxT_b", [P, GT])
        mpg = [sb(f"mpg{t}", [P, H]) for t in range(TILES)]
        mw_all = sb("mw", [P, TILES * P])
        mw = [mw_all[:, t * P:(t + 1) * P] for t in range(TILES)]
        hwT = mw
        up_rest = mw_all[0:REST, :]
        mwT = [sb(f"mwT{t}", [P, P]) for t in range(TILES)]
        mm = sb("mm", [P, TILES, 4])
        z = [sb(f"z{t}", [P, H]) for t in range(TILES)]

        pos_i = h3[0][0:SEQ, 0:P].bitcast(I32)
        type_parts = [(kT[0][:, 0:GT], 0, GT)] + [(buf[:, :], (k + 1) * GT, (k + 2) * GT) for k, buf in enumerate((z[0], z[1], h2[0], h2[1], h3[1]))]
        type_parts.append((h3m[0][:, :], 6 * GT, 8 * GT))
        w_gate2 = h3m[1][:, :].rearrange("p (c n) -> p c n", c=HC)
        pos_f = [h3[0][0:SEQ, P:2 * P], mwT[0][0:SEQ, :], mwT[1][0:SEQ, :]]

        xyz = [ctx.enter_context(nc.psum_tensor(f"xyz{t}", [P, 3, 512], F32)) for t in range(TILES)]
        xy = [xyz[t][:, 0:2, :] for t in range(TILES)]
        yz = [xyz[t][:, 1:3, :].rearrange("p b (a w) -> p (b a) w", w=P) for t in range(TILES)]
        X = [xy[t][:, 0, :] for t in range(TILES)]
        Y = [xy[t][:, 1, :] for t in range(TILES)]
        Z = [xyz[t][:, 2, :] for t in range(TILES)]
        B = [ctx.enter_context(nc.psum_tensor(f"b_ps{t}", [P, 512], F32)) for t in range(TILES)]
        C = [B[1], B[0]]

        names = """ld_cst ld_pos ld_types ld_type0 type0_step last_ready route0_ready ld_ln ld_wa ld_wb ld_x ld_xT ld_ca ld_cb ld_bias ld_norm
            wsplit_hi wsplit_lo cst_ready pos_step hot_ready rope_ps rope_ready zeroed type_step route_ready ld_types_t
            route_t_step route_t_ready small_ready cq_ready
            xh_ready xl_ready xv_hi xv_lo xs_hi xs_lo ssx r1v r1 roper
            qk_ps v_ps rope_a rope_b qkz_a_ready qkz_b_ready vb_ready q_ps k_ps qT_ready kc_ready kTa_ready kT_ready s_ps max_ready sub_ready exp_ready
            pT_psx pT_psy pT_readyx pT_ready pv_ps rec_ready att_ready attT_ps attT_hi attT_lo dense_ps h1a h1_ready ss1 r2v r2
            h1T_ps h1T_ready cq_ps ckv_ps cq_ev ck_ev cvb_ready cQ_ps cK_ps cqT_ready ckc_ready ckTa_ready ckT_ready cs_ps cmax csub cexp
            cpT_psx cpT_psy cpT_readyx cpT_ready cpv_ps crec catt_ready cattT_ps cattT_ready cdense_ps h2_ready ss2 r3v r3 mi_ready
            miT_ps mh_ready ml_ready mv_hi mv_lo ms_hi ms_lo gu_ps th_ready up_ready gt_ready hid_ready hid_hi hid_lo down_ps h3a h3_ready h3T_ps h3T_ready
            hw_ps hw_ready g1_ready g1b_ready mpg_ready fold_ps fold_ready ms_ps mmax mexp mrec mhalf mwT_ps mwT_ready gate_ps
            zb_ready tz_ready gm_ready fused_ready ss4 r4v r4 out_ready""".split()
        S = {n: sem(n) for n in names}

        def tl(n, t):
            return 2 * n + t + 1

        def add_turned(eng, t, b, done):
            rows = slice(b * SEQ, (b + 1) * SEQ)
            eng.tensor_tensor(qkz[t][rows, :, b * SEQ:(b + 1) * SEQ],
                              E[t][rows, 0:2 * H].rearrange("p (g c) -> p g c", g=8),
                              E[t][rows, 2 * H:4 * H].rearrange("p (g c) -> p g c", g=8), ALU.add).then_inc(done, 1)

        def expand(eng, t, groups, g0, g1, done):
            heads = NH // groups
            mask = cst[:, C_H16:C_H16 + 4] if heads == 4 else cst[:, C_H8:C_H8 + 8]
            shape = [P, g1 - g0, heads, SEQ]
            eng.tensor_tensor(kT[t][:, g0 * heads * SEQ:g1 * heads * SEQ].rearrange("p (g h k) -> p g h k", g=g1 - g0, h=heads),
                              kc[t][:, g0 * SEQ:g1 * SEQ].rearrange("p (g k) -> p g k", g=g1 - g0).unsqueeze(2).to_broadcast(shape),
                              mask.unsqueeze(1).unsqueeze(3).to_broadcast(shape), ALU.mult).then_inc(done, 1)

        def make_route(eng, k, step, done):
            ap, t0, t1 = type_parts[k]
            count = max(k, 1)
            eng.tensor_scalar(ap, ap.bitcast(I32), 1.0, None, ALU.is_equal).then_inc(step, 1)
            eng.wait_ge(step, count)
            hot = ap.rearrange("p (b s) -> p b s", s=SEQ)
            eng.tensor_tensor(route[:, t0:t1].rearrange("p (b s) -> p b s", s=SEQ)[:, :, 0:SEQ - 1],
                              hot[:, :, 0:SEQ - 1], hot[:, :, 1:SEQ], ALU.mult).then_inc(done, 1)

        def half(n, t, b):
            return 4 * n + 2 * t + b + 1

        def first(n):
            return isinstance(n, int) and n == 0

        stage = [raw[:, k, :] for k in range(4)]
        split = []
        for e, k in enumerate("vl"):
            for c in range(HC):
                split.append((d[f"L0_xattn_{k}_qkv"][c * P:(c + 1) * P, :], (0, c), w_qkv[0][:, e, c, :], w_qkv[1][:, e, c, :], P, 3 * H))
        N_QKV = len(split)
        for e, k in enumerate("vl"):
            split.append((d[f"L0_xattn_{k}_dense"].rearrange("(c p) n -> p c n", p=P), None, w_dense[0][:, :, e, :], w_dense[1][:, :, e, :], P, 2 * H))
        N_DENSE = len(split)
        for g, nm in enumerate(("gate", "up")):
            for e, k in enumerate("vl"):
                for c in range(HC):
                    cols = slice(g * INTER, (g + 1) * INTER)
                    split.append((d[f"L0_xattn_{k}_{nm}"][c * P:(c + 1) * P, :], (2, c), w_gu[0][:, e, c, cols], w_gu[1][:, e, c, cols], P, INTER))
        N_GU = len(split)
        for e, k in enumerate("vl"):
            split.append((d[f"L0_xattn_{k}_down"][0:3 * P, :].rearrange("(j p) n -> p j n", p=P), None,
                          w_down[0][:, 0:3, e, :], w_down[1][:, 0:3, e, :], P, 3 * H))
            for j in range(3, NJ):
                split.append((d[f"L0_xattn_{k}_down"][J0[j]:J0[j + 1], :], None,
                              w_down[0][0:JWS[j], j, e, :], w_down[1][0:JWS[j], j, e, :], JWS[j], H))
        NSTAGE = len(stage)

        def staged(k):
            _, _, hi, _, rows, cols = split[k]
            raw = stage[k % NSTAGE][0:rows, 0:cols]
            return raw if len(hi.shape) == 2 else raw.rearrange("p (j n) -> p j n", n=H)

        stored = [sem(f"stored{t}") for t in range(TILES)]
        wload = [sem(f"wload{k}") for k in range(NSTAGE)]

        FIRST = """
            first_routes:0 wsplit:0 xsplit:0 pos:0 table:0 wsplit:1 wsplit:2 wsplit:3 wsplit:4 route_t:0 wsplit:5
            xsq:0 qkv:0 xsq:1 rope:0 routes:1 qkT:0 wsplit:6 qkv:1 rope:1 score:0 qkT:1 wsplit:7 wsplit:8 wsplit:9
            wsplit:10 routes:2 probT:0 score:1 pv:0 ctxT:0 probT:1 wsplit:11 wsplit:12 routes:3 wsplit:13 dense:0
            pv:1 h1T:0 routes:4 wsplit:14 ctxT:1 cproj:0 wsplit:15 cqkT:0 wsplit:16 wsplit:17 routes:5 routes:6
            cscore:0 dense:1 fold:0 h1T:1 cproj:1 cprobT:0 cqkT:1 wsplit:18 cscore:1 cpv:0 cprobT:1 wsplit:19
            cctxT:0 next_xsplit:0 cdense:0 cpv:1 wsplit:20 next_qkv:0 mi:0 next_xsq:0 cctxT:1 next_rope:0 cdense:1
            next_xsq:1 next_qkv:1 wsplit:21 mi:1 next_rope:1"""
        STEADY = """
            miT:0 qkT:0 qkT:1 mlp:0 score:0 mlp:1 probT:0 hid:0 hid:1 mlp:2 pv:0 hid:2 mlp:3 hid:3 score:1 ctxT:0
            mlp:4 probT:1 dense:0 pv:1 hid:4 h1T:0 next_xsplit:0 mlp:5 cproj:0 hid:5 ctxT:1 down:0 cqkT:0 dense:1
            h3T:0 cscore:0 h1T:1 down:1 cprobT:0 cproj:1 hw:0 cqkT:1 h3T:1 mscore:0 cscore:1 cpv:0 hw:1 cprobT:1
            attnT:0 cctxT:0 mscore:1 cdense:0 gate:0 cpv:1 next_xsq:0 mi:0 next_qkv:0 cctxT:1 attnT:1 next_rope:0
            cdense:1 gate:1 mi:1 next_xsq:1 next_qkv:1 next_rope:1"""
        LAST = """
            miT:0 mlp:0 hid:0 mlp:1 hid:1 mlp:2 mlp:3 hid:2 hid:3 mlp:4 hid:4 mlp:5 hid:5 down:0 down:1 h3T:0 h3T:1
            hw:0 hw:1 mscore:0 mscore:1 attnT:0 attnT:1 gate:0 gate:1"""
        STAGE_B = "miT mlp hid down h3T hw mscore attnT gate".split()

        def run(eng, steps):
            def one(order, a, b, more=True):
                for name, i in [s.split(":") for s in order.split()]:
                    ahead = name.startswith("next_")
                    name = name.removeprefix("next_")
                    if name in steps and (more or not ahead):
                        steps[name](b if name in STAGE_B else a + 1 if ahead else a, int(i))
            one(FIRST, 0, None)
            one(STEADY, 1, 0)
            with eng.Fori(2, GROUPS - 1) as n:
                one(STEADY, n, n - 1)
            one(STEADY, GROUPS - 1, GROUPS - 2, more=False)
            one(LAST, None, GROUPS - 1)

        block = ctx.enter_context(nc.Block())

        @block.sync
        def _(sp):
            def load_xT(n):
                if not first(n):
                    sp.wait_ge(S["xl_ready"], n)
                sp.dma_start(xT[:, :, :], d["xT"][:, bass.ds(n * GT, GT)].rearrange("(c p) n -> p c n", p=P)).then_inc(S["ld_xT"], 16)

            def load_x(n):
                if not first(n):
                    sp.wait_ge(S["h1_ready"], tl(n, 1) - 2)
                sp.dma_start(x_sb[:, :, :], d["x"][bass.ds(n * GT, GT), :].rearrange("(t p) h -> p t h", p=P)).then_inc(S["ld_x"], 16)

            def load_ctx_a(n):
                if not first(n):
                    sp.wait_ge(S["ckv_ps"], tl(n, 1) - 2)
                sp.dma_start(ctxT_a[:, :], d["ctxT"][:, bass.ds(n * GT, GT)]).then_inc(S["ld_ca"], 16)

            def load_ctx_b(n):
                if not first(n):
                    sp.wait_ge(S["ms_ps"], tl(n, 1) - 2)
                sp.dma_start(ctxT_b[:, :], d["ctxT"][:, bass.ds(n * GT, GT)]).then_inc(S["ld_cb"], 16)

            def store(n):
                for t in range(TILES):
                    sp.wait_ge(S["out_ready"], tl(n, t))
                    sp.dma_start(out[bass.ds(n * GT + t * P, P), :], z[t][:, :]).then_inc(stored[t], 16)

            def load_raw(k):
                src, _, _, _, rows, cols = split[k]
                if k >= NSTAGE:
                    sp.wait_ge(S["wsplit_lo"], k - NSTAGE + 1)
                sp.dma_start(staged(k), src).then_inc(wload[k % NSTAGE], 16)

            sp.dma_start(ln[:, :, :].rearrange("p i c -> p (i c)"), d["ln"]).then_inc(S["ld_ln"], 16)
            load_raw(0)
            load_xT(0)
            for k in range(1, N_QKV):
                load_raw(k)
            load_x(0)
            sp.dma_start(types_t[:, :, :].rearrange("p a i -> p (a i)"), d["types_t"]).then_inc(S["ld_types_t"], 16)
            sp.dma_start(cst[:, :], d["consts"]).then_inc(S["ld_cst"], 16)
            for k in range(N_QKV, 2 * N_QKV):
                load_raw(k)
            for ap, t0, t1 in type_parts[1:]:
                sp.dma_start(ap.bitcast(I32), d["types"][0, t0:t1].partition_broadcast(P)).then_inc(S["ld_types"], 16)
            for c in range(HC):
                sp.dma_start(w_cq[:, c, :], d["L0_xattn_cq_w"][c * P:(c + 1) * P, :]).then_inc(S["ld_wa"], 16)
            sp.dma_start(w_ckv[:, :], d["L0_xattn_ckv_w"]).then_inc(S["ld_wa"], 16)
            sp.dma_start(w_cdense[:, :], d["L0_xattn_cdense_w"]).then_inc(S["ld_wa"], 16)
            load_ctx_a(0)
            for k in range(2 * N_QKV, N_GU):
                load_raw(k)
            load_xT(1)
            for k in range(N_GU, len(split)):
                load_raw(k)
            sp.dma_start(w_mem[:, :, :], d["W_mem"].rearrange("(c p) n -> p c n", p=P)).then_inc(S["ld_wb"], 16)
            sp.dma_start(w_gate2, d["W_gateT"][H:2 * H, :].rearrange("(c p) n -> p c n", p=P)).then_inc(S["ld_wb"], 16)
            sp.dma_start(w_memT[:, 0:H], d["W_memT"]).then_inc(S["ld_wb"], 16)
            sp.dma_start(w_gate[:, :, :], d["W_gateT"][0:H, :].rearrange("(c p) n -> p c n", p=P)).then_inc(S["ld_wb"], 16)
            sp.dma_start(b_gate[:, :], d["b_gate"].partition_broadcast(P)).then_inc(S["ld_bias"], 16)
            sp.dma_start(w_norm[:, :], d["w_norm"].partition_broadcast(P)).then_inc(S["ld_norm"], 16)
            load_x(1)
            load_ctx_a(1)
            load_ctx_b(0)
            with sp.Fori(2, GROUPS) as n:
                load_xT(n)
                load_x(n)
                load_ctx_a(n)
                load_ctx_b(n - 1)
                store(n - 2)
            load_ctx_b(GROUPS - 1)
            store(GROUPS - 2)
            store(GROUPS - 1)
            for t in range(TILES):
                sp.wait_ge(stored[t], 16 * GROUPS)

        @block.scalar
        def _(act):
            def wsplit(n, k):
                _, norm, hi, _, _, _ = split[k]
                if k == 0:
                    act.wait_ge(S["ld_ln"], 16)
                act.wait_ge(wload[k % NSTAGE], 16 * (k // NSTAGE + 1))
                act.activation(hi, staged(k), ACT.Copy, scale=ln[:, norm[0], norm[1]:norm[1] + 1] if norm else 1.0).then_inc(S["wsplit_hi"], 1)

            def square_sum(src, scratch, k, t, done):
                act.activation(scratch, src, ACT.Square, scale=H ** -0.5, accum_out=ss[:, k, t:t + 1]).then_inc(done, 1)

            def xsplit(n, t):
                act.wait_ge(S["ld_xT"], 16 * n + 16)
                if not first(n):
                    act.wait_ge(S["v_ps"], 2 * n)
                act.activation(xs[1][0][:, :, :], xT[:, :, :], ACT.Copy).then_inc(S["xh_ready"], 1)

            def xsq(n, t):
                act.wait_ge(S["ld_x"], 16 * n + 16)
                if not first(n):
                    act.wait_ge(S["h2_ready"], tl(n, t) - 2)
                square_sum(x_sb[:, t, :], h1[t][:, :], 0, t, S["ssx"])

            def rope_v(n, t):
                act.wait_ge(S["v_ps"], tl(n, t))
                act.wait_ge(S["r1"], tl(n, t))
                v = Y[t][:, 0:H].rearrange("p (a e k) -> p a e k", e=2, k=HD)
                for b in range(2):
                    rows = slice(b * SEQ, (b + 1) * SEQ)
                    for e in range(2):
                        act.activation(vb[t][e * SEQ:(e + 1) * SEQ, b, :, e, 0:HD], v[rows, :, e, :], ACT.Copy,
                                       scale=rstd[rows, 0, t:t + 1]).then_inc(S["vb_ready"], 1)

            def qkT(n, t):
                act.wait_ge(S["q_ps"], tl(n, t))
                act.activation(qT[t][:, :, :], Z[t][:, :].rearrange("p (g q) -> p g q", g=4), ACT.Copy).then_inc(S["qT_ready"], 1)

            def score(n, t):
                for b in range(2):
                    act.wait_ge(S["sub_ready"], half(n, t, b))
                    act.activation(E[t][:, b * 512:(b + 1) * 512], E[t][:, b * 512:(b + 1) * 512], ACT.Exp,
                                   scale=HD ** -0.5).then_inc(S["exp_ready"], 1)

            def probT(n, t):
                act.wait_ge(S["pT_psx"], tl(n, t))
                act.activation(pT[t][:, 0:4, :], X[t].rearrange("p (a q) -> p a q", a=4), ACT.Copy).then_inc(S["pT_readyx"], 1)

            def ctxT(n, t):
                act.wait_ge(S["attT_ps"], tl(n, t))
                act.activation(attT[t][0][:, :, :], Y[t][:, 0:H].rearrange("p (c q) -> p c q", c=HC), ACT.Copy).then_inc(S["attT_hi"], 1)

            def dense(n, t):
                act.wait_ge(S["h1_ready"], tl(n, t))
                square_sum(h1[t][:, :], att[t][:, :], 1, t, S["ss1"])

            def h1T_(n, t):
                act.wait_ge(S["h1T_ps"], tl(n, t))
                act.activation(h1T[t][:, :, :], Z[t][:, 0:H].rearrange("p (c q) -> p c q", c=HC), ACT.Copy).then_inc(S["h1T_ready"], 1)

            def cproj(n, t):
                act.wait_ge(S["ckv_ps"], tl(n, t))
                for b in range(2):
                    rows = slice(b * SEQ, (b + 1) * SEQ)
                    act.activation(qkz[t][rows, 2:4, b * SEQ:(b + 1) * SEQ],
                                   X[t][rows, 0:CC].rearrange("p (g c) -> p g c", g=2), ACT.Copy).then_inc(S["ck_ev"], 1)
                v = X[t][:, CC:2 * CC].rearrange("p (a e k) -> p a e k", e=2, k=CHD)
                for b in range(2):
                    rows = slice(b * SEQ, (b + 1) * SEQ)
                    for e in range(2):
                        act.activation(vb[t][e * SEQ:(e + 1) * SEQ, b, :, e, HD - CHD:HD], v[rows, :, e, :], ACT.Copy).then_inc(S["cvb_ready"], 1)

            def cqkT(n, t):
                act.wait_ge(S["cQ_ps"], tl(n, t))
                act.activation(qT[t][:, 0:2, :], Z[t][:, 0:2 * P].rearrange("p (g q) -> p g q", g=2), ACT.Copy).then_inc(S["cqT_ready"], 1)

            def cscore(n, t):
                for b in range(2):
                    act.wait_ge(S["csub"], half(n, t, b))
                    act.activation(E[t][:, b * 512:(b + 1) * 512], E[t][:, b * 512:(b + 1) * 512], ACT.Exp,
                                   scale=CHD ** -0.5).then_inc(S["cexp"], 1)

            def cprobT(n, t):
                act.wait_ge(S["cpT_psx"], tl(n, t))
                act.activation(pT[t][:, 0:4, :], X[t].rearrange("p (a q) -> p a q", a=4), ACT.Copy).then_inc(S["cpT_readyx"], 1)

            def cctxT(n, t):
                act.wait_ge(S["cattT_ps"], tl(n, t))
                act.activation(cattT[t], Y[t][:, 0:CC], ACT.Copy).then_inc(S["cattT_ready"], 1)

            def cdense(n, t):
                act.wait_ge(S["h2_ready"], tl(n, t))
                square_sum(h2[t][:, :], att[t][:, :], 2, t, S["ss2"])

            def miT(n, t):
                act.wait_ge(S["miT_ps"], n + 1)
                if not first(n):
                    act.wait_ge(S["gu_ps"], NJ * n)
                act.activation(ms[1][0][:, :, :], Z[1].rearrange("p (c q) -> p c q", c=HC), ACT.Copy).then_inc(S["mh_ready"], 1)

            def mlp(n, j):
                act.wait_ge(S["gu_ps"], NJ * n + j + 1)
                if j >= 2:
                    act.wait_ge(S["hid_lo"], NJ * n + j - 1)
                elif not first(n):
                    act.wait_ge(S["hid_lo"], NJ * n)
                act.activation(th[j % 2][0:JWS[j], :], B[(j + 1) % 2][0:JWS[j], 0:GT], ACT.Tanh, scale=0.5).then_inc(S["th_ready"], 1)
                if j == NJ - 1:
                    act.activation(up_rest[:, :], B[(j + 1) % 2][REST:P, 0:GT], ACT.Copy).then_inc(S["up_ready"], 1)

            def hid_hi(n, j):
                act.wait_ge(S["hid_ready"], NJ * n + j + 1)
                if not first(n):
                    act.wait_ge(S["down_ps"], 2 * n)
                act.activation(hid[0][0:JWS[j], j, :], th[j % 2][0:JWS[j], :], ACT.Copy).then_inc(S["hid_hi"], 1)

            def h3T_(n, t):
                act.wait_ge(S["h3T_ps"], tl(n, t))
                act.activation(h3m[t][:, :], C[t][:, :], ACT.Copy).then_inc(S["h3T_ready"], 1)

            def hw(n, t):
                act.wait_ge(S["hw_ps"], tl(n, t))
                act.activation(hwT[t], C[t][:, 0:P], ACT.Copy, scale=H ** -0.5).then_inc(S["hw_ready"], 1)
                if not first(n):
                    act.wait_ge(stored[t], 16 * n)
                act.activation(z[t][:, :], C[t][:, H:2 * H], ACT.Copy).then_inc(S["g1_ready"], 1)

            def fold(n, t):
                act.wait_ge(S["fold_ps"], 1)
                act.activation(w_memT[:, H:2 * H], B[0][:, 0:H], ACT.Copy).then_inc(S["fold_ready"], 1)

            def mscore(n, t):
                act.wait_ge(S["mmax"], tl(n, t))
                act.activation(mw[t], C[t][:, 0:P], ACT.Exp, bias=mm[:, t, 0:1], accum_out=mm[:, t, 1:2]).then_inc(S["mexp"], 1)
                act.activation(mpg[t][:, :], C[t][:, H:2 * H], ACT.Copy).then_inc(S["mpg_ready"], 1)

            def attnT(n, t):
                act.wait_ge(S["mwT_ps"], tl(n, t))
                act.activation(mwT[t][:, :], C[t][:, P:2 * P], ACT.Copy).then_inc(S["mwT_ready"], 1)

            def gate(n, t):
                act.wait_ge(S["zb_ready"], tl(n, t))
                act.activation(z[t][:, :], z[t][:, :], ACT.Tanh, scale=0.5).then_inc(S["tz_ready"], 1)
                act.wait_ge(S["fused_ready"], tl(n, t))
                square_sum(h3[t][:, :], z[t][:, :], 3, t, S["ss4"])

            run(act, dict(wsplit=wsplit, xsplit=xsplit, rope=rope_v, qkT=qkT, score=score, probT=probT, ctxT=ctxT, dense=dense, h1T=h1T_,
                          cproj=cproj, cqkT=cqkT, cscore=cscore, cprobT=cprobT, cctxT=cctxT, cdense=cdense, miT=miT, mlp=mlp,
                          hid=hid_hi, h3T=h3T_, hw=hw, fold=fold, mscore=mscore, attnT=attnT, gate=gate, xsq=xsq))

        @block.vector
        def _(dve):
            def first_routes(n, t):
                dve.wait_ge(S["last_ready"], 1)
                dve.wait_ge(S["ld_type0"], 16)
                make_route(dve, 0, S["type0_step"], S["route0_ready"])

            def pos_step(n, t):
                dve.wait_ge(S["ld_cst"], 16)
                dve.tensor_copy(ident_h[:, :], ident).then_inc(S["cst_ready"], 1)
                dve.tensor_copy(causal_h[:, :, :], cst[:, C_CAUS:C_CAUS + SEQ].unsqueeze(1).to_broadcast([P, 8, SEQ])).then_inc(S["cst_ready"], 1)
                dve.tensor_copy(block_h[:, :], cst[:, C_BLK:C_BLK + P]).then_inc(S["cst_ready"], 1)
                dve.wait_ge(S["ld_pos"], 32)
                dve.tensor_copy(pos_f[0], pos_i).then_inc(S["pos_step"], 1)
                dve.wait_ge(S["pos_step"], 1)
                dve.tensor_scalar(pos_f[1], pos_f[0], 0.0, float(SEQ), ALU.is_lt, ALU.mult).then_inc(S["pos_step"], 1)
                dve.wait_ge(S["pos_step"], 2)
                dve.tensor_tensor(pos_f[2], pos_f[0], pos_f[1], ALU.add).then_inc(S["pos_step"], 1)
                dve.wait_ge(S["pos_step"], 3)
                dve.tensor_scalar(pos_f[0], pos_f[2], 0.0, float(SEQ - 1), ALU.max, ALU.min).then_inc(S["pos_step"], 1)
                dve.wait_ge(S["pos_step"], 4)
                dve.tensor_scalar(pos_f[1], pos_f[0], cst[0:SEQ, C_IOTA:C_IOTA + 1], None, ALU.is_equal).then_inc(S["hot_ready"], 1)

            def table(n, t):
                dve.wait_ge(S["rope_ps"], 1)
                dve.tensor_copy(rope[:, :], Z[0][:, 0:2 * HD]).then_inc(S["rope_ready"], 1)
                dve.wait_ge(S["rope_ready"], 1)

            def route_t_step(n, t):
                dve.wait_ge(S["ld_types_t"], 16)
                dve.tensor_scalar(hot_t[:, :, :], types_t[:, :, :], 1.0, None, ALU.is_equal).then_inc(S["route_t_step"], 1)
                dve.wait_ge(S["route_t_step"], 1)
                dve.wait_ge(S["ld_cst"], 16)
                dve.scalar_tensor_tensor(out=route_t[:, 0, :], in0=hot_t[:, 0, :], scalar=cst[:, C_NEXT:C_NEXT + 1], in1=hot_t[:, 1, :],
                                         op0=ALU.mult, op1=ALU.mult).then_inc(S["route_t_ready"], 1)
                dve.wait_ge(S["route_t_ready"], 1)
                dve.tensor_scalar(route_t[:, 1, :], route_t[:, 0, :], -1.0, 1.0, ALU.mult, ALU.add).then_inc(S["route_t_ready"], 1)
                dve.wait_ge(S["route_t_ready"], 2)

            def wsplit(n, k):
                _, norm, hi, lo, _, _ = split[k]
                dve.wait_ge(S["wsplit_hi"], k + 1)
                if norm:
                    dve.scalar_tensor_tensor(out=lo, in0=staged(k), scalar=ln[:, norm[0], norm[1]:norm[1] + 1], in1=hi.bitcast(F32),
                                             op0=ALU.mult, op1=ALU.subtract).then_inc(S["wsplit_lo"], 1)
                else:
                    dve.tensor_tensor(lo, staged(k), hi.bitcast(F32), ALU.subtract).then_inc(S["wsplit_lo"], 1)
                if k == N_DENSE + 2 * HC:
                    dve.wait_ge(S["ld_wa"], 16 * (HC + 2))
                    for c in range(HC):
                        dve.tensor_scalar(w_cq[:, c, :], w_cq[:, c, :], ln[:, 1, c:c + 1], None, ALU.mult).then_inc(S["cq_ready"], 1)

            def route_hi(n, s, v_ready, ready):
                m = route[:, bass.ds(n * GT, GT)].unsqueeze(1).to_broadcast([P, HC, GT])
                dve.tensor_tensor(s[0][0][:, :, :], s[1][0][:, :, :].bitcast(F32), m, ALU.mult).then_inc(v_ready, 1)
                dve.wait_ge(v_ready, n + 1)
                dve.tensor_tensor(s[1][0][:, :, :], s[1][0][:, :, :].bitcast(F32), s[0][0][:, :, :].bitcast(F32),
                                  ALU.subtract).then_inc(ready, 1)

            def xsplit(n, t):
                if first(n):
                    dve.wait_ge(S["route0_ready"], 1)
                elif isinstance(n, int) and n == 1:
                    dve.wait_ge(S["route_ready"], 1)
                dve.wait_ge(S["xh_ready"], n + 1)
                dve.tensor_tensor(xs[1][1][:, :, :], xT[:, :, :], xs[1][0][:, :, :].bitcast(F32), ALU.subtract).then_inc(S["xl_ready"], 1)
                dve.wait_ge(S["xl_ready"], n + 1)
                route_hi(n, xs, S["xv_hi"], S["xs_hi"])

            def xsq(n, t):
                dve.wait_ge(S["r1"], tl(n, t))
                dve.tensor_scalar(rope_r[:, t, :], rope[:, :], rstd[:, 0, t:t + 1], None, ALU.mult).then_inc(S["roper"], 1)

            def rope_q(n, t):
                dve.wait_ge(S["qk_ps"], tl(n, t))
                dve.wait_ge(S["roper"], tl(n, t))
                if not first(n):
                    dve.wait_ge(S["cpT_psy"], tl(n, t) - 2)
                qk = X[t].rearrange("p (h d) -> p h d", d=HD)
                straight = E[t][:, 0:2 * H].rearrange("p (h d) -> p h d", d=HD)
                turned = E[t][:, 2 * H:4 * H].rearrange("p (h d) -> p h d", d=HD)
                hd2 = HD // 2

                def table(a, b):
                    return rope_r[:, t, a:b].unsqueeze(1).to_broadcast([P, 2 * NH, b - a])
                dve.tensor_tensor(straight, qk, table(0, HD), ALU.mult).then_inc(S["rope_a"], 1)
                dve.tensor_tensor(turned[:, :, 0:hd2], qk[:, :, hd2:HD], table(HD, HD + hd2), ALU.mult).then_inc(S["rope_b"], 1)
                dve.tensor_tensor(turned[:, :, hd2:HD], qk[:, :, 0:hd2], table(HD + hd2, 2 * HD), ALU.mult).then_inc(S["rope_b"], 1)
                dve.wait_ge(S["rope_b"], 4 * n + 2 * t + 2)
                add_turned(dve, t, 1, S["qkz_b_ready"])

            def compact(t, groups, done):
                dve.tensor_reduce(kc[t][:, 0:groups * SEQ].rearrange("p (g k) -> p g k", g=groups),
                                  Y[t][:, 0:groups * P].rearrange("p (g b k) -> p g k b", g=groups, b=2), AX.X, ALU.add).then_inc(done, 1)

            def qkT(n, t):
                dve.wait_ge(S["k_ps"], tl(n, t))
                if not first(n):
                    dve.wait_ge(S["miT_ps"], n)
                compact(t, 4, S["kc_ready"])
                dve.wait_ge(S["kc_ready"], tl(n, t))
                if not first(n):
                    dve.wait_ge(S["cpv_ps"], tl(n, t) - 2)
                expand(dve, t, 4, 0, 2, S["kTa_ready"])

            def max_sub(t, n, s_ps, max_ready, sub_ready):
                for b in range(2):
                    s = xy[t][:, b, :].rearrange("p (h k) -> p h k", k=SEQ)
                    heads = slice(b * PAIRS, (b + 1) * PAIRS)
                    dve.wait_ge(s_ps, half(n, t, b))
                    dve.tensor_reduce(mx[:, t, heads], s, AX.X, ALU.max).then_inc(max_ready, 1)
                    dve.wait_ge(max_ready, half(n, t, b))
                    dve.tensor_tensor(E[t][:, b * 512:(b + 1) * 512].rearrange("p (h k) -> p h k", k=SEQ), s,
                                      mx[:, t, heads].unsqueeze(2).to_broadcast([P, PAIRS, SEQ]), ALU.subtract).then_inc(sub_ready, 1)

            def score(n, t):
                max_sub(t, n, S["s_ps"], S["max_ready"], S["sub_ready"])

            def probT(n, t):
                dve.wait_ge(S["pT_psy"], tl(n, t))
                dve.tensor_copy(pT[t][:, 4:8, :], Y[t].rearrange("p (a q) -> p a q", a=4)).then_inc(S["pT_ready"], 1)

            def normed(n, t, hd, pv_ps, rec_ready, done):
                o = yz[t][:, :, 0:4 * (hd + 1)].rearrange("p a (b e d) -> p b a e d", b=2, e=2)
                dve.wait_ge(pv_ps, tl(n, t))
                for b in range(2):
                    rows = slice(b * SEQ, (b + 1) * SEQ)
                    dve.reciprocal(rec[rows, t, :].rearrange("p (a e) -> p a e", e=2), o[rows, b, :, :, hd]).then_inc(rec_ready, 1)
                for b in range(2):
                    rows = slice(b * SEQ, (b + 1) * SEQ)
                    dve.wait_ge(rec_ready, half(n, t, b))
                    dve.tensor_tensor(att[t][rows, 0:NH * hd].rearrange("p (a e d) -> p a e d", a=PAIRS, e=2), o[rows, b, :, :, 0:hd],
                                      rec[rows, t, :].rearrange("p (a e) -> p a e", e=2).unsqueeze(3).to_broadcast([SEQ, PAIRS, 2, hd]),
                                      ALU.mult).then_inc(done, 1)

            def pv(n, t):
                normed(n, t, HD, S["pv_ps"], S["rec_ready"], S["att_ready"])

            def routed_add(out_, ps, rest, n, t, mid, done):
                dve.scalar_tensor_tensor(out=out_, in0=ps[:, 0:H], scalar=route_t[:, 0, bass.ds(2 * n + t, 1)], in1=rest,
                                         op0=ALU.mult, op1=ALU.add).then_inc(mid, 1)
                dve.wait_ge(mid, tl(n, t))
                dve.scalar_tensor_tensor(out=out_, in0=ps[:, H:2 * H], scalar=route_t[:, 1, bass.ds(2 * n + t, 1)], in1=out_,
                                         op0=ALU.mult, op1=ALU.add).then_inc(done, 1)

            def ctxT(n, t):
                dve.wait_ge(S["attT_hi"], tl(n, t))
                dve.tensor_tensor(attT[t][1][:, :, :], Y[t][:, 0:H].rearrange("p (c q) -> p c q", c=HC),
                                  attT[t][0][:, :, :].bitcast(F32), ALU.subtract).then_inc(S["attT_lo"], 1)

            def dense(n, t):
                dve.wait_ge(S["dense_ps"], tl(n, t))
                if not first(n):
                    dve.wait_ge(S["h2_ready"], tl(n, t) - 2)
                routed_add(h1[t][:, :], X[t], x_sb[:, t, :], n, t, S["h1a"], S["h1_ready"])

            def cproj(n, t):
                dve.wait_ge(S["cq_ps"], tl(n, t))
                dve.wait_ge(S["r2"], tl(n, t))
                for b in range(2):
                    rows = slice(b * SEQ, (b + 1) * SEQ)
                    dve.tensor_scalar(qkz[t][rows, 0:2, b * SEQ:(b + 1) * SEQ],
                                      Y[t][rows, 0:CC].rearrange("p (g c) -> p g c", g=2),
                                      rstd[rows, 1, t:t + 1], None, ALU.mult).then_inc(S["cq_ev"], 1)

            def cqkT(n, t):
                dve.wait_ge(S["cK_ps"], tl(n, t))
                compact(t, 2, S["ckc_ready"])
                dve.wait_ge(S["ckc_ready"], tl(n, t))
                expand(dve, t, 2, 0, 1, S["ckTa_ready"])

            def cscore(n, t):
                max_sub(t, n, S["cs_ps"], S["cmax"], S["csub"])

            def cprobT(n, t):
                dve.wait_ge(S["cpT_psy"], tl(n, t))
                dve.tensor_copy(pT[t][:, 4:8, :], Y[t].rearrange("p (a q) -> p a q", a=4)).then_inc(S["cpT_ready"], 1)

            def cpv(n, t):
                normed(n, t, CHD, S["cpv_ps"], S["crec"], S["catt_ready"])

            def cdense(n, t):
                dve.wait_ge(S["cdense_ps"], tl(n, t))
                if not first(n):
                    dve.wait_ge(S["h3_ready"], tl(n, t) - 2)
                dve.tensor_tensor(h2[t][:, :], X[t][:, 0:H], h1[t][:, :], ALU.add).then_inc(S["h2_ready"], 1)

            def mi_(n, t):
                dve.wait_ge(S["r3"], tl(n, t))
                dve.tensor_scalar(mi[t][:, :], h2[t][:, :], rstd[:, 2, t:t + 1], None, ALU.mult).then_inc(S["mi_ready"], 1)

            def miT(n, t):
                dve.wait_ge(S["mh_ready"], n + 1)
                dve.tensor_tensor(ms[1][1][:, :, :], Z[1].rearrange("p (c q) -> p c q", c=HC),
                                  ms[1][0][:, :, :].bitcast(F32), ALU.subtract).then_inc(S["ml_ready"], 1)
                dve.wait_ge(S["ml_ready"], n + 1)
                route_hi(n, ms, S["mv_hi"], S["ms_hi"])
                dve.wait_ge(S["mv_lo"], n + 1)
                dve.tensor_tensor(ms[1][1][:, :, :], ms[1][1][:, :, :].bitcast(F32), ms[0][1][:, :, :].bitcast(F32),
                                  ALU.subtract).then_inc(S["ms_lo"], 1)

            def mlp(n, j):
                w, g = JWS[j], B[(j + 1) % 2][0:JWS[j], 0:GT]
                u = B[(j + 1) % 2][0:w, GT:2 * GT] if j < NJ - 1 else up_rest[:, :]
                dve.wait_ge(S["th_ready"], NJ * n + j + 1)
                dve.scalar_tensor_tensor(out=th[j % 2][0:w, :], in0=th[j % 2][0:w, :], scalar=1.0, in1=g,
                                         op0=ALU.add, op1=ALU.mult).then_inc(S["gt_ready"], 1)
                dve.wait_ge(S["gt_ready"], NJ * n + j + 1)
                if j == NJ - 1:
                    dve.wait_ge(S["up_ready"], n + 1)
                dve.scalar_tensor_tensor(out=th[j % 2][0:w, :], in0=th[j % 2][0:w, :], scalar=0.5, in1=u,
                                         op0=ALU.mult, op1=ALU.mult).then_inc(S["hid_ready"], 1)

            def down(n, t):
                dve.wait_ge(S["down_ps"], tl(n, t))
                if not first(n):
                    dve.wait_ge(S["out_ready"], tl(n, t) - 2)
                routed_add(h3[t][:, :], C[t], h2[t][:, :], n, t, S["h3a"], S["h3_ready"])

            def mscore(n, t):
                dve.wait_ge(S["ms_ps"], tl(n, t))
                dve.tensor_reduce(mm[:, t, 0:1], C[t][:, 0:P], AX.X, ALU.max, negate=True).then_inc(S["mmax"], 1)

            def attnT(n, t):
                dve.wait_ge(S["mexp"], tl(n, t))
                dve.reciprocal(mm[:, t, 2:3], mm[:, t, 1:2]).then_inc(S["mrec"], 1)
                dve.wait_ge(S["mrec"], tl(n, t))
                dve.tensor_scalar(mm[:, t, 3:4], mm[:, t, 2:3], 0.5, None, ALU.mult).then_inc(S["mhalf"], 1)

            def gate(n, t):
                dve.wait_ge(S["gate_ps"], tl(n, t))
                if first(n) and t == 0:
                    dve.wait_ge(S["ld_norm"], 16)
                dve.wait_ge(S["g1b_ready"], tl(n, t))
                dve.scalar_tensor_tensor(out=z[t][:, :], in0=C[t][:, H:2 * H], scalar=mm[:, t, 2:3], in1=z[t][:, :],
                                         op0=ALU.mult, op1=ALU.add).then_inc(S["zb_ready"], 1)
                dve.wait_ge(S["tz_ready"], tl(n, t))
                dve.scalar_tensor_tensor(out=z[t][:, :], in0=z[t][:, :], scalar=1.0, in1=C[t][:, 0:H],
                                         op0=ALU.add, op1=ALU.mult).then_inc(S["gm_ready"], 1)
                dve.wait_ge(S["gm_ready"], tl(n, t))
                dve.wait_ge(S["mhalf"], tl(n, t))
                dve.scalar_tensor_tensor(out=h3[t][:, :], in0=z[t][:, :], scalar=mm[:, t, 3:4], in1=h3[t][:, :],
                                         op0=ALU.mult, op1=ALU.add).then_inc(S["fused_ready"], 1)
                dve.wait_ge(S["r4"], tl(n, t))
                dve.scalar_tensor_tensor(out=z[t][:, :], in0=h3[t][:, :], scalar=rstd[:, 3, t:t + 1], in1=w_norm[:, :],
                                         op0=ALU.mult, op1=ALU.mult).then_inc(S["out_ready"], 1)

            run(dve, dict(first_routes=first_routes, pos=pos_step, table=table, route_t=route_t_step, wsplit=wsplit, xsplit=xsplit, rope=rope_q, qkT=qkT, score=score, probT=probT, pv=pv, ctxT=ctxT, dense=dense, cproj=cproj,
                          cqkT=cqkT, cscore=cscore, cprobT=cprobT, cpv=cpv, cdense=cdense, mi=mi_, miT=miT, mlp=mlp, down=down,
                          mscore=mscore, attnT=attnT, gate=gate, xsq=xsq))

        @block.gpsimd
        def _(pool):
            pool.dma_start(type_parts[0][0].bitcast(I32), d["types"][0, 0:GT].partition_broadcast(P)).then_inc(S["ld_type0"], 16)
            for k in range(2):
                pool.dma_start(pos_i[:, k * SEQ:(k + 1) * SEQ], d["pos"][0, :].partition_broadcast(SEQ)).then_inc(S["ld_pos"], 16)
            pool.memset(route[:, SEQ - 1:N_TOK:SEQ], 0.0).then_inc(S["last_ready"], 1)
            pool.memset(pow_eps[:, 0:1], -0.5).then_inc(S["small_ready"], 1)
            pool.memset(pow_eps[:, 1:2], EPS).then_inc(S["small_ready"], 1)
            pool.wait_ge(S["small_ready"], 2)
            for t in range(TILES):
                pool.memset(qkz[t][:, :, :], 0.0).then_inc(S["zeroed"], 1)
                pool.memset(vb[t][:, :, :, :, :], 0.0).then_inc(S["zeroed"], 1)
            pool.wait_ge(S["zeroed"], 2 * TILES)
            for t in range(TILES):
                for e in range(2):
                    rows = slice(e * SEQ, (e + 1) * SEQ)
                    pool.memset(vb[t][rows, :, :, e, HD:HD + 1], 1.0).then_inc(S["zeroed"], 1)
                    pool.wait_ge(S["zeroed"], 2 * TILES + 2 * t + e + 1)

            def inv_rms(k, t, n, sums, mid, done):
                pool.wait_ge(sums, tl(n, t))
                pool.tensor_tensor(var[:, k, t:t + 1], ss[:, k, t:t + 1], pow_eps[:, 1:2], ALU.add).then_inc(mid, 1)
                pool.wait_ge(mid, tl(n, t))
                pool.tensor_tensor(rstd[:, k, t:t + 1], var[:, k, t:t + 1], pow_eps[:, 0:1], ALU.pow).then_inc(done, 1)

            def route_v_lo(n, s, lo_ready, v_ready):
                m = route[:, bass.ds(n * GT, GT)].unsqueeze(1).to_broadcast([P, HC, GT])
                pool.wait_ge(S["zeroed"], 4 * TILES)
                if isinstance(n, int) and n == 1:
                    pool.wait_ge(S["route_ready"], len(type_parts) - 1)
                pool.wait_ge(lo_ready, n + 1)
                pool.tensor_tensor(s[0][1][:, :, :], s[1][1][:, :, :].bitcast(F32), m, ALU.mult).then_inc(v_ready, 1)

            def routes(n, k):
                pool.wait_ge(S["ld_types"], 16 * (len(type_parts) - 1))
                make_route(pool, k, S["type_step"], S["route_ready"])

            def xsplit(n, t):
                if first(n):
                    pool.wait_ge(S["route0_ready"], 1)
                route_v_lo(n, xs, S["xl_ready"], S["xv_lo"])
                pool.wait_ge(S["xv_lo"], n + 1)
                pool.tensor_tensor(xs[1][1][:, :, :], xs[1][1][:, :, :].bitcast(F32), xs[0][1][:, :, :].bitcast(F32),
                                   ALU.subtract).then_inc(S["xs_lo"], 1)

            def xsq(n, t):
                if not first(n):
                    pool.wait_ge(S["vb_ready"], 4 * (tl(n, t) - 2))
                inv_rms(0, t, n, S["ssx"], S["r1v"], S["r1"])

            def rope_add(n, t):
                pool.wait_ge(S["rope_a"], tl(n, t))
                pool.wait_ge(S["rope_b"], 4 * n + 2 * t + 2)
                add_turned(pool, t, 0, S["qkz_a_ready"])
                pool.wait_ge(S["qkz_a_ready"], tl(n, t))

            def qkT(n, t):
                pool.wait_ge(S["kc_ready"], tl(n, t))
                if not first(n):
                    pool.wait_ge(S["cpv_ps"], tl(n, t) - 2)
                expand(pool, t, 4, 2, 4, S["kT_ready"])

            def cqkT(n, t):
                pool.wait_ge(S["ckc_ready"], tl(n, t))
                expand(pool, t, 2, 1, 2, S["ckT_ready"])

            def dense(n, t):
                inv_rms(1, t, n, S["ss1"], S["r2v"], S["r2"])

            def cdense(n, t):
                inv_rms(2, t, n, S["ss2"], S["r3v"], S["r3"])

            def miT(n, t):
                route_v_lo(n, ms, S["ml_ready"], S["mv_lo"])

            def hid_lo(n, j):
                pool.wait_ge(S["hid_hi"], NJ * n + j + 1)
                pool.tensor_tensor(hid[1][0:JWS[j], j, :], th[j % 2][0:JWS[j], :], hid[0][0:JWS[j], j, :].bitcast(F32),
                                   ALU.subtract).then_inc(S["hid_lo"], 1)

            def hw(n, t):
                if first(n):
                    pool.wait_ge(S["ld_bias"], 16)
                pool.wait_ge(S["g1_ready"], tl(n, t))
                pool.tensor_tensor(z[t][:, :], z[t][:, :], b_gate[:, :], ALU.add).then_inc(S["g1b_ready"], 1)

            def gate(n, t):
                inv_rms(3, t, n, S["ss4"], S["r4v"], S["r4"])

            run(pool, dict(routes=routes, xsplit=xsplit, xsq=xsq, rope=rope_add, qkT=qkT, cqkT=cqkT, dense=dense, cdense=cdense, miT=miT, hid=hid_lo, hw=hw, gate=gate))

        @block.tensor
        def _(pe):
            def split_product(o, stationary, moving, start, stop):
                (sh, sl), (mh, ml) = stationary, moving
                pe.matmul(o, sh, mh, start=start, stop=False)
                pe.matmul(o, sh, ml, start=False, stop=False)
                return pe.matmul(o, sl, mh, start=False, stop=stop)

            def table(n, t):
                pe.wait_ge(S["ld_cst"], 16)
                pe.wait_ge(S["hot_ready"], 1)
                pe.matmul(Z[0][:, 0:2 * HD], pos_f[1], cst[0:SEQ, C_ROPE:C_ROPE + 2 * HD], start=True, stop=True).then_inc(S["rope_ps"], 1)

            def qkv(n, t):
                cols = slice(t * P, (t + 1) * P)
                pe.wait_ge(S["xv_hi"], n + 1)
                if first(n):
                    pe.wait_ge(S["wsplit_lo"], 4)
                    pe.wait_ge(S["zeroed"], 4 * TILES)
                else:
                    pe.wait_ge(S["h2_ready"], tl(n, t) - 2)
                for o, a, b, done in ((X[t], 0, 2 * H, S["qk_ps"]), (Y[t][:, 0:H], 2 * H, 3 * H, S["v_ps"])):
                    for e in range(2):
                        if e == 1:
                            pe.wait_ge(S["xs_hi"], n + 1)
                        for c in range(HC):
                            for s in range(2):
                                pe.matmul(o, xs[e][0][:, c, cols], w_qkv[s][:, e, c, a:b], start=(e == 0 and c == 0 and s == 0), stop=False)
                    pe.wait_ge(S["xs_lo"], n + 1)
                    for e in range(2):
                        for c in range(HC):
                            last = pe.matmul(o, xs[e][1][:, c, cols], w_qkv[0][:, e, c, a:b], start=False, stop=(e == 1 and c == HC - 1))
                    last.then_inc(done, 1)

            def turn(n, t, groups, q_ps, k_ps):
                for g in range(groups):
                    last = pe.transpose(Z[t][:, g * P:(g + 1) * P], qkz[t][:, g, :], ident)
                last.then_inc(q_ps, 1)
                for g in range(groups):
                    last = pe.transpose(Y[t][:, g * P:(g + 1) * P], qkz[t][:, groups + g, :], ident)
                last.then_inc(k_ps, 1)

            def qkT(n, t):
                pe.wait_ge(S["qkz_a_ready"], tl(n, t))
                pe.wait_ge(S["qkz_b_ready"], tl(n, t))
                pe.wait_ge(S["vb_ready"], 4 * tl(n, t))
                if t == 1 and not first(n):
                    pe.wait_ge(S["ml_ready"], n)
                turn(n, t, 4, S["q_ps"], S["k_ps"])

            def score(n, t):
                pe.wait_ge(S["qT_ready"], tl(n, t))
                for b in range(2):
                    pe.wait_ge(S[("kTa_ready", "kT_ready")[b]], tl(n, t))
                    pe.matmul(xy[t][:, b, :], ident_h[:, :], causal_h[:, :, :].rearrange("p h k -> p (h k)"), start=True, stop=False)
                    for g in (2 * b, 2 * b + 1):
                        last = pe.matmul(xy[t][:, b, (g % 2) * GT:(g % 2 + 1) * GT], qT[t][:, g, :], kT[t][:, g * GT:(g + 1) * GT],
                                         start=False, stop=(g % 2 == 1))
                    last.then_inc(S["s_ps"], 1)

            def turn_probs(n, t, exp_ready, psx, psy):
                for a in range(PAIRS):
                    if a % 4 == 0:
                        pe.wait_ge(exp_ready, half(n, t, a // 4))
                    last = pe.transpose(xy[t][:, a // 4, (a % 4) * P:(a % 4 + 1) * P], E[t][:, a * P:(a + 1) * P], ident)
                    if a == 3:
                        last.then_inc(psx, 1)
                last.then_inc(psy, 1)

            def probT(n, t):
                turn_probs(n, t, S["exp_ready"], S["pT_psx"], S["pT_psy"])

            def apply(t, hd, done):
                for a in range(PAIRS):
                    last = pe.matmul(yz[t][:, a, 0:4 * (hd + 1)], pT[t][:, a, :], vb[t][:, :, a, :, HD - hd:HD + 1], start=True, stop=True)
                last.then_inc(done, 1)

            def pv(n, t):
                pe.wait_ge(S["pT_readyx"], tl(n, t))
                pe.wait_ge(S["pT_ready"], tl(n, t))
                apply(t, HD, S["pv_ps"])

            def ctxT(n, t):
                pe.wait_ge(S["att_ready"], half(n, t, 1))
                for c in range(HC):
                    last = pe.transpose(Y[t][:, c * P:(c + 1) * P], att[t][:, c * P:(c + 1) * P], ident)
                last.then_inc(S["attT_ps"], 1)

            def dense(n, t):
                pe.wait_ge(S["attT_lo"], tl(n, t))
                if first(n):
                    pe.wait_ge(S["wsplit_lo"], N_DENSE)
                for c in range(HC):
                    last = split_product(X[t], [attT[t][s][:, c, :] for s in range(2)],
                                         [w_dense[s][:, c, :, :].rearrange("p e n -> p (e n)") for s in range(2)],
                                         start=(c == 0), stop=(c == HC - 1))
                last.then_inc(S["dense_ps"], 1)

            def h1T_(n, t):
                pe.wait_ge(S["h1_ready"], tl(n, t))
                for c in range(HC):
                    last = pe.transpose(Z[t][:, c * P:(c + 1) * P], h1[t][:, c * P:(c + 1) * P], ident)
                last.then_inc(S["h1T_ps"], 1)

            def cproj(n, t):
                pe.wait_ge(S["ld_ca"], 16 * n + 16)
                pe.wait_ge(S["h1T_ready"], tl(n, t))
                if first(n):
                    pe.wait_ge(S["ld_wa"], 16 * (HC + 2))
                    pe.wait_ge(S["cq_ready"], HC)
                pe.matmul(X[t][:, 0:2 * CC], ctxT_a[:, t * P:(t + 1) * P], w_ckv[:, :], start=True, stop=True).then_inc(S["ckv_ps"], 1)
                for c in range(HC):
                    last = pe.matmul(Y[t][:, 0:CC], h1T[t][:, c, :], w_cq[:, c, :], start=(c == 0), stop=(c == HC - 1))
                last.then_inc(S["cq_ps"], 1)

            def cqkT(n, t):
                pe.wait_ge(S["cq_ev"], 2 * tl(n, t))
                pe.wait_ge(S["ck_ev"], 2 * tl(n, t))
                turn(n, t, 2, S["cQ_ps"], S["cK_ps"])

            def cscore(n, t):
                pe.wait_ge(S["cqT_ready"], tl(n, t))
                pe.wait_ge(S["cvb_ready"], 4 * tl(n, t))
                for g in range(2):
                    pe.wait_ge(S[("ckTa_ready", "ckT_ready")[g]], tl(n, t))
                    pe.matmul(xy[t][:, g, :], qT[t][:, g, :], kT[t][:, g * 512:(g + 1) * 512], start=True, stop=True).then_inc(S["cs_ps"], 1)

            def cprobT(n, t):
                turn_probs(n, t, S["cexp"], S["cpT_psx"], S["cpT_psy"])

            def cpv(n, t):
                pe.wait_ge(S["cpT_readyx"], tl(n, t))
                pe.wait_ge(S["cpT_ready"], tl(n, t))
                apply(t, CHD, S["cpv_ps"])

            def cctxT(n, t):
                pe.wait_ge(S["catt_ready"], half(n, t, 1))
                pe.transpose(Y[t][:, 0:CC], att[t][:, 0:CC], ident).then_inc(S["cattT_ps"], 1)

            def cdense(n, t):
                pe.wait_ge(S["cattT_ready"], tl(n, t))
                pe.matmul(X[t][:, 0:H], cattT[t], w_cdense[:, :], start=True, stop=True).then_inc(S["cdense_ps"], 1)

            def miT(n, t):
                for t in range(TILES):
                    pe.wait_ge(S["mi_ready"], tl(n, t))
                    for c in range(HC):
                        last = pe.transpose(Z[1][:, c * GT + t * P:c * GT + (t + 1) * P], mi[t][:, c * P:(c + 1) * P], ident)
                last.then_inc(S["miT_ps"], 1)

            def mlp(n, j):
                w, bank = JWS[j], B[(j + 1) % 2]
                pe.wait_ge(S["mv_hi"], n + 1)
                if first(n) and j == 0:
                    pe.wait_ge(S["wsplit_lo"], N_GU)
                if j >= 2:
                    pe.wait_ge(S["hid_ready"], NJ * n + j - 1)
                elif not first(n):
                    pe.wait_ge(S["gm_ready"], tl(n, j) - 2)
                for g, (c0, c1) in enumerate([(J0[j], J0[j] + w), (INTER + REST + J0[j], INTER + REST + J0[j] + w)] if j < NJ - 1 else
                                             [(INTER - REST, INTER + REST)]):
                    o = bank[0:c1 - c0, g * GT:(g + 1) * GT]
                    for e in range(2):
                        if e == 1:
                            pe.wait_ge(S["ms_hi"], n + 1)
                        for c in range(HC):
                            for s in range(2):
                                pe.matmul(o, w_gu[s][:, e, c, c0:c1], ms[e][0][:, c, :], start=(e == 0 and c == 0 and s == 0), stop=False)
                    pe.wait_ge(S["ms_lo"], n + 1)
                    for e in range(2):
                        for c in range(HC):
                            last = pe.matmul(o, w_gu[0][:, e, c, c0:c1], ms[e][1][:, c, :], start=False, stop=(e == 1 and c == HC - 1))
                last.then_inc(S["gu_ps"], 1)

            def down(n, t):
                pe.wait_ge(S["hid_ready"], NJ * n + NJ - 1 + t)
                if first(n) and t == 0:
                    pe.wait_ge(S["wsplit_lo"], len(split))
                for j in range(NJ):
                    if t == 0:
                        pe.wait_ge(S["hid_lo"], NJ * n + j + 1)
                    last = split_product(C[t][:, :], [hid[s][0:JWS[j], j, t * P:(t + 1) * P] for s in range(2)],
                                         [w_down[s][0:JWS[j], j, :, :].rearrange("p e n -> p (e n)") for s in range(2)],
                                         start=(j == 0), stop=(j == NJ - 1))
                last.then_inc(S["down_ps"], 1)

            def h3T_(n, t):
                pe.wait_ge(S["h3_ready"], tl(n, t))
                for c in range(HC):
                    last = pe.transpose(C[t][:, c * P:(c + 1) * P], h3[t][:, c * P:(c + 1) * P], ident)
                pe.wait_ge(S["ld_cb"], 16 * n + 16)
                pe.matmul(C[t][:, H:2 * H], ctxT_b[:, t * P:(t + 1) * P], w_memT[:, 0:H], start=True, stop=True).then_inc(S["h3T_ps"], 1)

            def hw(n, t):
                pe.wait_ge(S["h3T_ready"], tl(n, t))
                for c in range(HC):
                    pe.matmul(C[t][:, 0:P], w_mem[:, c, :], h3T[t][:, c, :], start=(c == 0), stop=(c == HC - 1))
                for c in range(HC):
                    last = pe.matmul(C[t][:, H:2 * H], h3T[t][:, c, :], w_gate[:, c, :], start=(c == 0), stop=(c == HC - 1))
                last.then_inc(S["hw_ps"], 1)

            def fold(n, t):
                pe.wait_ge(S["ld_wb"], 16 * 4)
                for c in range(HC):
                    last = pe.matmul(B[0][:, 0:H], w_mem[:, c, :], w_gate2[:, c, :], start=(c == 0), stop=(c == HC - 1))
                last.then_inc(S["fold_ps"], 1)
                pe.wait_ge(S["fold_ready"], 1)

            def mscore(n, t):
                pe.wait_ge(S["hw_ready"], tl(n, t))
                pe.wait_ge(S["g1_ready"], tl(n, t))
                pe.matmul(C[t][:, 0:P], ident_h[:, :], block_h[:, :], start=True, stop=False)
                pe.matmul(C[t][:, 0:P], hwT[t], ctxT_b[:, t * P:(t + 1) * P], start=False, stop=True)
                pe.matmul(C[t][:, H:2 * H], ctxT_b[:, t * P:(t + 1) * P], w_memT[:, H:2 * H], start=True, stop=True).then_inc(S["ms_ps"], 1)

            def attnT(n, t):
                pe.wait_ge(S["mexp"], tl(n, t))
                pe.wait_ge(S["mpg_ready"], tl(n, t))
                pe.transpose(C[t][:, P:2 * P], mw[t], ident).then_inc(S["mwT_ps"], 1)

            def gate(n, t):
                pe.wait_ge(S["mwT_ready"], tl(n, t))
                pe.matmul(C[t][:, 0:H], mwT[t][:, :], mp[t], start=True, stop=True)
                pe.matmul(C[t][:, H:2 * H], mwT[t][:, :], mpg[t][:, :], start=True, stop=True).then_inc(S["gate_ps"], 1)

            run(pe, dict(table=table, qkv=qkv, qkT=qkT, score=score, probT=probT, pv=pv, ctxT=ctxT, dense=dense, h1T=h1T_, cproj=cproj,
                         cqkT=cqkT, cscore=cscore, cprobT=cprobT, cpv=cpv, cctxT=cctxT, cdense=cdense, miT=miT, mlp=mlp,
                         down=down, h3T=h3T_, hw=hw, fold=fold, mscore=mscore, attnT=attnT, gate=gate))


def kernel(**inputs):
    import concourse.bacc as bacc
    from concourse.bass_utils import run_bass_kernel_spmd

    a = {k: np.asarray(v) for k, v in inputs.items()}
    feeds = {k: a[k] for k in a if k.startswith("L0_xattn_") and not k.startswith("L0_xattn_ln_")}
    for k in "vl":
        w = a[f"L0_xattn_{k}_up"]
        feeds[f"L0_xattn_{k}_up"] = np.concatenate([w[:, INTER - REST:], w[:, :INTER - REST]], 1)
    norms = [a["L0_xattn_" + k] for k in ("ln_in_w", "ln_post_cross_w", "ln_post_attn_w")]
    feeds.update(
        x=a["x"].reshape(N_TOK, H), xT=a["x"].reshape(N_TOK, H).T, ctxT=a["ctx_1024"].reshape(N_TOK, CC).T,
        types=a["mask_BxS_ik0"].reshape(1, N_TOK), pos=a["pos_1xS"],
        W_mem=a["L1_xattn_W_mem"], W_memT=a["L1_xattn_W_mem"].T, W_gateT=a["L1_xattn_W_gate"].T, b_gate=a["L1_xattn_b_gate"], w_norm=a["L1_xattn_norm_w"],
        ln=np.stack(norms).reshape(3 * HC, P).T, consts=shape_constants(),
    )
    types = a["mask_BxS_ik0"].reshape(N_TOK)
    feeds["types_t"] = np.concatenate([types.reshape(-1, P).T, np.append(types[1:], types[:1]).reshape(-1, P).T], 1)
    nc = bacc.Bacc("TRN2", target_bir_lowering=False, num_devices=1)
    arrays, d = {}, {}
    for name, v in feeds.items():
        v = np.ascontiguousarray(v)
        arrays[f"in_{name}_dram"] = v
        d[name] = nc.dram_tensor(f"in_{name}_dram", v.shape, mybir.dt.from_np(v.dtype), kind="ExternalInput").ap()
    out = nc.dram_tensor("out_0_dram", (N_TOK, H), F32, kind="ExternalOutput").ap()
    xattn_kernel(nc, d, out)
    r = run_bass_kernel_spmd(nc, [arrays], core_ids=[0])
    return r.results[0]["out_0_dram"].reshape(BATCH, SEQ, H)
```
